# Optimizing a Trainium2 kernel written in Bass

```python
import numpy as np
import jax
import jax.numpy as jnp

def _softmax(x, axis=-1):
    return jax.nn.softmax(x, axis=axis)

def _gelu(x):
    return jax.nn.gelu(x, approximate=True)

def _silu(x):
    return jax.nn.silu(x)

def _sigmoid(x):
    return jax.nn.sigmoid(x)

def _layernorm(x, axis=-1, eps=1e-05):
    m = jnp.mean(x, axis=axis, keepdims=True)
    v = jnp.var(x, axis=axis, keepdims=True)
    return (x - m) / jnp.sqrt(v + eps)

def _scatter_add(tgt, idx, src, axis=0):
    return tgt.at[idx].add(src)

def _segment_sum(src, seg, n):
    return jax.ops.segment_sum(src, seg, n)
kernel_name = 'mk_sandwich_d2_jaxref_r8_330f76'

def setup_inputs(seed: int=0):
    np.random.seed(seed)
    _w = jnp.asarray

    def _L0_attn_setup():
        import jax, jax.numpy as jnp
        import numpy as np
        B, S, HID = (2, 256, 256)
        HV, HK, DK, DV = (32, 16, 128, 128)
        KEY_DIM = HK * DK
        VAL_DIM = HV * DV
        CONV_DIM = 2 * KEY_DIM + VAL_DIM
        KS = 4
        EPS = 1e-06

        def _l2norm(x):
            return x / jnp.maximum(jnp.linalg.norm(x, axis=-1, keepdims=True), EPS)
        key = jax.random.key(seed)
        ks = jax.random.split(key, 8)
        s = lambda k, shape, scale: jax.random.normal(k, shape, dtype=jnp.float32) * scale
        return {'hidden_states': s(ks[0], (B, S, HID), 1.0), 'W_qkv': s(ks[1], (CONV_DIM, HID), 0.02), 'W_z': s(ks[2], (VAL_DIM, HID), 0.02), 'W_a': s(ks[3], (HV, HID), 0.02), 'W_b': s(ks[4], (HV, HID), 0.02), 'conv_w': s(ks[5], (CONV_DIM, KS), 0.2), 'A_log': jnp.zeros((HV,), jnp.float32), 'dt_bias': jnp.ones((HV,), jnp.float32), 'norm_w': jnp.ones((DV,), jnp.float32), 'W_out': s(ks[6], (HID, VAL_DIM), 0.02)}
    _L0_attn_in = _L0_attn_setup()

    def _L0_ffn_setup():
        import jax, jax.numpy as jnp
        import numpy as np
        B, S, H = (1, 256, 256)
        E, K, I = (16, 4, 176)
        IS = 352
        CAP = 128
        key = jax.random.key(seed)
        ks = jax.random.split(key, 8)
        sc = 0.02
        return {'hidden_states': jax.random.normal(ks[0], (B, S, H), jnp.float32), 'gate_w': jax.random.normal(ks[1], (E, H), jnp.float32) * sc, 'w_gate': jax.random.normal(ks[2], (E, H, I), jnp.float32) * sc, 'w_up': jax.random.normal(ks[3], (E, H, I), jnp.float32) * sc, 'w_down': jax.random.normal(ks[4], (E, I, H), jnp.float32) * sc, 'sw_gate': jax.random.normal(ks[5], (H, IS), jnp.float32) * sc, 'sw_up': jax.random.normal(ks[6], (H, IS), jnp.float32) * sc, 'sw_down': jax.random.normal(ks[7], (IS, H), jnp.float32) * sc}
    _L0_ffn_in = _L0_ffn_setup()

    def _L1_attn_setup():
        import jax, jax.numpy as jnp
        import numpy as np
        D_MODEL = 256
        N_HEADS = 16
        N_KV_HEADS = 4
        D_HEAD = 128
        MAX_SEQ_LEN = 512
        RANK = 32
        GAMMA_INIT = 0.05
        ROPE_BASE = 10000.0

        def _rope(x, offset=0):
            B, H, T, D = x.shape
            inv_freq = 1.0 / ROPE_BASE ** (jnp.arange(0, D, 2, dtype=jnp.float32) / D)
            pos = jnp.arange(T, dtype=jnp.float32) + offset
            ang = pos[:, None] * inv_freq[None, :]
            cos = jnp.cos(ang)[None, None]
            sin = jnp.sin(ang)[None, None]
            x1, x2 = (x[..., :D // 2], x[..., D // 2:])
            return jnp.concatenate([x1 * cos - x2 * sin, x2 * cos + x1 * sin], axis=-1)
        key = jax.random.key(seed)
        ks = jax.random.split(key, 10)
        B, T = (1, 256)
        s = lambda fan_in: 1.0 / np.sqrt(fan_in)
        x = jax.random.normal(ks[0], (B, T, D_MODEL), dtype=jnp.float32)
        Wq = jax.random.normal(ks[1], (D_MODEL, N_HEADS * D_HEAD), dtype=jnp.float32) * s(D_MODEL)
        Wk = jax.random.normal(ks[2], (D_MODEL, N_KV_HEADS * D_HEAD), dtype=jnp.float32) * s(D_MODEL)
        Wv = jax.random.normal(ks[3], (D_MODEL, N_KV_HEADS * D_HEAD), dtype=jnp.float32) * s(D_MODEL)
        Wo = jax.random.normal(ks[4], (N_HEADS * D_HEAD, D_MODEL), dtype=jnp.float32) * s(N_HEADS * D_HEAD)
        pol_dir = jax.random.normal(ks[5], (N_HEADS,), dtype=jnp.float32) * 0.1
        pol_WA = jax.random.normal(ks[6], (D_MODEL, RANK), dtype=jnp.float32) * s(D_MODEL)
        pol_WB = jax.random.normal(ks[7], (D_MODEL, RANK), dtype=jnp.float32) * s(D_MODEL)
        pol_gate = jnp.full((N_HEADS,), -3.0, dtype=jnp.float32)
        slopes = np.linspace(3.0, -3.0, N_HEADS)
        gamma_t = np.clip(GAMMA_INIT * 2.0 ** slopes, 0.0001, None)
        gtp_gamma = jnp.asarray(np.log(np.expm1(gamma_t)), dtype=jnp.float32)
        return {'x': x, 'Wq': Wq, 'Wk': Wk, 'Wv': Wv, 'Wo': Wo, 'pol_dir': pol_dir, 'pol_WA': pol_WA, 'pol_WB': pol_WB, 'pol_gate': pol_gate, 'gtp_gamma': gtp_gamma}
    _L1_attn_in = _L1_attn_setup()

    def _L1_ffn_setup():
        import jax, jax.numpy as jnp
        import numpy as np
        HIDDEN = 256
        INTER = 688
        LUT_SIZE = 16

        def _ghost_linear(x, idx, lut):
            w = lut[idx]
            return jnp.einsum('bsh,oh->bso', x, w)
        key = jax.random.key(seed)
        k_x, k_lut, k_g, k_u, k_d = jax.random.split(key, 5)
        x = jax.random.normal(k_x, (2, 512, HIDDEN), dtype=jnp.float32)
        lut = jax.random.normal(k_lut, (LUT_SIZE,), dtype=jnp.float32) * 0.02
        gate_idx = jax.random.randint(k_g, (INTER, HIDDEN), 0, LUT_SIZE, dtype=jnp.int32)
        up_idx = jax.random.randint(k_u, (INTER, HIDDEN), 0, LUT_SIZE, dtype=jnp.int32)
        down_idx = jax.random.randint(k_d, (HIDDEN, INTER), 0, LUT_SIZE, dtype=jnp.int32)
        return {'x': x, 'lut': lut, 'gate_idx': gate_idx, 'up_idx': up_idx, 'down_idx': down_idx}
    _L1_ffn_in = _L1_ffn_setup()
    _d = {'L0_attn_hidden_states': _L0_attn_in['hidden_states'], 'L0_attn_W_qkv': _L0_attn_in['W_qkv'], 'L0_attn_W_z': _L0_attn_in['W_z'], 'L0_attn_W_a': _L0_attn_in['W_a'], 'L0_attn_W_b': _L0_attn_in['W_b'], 'L0_attn_conv_w': _L0_attn_in['conv_w'], 'L0_attn_A_log': _L0_attn_in['A_log'], 'L0_attn_dt_bias': _L0_attn_in['dt_bias'], 'L0_attn_norm_w': _L0_attn_in['norm_w'], 'L0_attn_W_out': _L0_attn_in['W_out'], 'L0_ffn_gate_w': _L0_ffn_in['gate_w'], 'L0_ffn_w_gate': _L0_ffn_in['w_gate'], 'L0_ffn_w_up': _L0_ffn_in['w_up'], 'L0_ffn_w_down': _L0_ffn_in['w_down'], 'L0_ffn_sw_gate': _L0_ffn_in['sw_gate'], 'L0_ffn_sw_up': _L0_ffn_in['sw_up'], 'L0_ffn_sw_down': _L0_ffn_in['sw_down'], 'L1_attn_Wq': _L1_attn_in['Wq'], 'L1_attn_Wk': _L1_attn_in['Wk'], 'L1_attn_Wv': _L1_attn_in['Wv'], 'L1_attn_Wo': _L1_attn_in['Wo'], 'L1_attn_pol_dir': _L1_attn_in['pol_dir'], 'L1_attn_pol_WA': _L1_attn_in['pol_WA'], 'L1_attn_pol_WB': _L1_attn_in['pol_WB'], 'L1_attn_pol_gate': _L1_attn_in['pol_gate'], 'L1_attn_gtp_gamma': _L1_attn_in['gtp_gamma'], 'L1_ffn_lut': _L1_ffn_in['lut'], 'L1_ffn_gate_idx': _L1_ffn_in['gate_idx'], 'L1_ffn_up_idx': _L1_ffn_in['up_idx'], 'L1_ffn_down_idx': _L1_ffn_in['down_idx']}
    _x0 = _d['L0_attn_hidden_states']
    _d['L0_attn_hidden_states'] = jax.random.normal(jax.random.fold_in(jax.random.key(seed), 1), (8, 256, 256), dtype=_x0.dtype)
    del _x0
    return _d

def reference(L0_attn_hidden_states, L0_attn_W_qkv, L0_attn_W_z, L0_attn_W_a, L0_attn_W_b, L0_attn_conv_w, L0_attn_A_log, L0_attn_dt_bias, L0_attn_norm_w, L0_attn_W_out, L0_ffn_gate_w, L0_ffn_w_gate, L0_ffn_w_up, L0_ffn_w_down, L0_ffn_sw_gate, L0_ffn_sw_up, L0_ffn_sw_down, L1_attn_Wq, L1_attn_Wk, L1_attn_Wv, L1_attn_Wo, L1_attn_pol_dir, L1_attn_pol_WA, L1_attn_pol_WB, L1_attn_pol_gate, L1_attn_gtp_gamma, L1_ffn_lut, L1_ffn_gate_idx, L1_ffn_up_idx, L1_ffn_down_idx):

    def _L0_attn_ref(hidden_states, W_qkv, W_z, W_a, W_b, conv_w, A_log, dt_bias, norm_w, W_out):
        import jax, jax.numpy as jnp
        import numpy as np
        B, S, HID = (2, 256, 256)
        HV, HK, DK, DV = (32, 16, 128, 128)
        KEY_DIM = HK * DK
        VAL_DIM = HV * DV
        CONV_DIM = 2 * KEY_DIM + VAL_DIM
        KS = 4
        EPS = 1e-06

        def _l2norm(x):
            return x / jnp.maximum(jnp.linalg.norm(x, axis=-1, keepdims=True), EPS)
        Bn, Sn, _ = hidden_states.shape
        qkv = hidden_states @ W_qkv.T
        z = hidden_states @ W_z.T
        a = hidden_states @ W_a.T
        b = hidden_states @ W_b.T
        xp = jnp.pad(qkv, ((0, 0), (KS - 1, 0), (0, 0)))
        conv = sum((xp[:, k:k + Sn, :] * conv_w[:, k] for k in range(KS)))
        mixed = jax.nn.silu(conv)
        q = mixed[..., :KEY_DIM].reshape(Bn, Sn, HK, DK)
        k = mixed[..., KEY_DIM:2 * KEY_DIM].reshape(Bn, Sn, HK, DK)
        v = mixed[..., 2 * KEY_DIM:].reshape(Bn, Sn, HV, DV)
        rep = HV // HK
        q = jnp.repeat(q, rep, axis=2)
        k = jnp.repeat(k, rep, axis=2)
        q = _l2norm(q) * DK ** (-0.5)
        k = _l2norm(k)
        g = -jnp.exp(A_log) * jax.nn.softplus(a + dt_bias)
        beta = jax.nn.sigmoid(b)
        qs = q.transpose(1, 0, 2, 3)
        ks_ = k.transpose(1, 0, 2, 3)
        vs = v.transpose(1, 0, 2, 3)
        gs = g.transpose(1, 0, 2)
        bs = beta.transpose(1, 0, 2)

        def step(state, inp):
            qt, kt, vt, gt, bt = inp
            state = state * jnp.exp(gt)[..., None, None]
            kv = jnp.einsum('bhk,bhkv->bhv', kt, state)
            delta = (vt - kv) * bt[..., None]
            state = state + jnp.einsum('bhk,bhv->bhkv', kt, delta)
            out = jnp.einsum('bhk,bhkv->bhv', qt, state)
            return (state, out)
        state0 = jnp.zeros((Bn, HV, DK, DV), hidden_states.dtype)
        _, outs = jax.lax.scan(step, state0, (qs, ks_, vs, gs, bs))
        o = outs.transpose(1, 0, 2, 3)
        var = jnp.mean(jnp.square(o), axis=-1, keepdims=True)
        o = o * jax.lax.rsqrt(var + EPS) * norm_w
        o = o * jax.nn.silu(z.reshape(Bn, Sn, HV, DV))
        return o.reshape(Bn, Sn, VAL_DIM) @ W_out.T

    def _L0_ffn_ref(hidden_states, gate_w, w_gate, w_up, w_down, sw_gate, sw_up, sw_down):
        import jax, jax.numpy as jnp
        import numpy as np
        B, S, H = (1, 256, 256)
        E, K, I = (16, 4, 176)
        IS = 352
        CAP = 128
        b, s, h = hidden_states.shape
        x = hidden_states.reshape(-1, h)
        T = x.shape[0]
        scores = jax.nn.softmax(x @ gate_w.T, axis=-1)
        topk_w, topk_i = jax.lax.top_k(scores, K)
        topk_w = topk_w / (topk_w.sum(-1, keepdims=True) + 1e-20)
        flat_i = topk_i.reshape(-1)
        flat_w = topk_w.reshape(-1)
        order = jnp.argsort(flat_i)
        se = flat_i[order]
        counts = jax.ops.segment_sum(jnp.ones_like(flat_i), flat_i, num_segments=E)
        starts = jnp.cumsum(counts) - counts
        rank = jnp.arange(T * K) - starts[se]
        tok = order // K
        slot = jnp.where(rank < CAP, rank, CAP)
        buf = jnp.full((E, CAP + 1), T, dtype=jnp.int32).at[se, slot].set(tok)[:, :CAP]
        wbuf = jnp.zeros((E, CAP + 1), x.dtype).at[se, slot].set(flat_w[order])[:, :CAP]
        xpad = jnp.concatenate([x, jnp.zeros((1, h), x.dtype)], axis=0)
        xg = xpad[buf]
        gact = jax.nn.silu(jnp.einsum('ech,ehi->eci', xg, w_gate))
        mid = gact * jnp.einsum('ech,ehi->eci', xg, w_up)
        eout = jnp.einsum('eci,eih->ech', mid, w_down) * wbuf[..., None]
        y = jnp.zeros((T + 1, h), x.dtype).at[buf.reshape(-1)].add(eout.reshape(-1, h))[:T]
        shared = jax.nn.silu(x @ sw_gate) * (x @ sw_up) @ sw_down
        return (y + shared).reshape(b, s, h)

    def _L1_attn_ref(x, Wq, Wk, Wv, Wo, pol_dir, pol_WA, pol_WB, pol_gate, gtp_gamma):
        import jax, jax.numpy as jnp
        import numpy as np
        D_MODEL = 256
        N_HEADS = 16
        N_KV_HEADS = 4
        D_HEAD = 128
        MAX_SEQ_LEN = 512
        RANK = 32
        GAMMA_INIT = 0.05
        ROPE_BASE = 10000.0

        def _rope(x, offset=0):
            B, H, T, D = x.shape
            inv_freq = 1.0 / ROPE_BASE ** (jnp.arange(0, D, 2, dtype=jnp.float32) / D)
            pos = jnp.arange(T, dtype=jnp.float32) + offset
            ang = pos[:, None] * inv_freq[None, :]
            cos = jnp.cos(ang)[None, None]
            sin = jnp.sin(ang)[None, None]
            x1, x2 = (x[..., :D // 2], x[..., D // 2:])
            return jnp.concatenate([x1 * cos - x2 * sin, x2 * cos + x1 * sin], axis=-1)
        B, T, _ = x.shape
        H, Hkv, D = (N_HEADS, N_KV_HEADS, D_HEAD)
        n_rep = H // Hkv
        Q = (x @ Wq).reshape(B, T, H, D).transpose(0, 2, 1, 3)
        K = (x @ Wk).reshape(B, T, Hkv, D).transpose(0, 2, 1, 3)
        V = (x @ Wv).reshape(B, T, Hkv, D).transpose(0, 2, 1, 3)
        Q = _rope(Q)
        K = _rope(K)
        K = jnp.repeat(K, n_rep, axis=1)
        V = jnp.repeat(V, n_rep, axis=1)
        idx = jnp.arange(T)
        delta = (idx[:, None] - idx[None, :]).astype(jnp.float32)
        causal = delta >= 0
        pol = jnp.clip(pol_dir, -1.0, 1.0)
        polarity_bias = -pol[:, None, None] * (delta / float(MAX_SEQ_LEN))[None]
        gamma = jnp.maximum(jax.nn.softplus(gtp_gamma), 1e-06)
        gtp_bias = -gamma[:, None, None] * jnp.maximum(delta, 0.0)[None]
        bias = (polarity_bias + gtp_bias)[None]
        A = x @ pol_WA
        Bm = x @ pol_WB
        M = jax.nn.sigmoid(jnp.einsum('bir,bjr->bij', A, Bm))
        gate = jax.nn.sigmoid(pol_gate)[None, :, None, None]
        bias = bias + gate * M[:, None]
        neg_inf = jnp.finfo(bias.dtype).min
        bias = jnp.where(causal[None, None], bias, neg_inf)
        scores = jnp.einsum('bhid,bhjd->bhij', Q, K) / jnp.sqrt(jnp.float32(D)) + bias
        attn = jax.nn.softmax(scores, axis=-1)
        out = jnp.einsum('bhij,bhjd->bhid', attn, V)
        out = out.transpose(0, 2, 1, 3).reshape(B, T, H * D)
        return out @ Wo

    def _L1_ffn_ref(x, lut, gate_idx, up_idx, down_idx):
        import jax, jax.numpy as jnp
        import numpy as np
        HIDDEN = 256
        INTER = 688
        LUT_SIZE = 16

        def _ghost_linear(x, idx, lut):
            w = lut[idx]
            return jnp.einsum('bsh,oh->bso', x, w)
        gate = _ghost_linear(x, gate_idx, lut)
        up = _ghost_linear(x, up_idx, lut)
        h = jax.nn.silu(gate) * up
        return _ghost_linear(h, down_idx, lut)
    x = L0_attn_hidden_states
    x = x + _layernorm(_L0_attn_ref(_layernorm(x, axis=-1), L0_attn_W_qkv, L0_attn_W_z, L0_attn_W_a, L0_attn_W_b, L0_attn_conv_w, L0_attn_A_log, L0_attn_dt_bias, L0_attn_norm_w, L0_attn_W_out), axis=-1)
    x = x + _layernorm(_L0_ffn_ref(_layernorm(x, axis=-1), L0_ffn_gate_w, L0_ffn_w_gate, L0_ffn_w_up, L0_ffn_w_down, L0_ffn_sw_gate, L0_ffn_sw_up, L0_ffn_sw_down), axis=-1)
    x = x + _layernorm(_L1_attn_ref(_layernorm(x, axis=-1), L1_attn_Wq, L1_attn_Wk, L1_attn_Wv, L1_attn_Wo, L1_attn_pol_dir, L1_attn_pol_WA, L1_attn_pol_WB, L1_attn_pol_gate, L1_attn_gtp_gamma), axis=-1)
    x = x + _layernorm(_L1_ffn_ref(_layernorm(x, axis=-1), L1_ffn_lut, L1_ffn_gate_idx, L1_ffn_up_idx, L1_ffn_down_idx), axis=-1)
    return x

_drawn_inputs = setup_inputs


def setup_inputs(seed=0):
    import zlib

    import numpy as np

    out = dict(_drawn_inputs(seed))
    spreads = {'L0_attn_A_log': (0.0, 0.1),
     'L0_attn_dt_bias': (1.0, 0.2),
     'L0_attn_norm_w': (1.0, 0.2),
     'L1_attn_pol_gate': (-3.0, 0.6)}
    factors = {'L1_attn_pol_dir': 8.0, 'L1_attn_pol_WA': 5.432, 'L1_attn_pol_WB': 5.435}
    for name, (base, spread) in spreads.items():
        noise = np.random.default_rng([zlib.crc32(name.encode()), seed]).standard_normal(out[name].shape)
        drawn = base * np.exp(spread * noise) if base else spread * noise
        out[name] = jnp.asarray(drawn.astype(out[name].dtype))
    for name, factor in factors.items():
        out[name] = (out[name] * factor).astype(out[name].dtype)
    return out
```

```python
from contextlib import ExitStack

import numpy as np

import concourse.bass as bass
from concourse import mybir

ALU = mybir.AluOpType
ACT = mybir.ActivationFunctionType
AX = mybir.AxisListType
F32 = mybir.dt.float32
I32 = mybir.dt.int32
U32 = mybir.dt.uint32

P = 128
B, S, H = 8, 256, 256
TOK = B * S
NT = TOK // P
KT = H // P
LN_EPS = 1e-5

HV, HK, DK = 32, 16, 128
TAPS = 4
NF = 4
LEVELS = 5
DELTA_EPS = 1e-6
STEPS = HK * B


def wait(eng, sem, value):
    if isinstance(value, int) and value <= 0:
        return
    eng.wait_ge(sem, value)


class Memory:

    def __init__(self, nc, stack):
        self.nc, self.stack, self.sems = nc, stack, []

    def sb(self, name, shape, dt=F32):
        return self.stack.enter_context(self.nc.sbuf_tensor(name, shape, dt))

    def ps(self, name, shape=(P, 512), dt=F32):
        return self.stack.enter_context(self.nc.psum_tensor(name, list(shape), dt))

    def sem(self, name):
        handle = self.stack.enter_context(self.nc.semaphore(name))
        self.sems.append(handle)
        return handle

    def clear(self):
        with self.nc.Block() as block:

            @block.gpsimd
            def _(pool):
                for handle in self.sems:
                    pool.sem_clear(handle)


def make_constants(nc, c):
    with ExitStack() as stack:
        m = Memory(nc, stack)
        step = m.sem("const_step")
        inner = stack.enter_context(ExitStack())
        block = inner.enter_context(nc.Block())

        @block.gpsimd
        def _(pool):
            n = 0

            def done(ins):
                nonlocal n
                n += 1
                ins.then_inc(step, 1)
                pool.wait_ge(step, n)

            def select(ap, op, base, pattern, mult, fill):
                done(nc.gpsimd.affine_select(out=ap, in_=ap, compare_op=op, fill=fill, base=base,
                                             pattern=pattern, channel_multiplier=mult))

            done(nc.gpsimd.memset(c.ones[:, :], 1.0))
            done(nc.gpsimd.memset(c.ident[:, :], 0.0))
            select(c.ident[:, :], ALU.not_equal, 0, [[-1, P]], 1, 1.0)
            done(nc.gpsimd.memset(c.tri[:, :], 1.0))
            select(c.tri[:, :], ALU.is_ge, 0, [[1, P]], -1, 0.0)
            done(nc.gpsimd.memset(c.tri_strict[:, :], 1.0))
            select(c.tri_strict[:, :], ALU.is_gt, 0, [[1, P]], -1, 0.0)
            done(nc.gpsimd.memset(c.cut[:, :], 0.0))
            select(c.cut[:, 0:P], ALU.is_ge, 0, [[1, P]], -1, -30000.0)
            for l in range(LEVELS + 1):
                b = 1 << l
                val = -1.0 if l == 0 else 1.0
                v = c.level[:, l, :].rearrange("p (n two i) -> p n two i", two=2, i=b)
                done(nc.gpsimd.memset(c.level[:, l, :], val))
                done(nc.gpsimd.memset(v[:, :, 0, :], 0.0))
                odd = v[:, :, 1, :]
                select(odd, ALU.is_ge, 0, [[-2 * b, P // (2 * b)], [0, b]], 1, 0.0)
                select(odd, ALU.is_gt, b, [[2 * b, P // (2 * b)], [0, b]], -1, 0.0)

        inner.close()
        m.clear()


def normalise(nc, c, tag, src, first=False, last=None):
    with ExitStack() as stack:
        m = Memory(nc, stack)
        stats = m.sb(tag + "stats", [P, NT, 6])
        mv_y = m.sb(tag + "mv_y", [P, NT, 2])
        mv_x = m.sb(tag + "mv_x", [P, NT, 2])
        var_y = m.sb(tag + "var_y", [P, NT])
        var_x = m.sb(tag + "var_x", [P, NT])
        power = m.sb(tag + "power", [P, NT])
        rstd_y = m.sb(tag + "rstd_y", [P, NT])
        rstd_x = m.sb(tag + "rstd_x", [P, NT])
        xn = c.xn
        pt = [m.ps(f"{tag}pt{i}") for i in range(4)]
        loaded, dve, var_ready, rstd_ready, xn_ready, turned, copied, stored, power_ready = (
            m.sem(tag + n) for n in ("loaded", "dve", "var_ready", "rstd_ready", "xn_ready", "turned",
                                     "copied", "stored", "power_ready"))
        inner = stack.enter_context(ExitStack())
        block = inner.enter_context(nc.Block())

        @block.sync
        def _(sp):
            if first:
                sp.dma_start(c.x[:, :, :], src).then_inc(loaded, 16)
            if last is not None:
                for q in range(4):
                    sp.wait_ge(xn_ready, 4 * q + 4)
                    sp.dma_start(last[:, 4 * q:4 * q + 4, :], c.x[:, 4 * q:4 * q + 4, :]).then_inc(stored, 16)
                sp.wait_ge(stored, 64)

        @block.gpsimd
        def _(pool):
            nc.gpsimd.memset(power[:, :], -0.5).then_inc(power_ready, 1)
            pool.wait_ge(power_ready, 1)
            pairs = ([] if first else [(rstd_y, var_y)]) + ([] if last is not None else [(rstd_x, var_x)])
            for i, (out, var) in enumerate(pairs):
                pool.wait_ge(var_ready, i + 1)
                nc.gpsimd.tensor_tensor(out[:, :], var[:, :], power[:, :], ALU.pow).then_inc(rstd_ready, 1)

        @block.vector
        def _(vec):
            n = 0

            def chain(ins):
                nonlocal n
                n += 1
                ins.then_inc(dve, 1)

            def statistics(of, mv, var):
                for t in range(NT):
                    chain(nc.vector.bn_stats(stats[:, t, :], of[:, t, :]))
                vec.wait_ge(dve, n)
                for t in range(NT):
                    chain(nc.vector.bn_aggr(mv[:, t, :], stats[:, t, :]))
                vec.wait_ge(dve, n)
                nc.vector.tensor_scalar(var[:, :], mv[:, :, 1], LN_EPS, None, ALU.add).then_inc(var_ready, 1)

            if first:
                vec.wait_ge(loaded, 16)
            else:
                statistics(src, mv_y, var_y)
                vec.wait_ge(rstd_ready, 1)
                for t in range(NT):
                    chain(nc.vector.tensor_scalar(src[:, t, :], src[:, t, :], mv_y[:, t, 0:1], rstd_y[:, t:t + 1],
                                                  ALU.subtract, ALU.mult))
                    vec.wait_ge(dve, n)
                    ins = nc.vector.tensor_tensor(c.x[:, t, :], c.x[:, t, :], src[:, t, :], ALU.add)
                    if last is not None:
                        ins.then_inc(xn_ready, 1)
                    else:
                        chain(ins)
                vec.wait_ge(dve, n)
            if last is None:
                statistics(c.x, mv_x, var_x)
                vec.wait_ge(rstd_ready, 1 if first else 2)
                for t in range(NT):
                    nc.vector.tensor_scalar(xn[:, t, :], c.x[:, t, :], mv_x[:, t, 0:1], rstd_x[:, t:t + 1],
                                            ALU.subtract, ALU.mult).then_inc(xn_ready, 1)

        if last is None:
            @block.tensor
            def _(pe):
                for u in range(NT // 2):
                    if u >= 4:
                        pe.wait_ge(copied, u - 3)
                    pe.wait_ge(xn_ready, 2 * u + 2)
                    for k in range(KT):
                        for i in range(2):
                            ins = nc.tensor.transpose(pt[u % 4][:, (2 * k + i) * P:(2 * k + i + 1) * P],
                                                      xn[:, 2 * u + i, k * P:(k + 1) * P], c.ident[:, :])
                    ins.then_inc(turned, 1)

            @block.scalar
            def _(act):
                for u in range(NT // 2):
                    act.wait_ge(turned, u + 1)
                    nc.scalar.activation(c.xnT[:, :, u * S:(u + 1) * S],
                                         pt[u % 4][:, :].rearrange("p (k t) -> p k t", k=KT),
                                         ACT.Copy).then_inc(copied, 1)

        inner.close()
        m.clear()


def delta_gates(nc, c, w_ab, a_log, dt_bias, g_dram):
    with ExitStack() as stack:
        m = Memory(nc, stack)
        wab = m.sb("wab", [P, KT, 2 * HV])
        dtb = m.sb("dtb", [P, HV])
        alog = m.sb("alog", [P, HV])
        ea = m.sb("ea", [P, HV])
        u = m.sb("g_u", [P, NT, HV])
        mn = m.sb("g_mn", [P, NT, HV])
        ex = m.sb("g_ex", [P, NT, HV])
        ln = m.sb("g_ln", [P, NT, HV])
        sp_ = m.sb("g_sp", [P, NT, HV])
        g = m.sb("g_g", [P, NT, HV])
        th = m.sb("g_th", [P, NT, HV])
        gT = m.sb("g_gT", [HV, TOK])
        pab = [m.ps(f"pab{i}", (P, NT // 2, 2 * HV)) for i in range(2)]
        pg = m.ps("pg", (P, NT, HV))
        pgT = [m.ps(f"pgT{i}", (HV, 512)) for i in range(4)]
        loaded, projected, dve, act_done, g_ready, summed, G_ready, turned, gT_ready, stored = (
            m.sem("gates_" + n) for n in ("loaded", "projected", "dve", "act_done", "g_ready", "summed",
                                          "G_ready", "turned", "gT_ready", "stored"))
        inner = stack.enter_context(ExitStack())
        block = inner.enter_context(nc.Block())

        @block.sync
        def _(sp):
            sp.dma_start(wab[:, :, :], w_ab).then_inc(loaded, 16)
            sp.dma_start(dtb[:, :], dt_bias[None, :].to_broadcast([P, HV])).then_inc(loaded, 16)
            sp.dma_start(alog[:, :], a_log[None, :].to_broadcast([P, HV])).then_inc(loaded, 16)
            sp.wait_ge(gT_ready, 4)
            sp.dma_start(g_dram, gT[:, :]).then_inc(stored, 16)
            sp.wait_ge(stored, 16)

        @block.tensor
        def _(pe):
            pe.wait_ge(loaded, 48)
            for t in range(NT):
                for k in range(KT):
                    ins = nc.tensor.matmul(pab[t // 8][:, t % 8, :], c.xnT[:, k, t * P:(t + 1) * P], wab[:, k, :],
                                           start=(k == 0), stop=(k == KT - 1))
                if t % 8 == 7:
                    ins.then_inc(projected, 1)
            pe.wait_ge(g_ready, 1)
            nc.tensor.matmul(pg[:, :, :], c.tri[:, :], g[:, :, :], start=True, stop=False, skip_group_check=True)
            pairs = g[:, :, :].rearrange("p (b c) h -> p b c h", c=2)
            out = pg[:, :, :].rearrange("p (b c) h -> p b c h", c=2)
            nc.tensor.matmul(out[:, :, 1, :], c.ones[:, :], pairs[:, :, 0, :], start=False, stop=True,
                             skip_group_check=True).then_inc(summed, 1)
            pe.wait_ge(G_ready, 1)
            for t in range(NT):
                ins = nc.tensor.transpose(pgT[t // 4][:, (t % 4) * P:(t % 4 + 1) * P], c.G[:, t, :], c.ident[:, :])
                if t % 4 == 3:
                    ins.then_inc(turned, 1)

        @block.vector
        def _(vec):
            n = 0

            def done(ins):
                nonlocal n
                n += 1
                ins.then_inc(dve, 1)
                vec.wait_ge(dve, n)

            vec.wait_ge(loaded, 48)
            for i in range(2):
                vec.wait_ge(projected, i + 1)
                half = slice(8 * i, 8 * i + 8)
                done(nc.vector.tensor_tensor(u[:, half, :], pab[i][:, :, 0:HV],
                                             dtb[:, None, :].to_broadcast([P, 8, HV]), ALU.add))
                done(nc.vector.tensor_copy(c.beta[:, half, :], pab[i][:, :, HV:2 * HV]))
            done(nc.vector.scalar_tensor_tensor(out=mn[:, :, :], in0=u[:, :, :], scalar=-1.0, in1=u[:, :, :],
                                                op0=ALU.mult, op1=ALU.min))
            vec.wait_ge(act_done, 4)
            done(nc.vector.scalar_tensor_tensor(out=sp_[:, :, :], in0=u[:, :, :], scalar=0.0, in1=ln[:, :, :],
                                                op0=ALU.max, op1=ALU.add))
            nc.vector.scalar_tensor_tensor(out=g[:, :, :], in0=sp_[:, :, :], scalar=-1.0,
                                           in1=ea[:, None, :].to_broadcast([P, NT, HV]),
                                           op0=ALU.mult, op1=ALU.mult).then_inc(g_ready, 1)
            done(nc.vector.tensor_scalar(c.beta[:, :, :], th[:, :, :], 0.5, 0.5, ALU.mult, ALU.add))
            vec.wait_ge(summed, 1)
            nc.vector.tensor_copy(c.G[:, :, :], pg[:, :, :]).then_inc(G_ready, 1)
            for i in range(4):
                vec.wait_ge(turned, i + 1)
                nc.vector.tensor_copy(gT[:, 512 * i:512 * i + 512], pgT[i][:, :]).then_inc(gT_ready, 1)

        @block.scalar
        def _(act):
            act.wait_ge(loaded, 48)
            nc.scalar.activation(ea[:, :], alog[:, :], ACT.Exp).then_inc(act_done, 1)
            act.wait_ge(dve, 5)
            nc.scalar.activation(ex[:, :, :], mn[:, :, :], ACT.Exp).then_inc(act_done, 1)
            act.wait_ge(act_done, 2)
            nc.scalar.activation(ln[:, :, :], ex[:, :, :], ACT.Ln, bias=c.ones[:, 0:1]).then_inc(act_done, 1)
            nc.scalar.activation(th[:, :, :], c.beta[:, :, :], ACT.Tanh, scale=0.5).then_inc(act_done, 1)

        inner.close()
        m.clear()


def delta_rule(nc, c, w_qkv, w_z, conv_w, w_out, norm_w, g_dram, steps=STEPS):
    EPS_Q = DELTA_EPS * 4.0 * DK
    with ExitStack() as stack:
        m = Memory(nc, stack)
        wp = m.sb("wp", [P, KT, NF, P])
        wz = m.sb("wz", [P, KT, 2 * P])
        cw = m.sb("cw", [P, HK, NF, TAPS])
        wo = m.sb("wo", [P, 2, H])
        nw = m.sb("nw", [P, 1])
        xb = m.sb("xb", [P, KT, S])
        grow = m.sb("grow", [P, 2, S])
        gcol = m.sb("gcol", [P, 2, 2])
        bcol = m.sb("bcol", [P, 2, 2])
        cv = m.sb("cv", [P, NF, S])
        th = m.sb("th", [P, NF, S])
        s2 = m.sb("s2", [P, NF, S])
        sq = m.sb("sq", [P, 2, S])
        thz = m.sb("thz", [P, 2, 2 * P])
        zs = m.sb("zs", [P, 2, 2 * P])
        ns = m.sb("ns", [P, 4])
        nq = m.sb("nq", [P, 2])
        rk = m.sb("rk", [P, 2])
        sc = m.sb("sc", [P, 2, 2])
        kn = m.sb("kn", [P, 2])
        half = m.sb("half", [P, 4])
        mhalf = m.sb("mhalf", [P, 4])
        arg = m.sb("arg", [P, 2, 3 * P])
        dec = m.sb("dec", [P, 2, 3 * P])
        up = m.sb("up", [P, 8, 2, P])
        dg = up[:, 0:2, :, :].rearrange("p n h t -> p (n h) t")
        cm = m.sb("cm", [P, LEVELS, 4, P])
        TRs = m.sb("TRs", [P, 2, 4, P])
        T, R = TRs[:, 0], TRs[:, 1]
        seed = m.sb("seed", [P, 4, P])
        cwj = m.sb("cwj", [P, NF, TAPS])
        W = m.sb("W", [P, 4, P])
        s64 = m.sb("s64", [P, 4, 64])
        V = m.sb("V", [P, 2, 2, P])
        Z0 = m.sb("Z0", [P, 2, P])
        V1 = m.sb("V1", [P, 2, P])
        Z1 = m.sb("Z1", [P, 2, P])
        osq = m.sb("osq", [P, 4, P])
        oss = m.sb("oss", [P, 4])
        orr = m.sb("orr", [P, 4])
        rs = m.sb("rs", [P, 4])
        og = m.sb("og", [P, 4, P])
        ogT = m.sb("ogT", [P, 4, P])
        X0, X1, X2, X3 = (m.ps(f"dx{i}") for i in range(4))
        S1 = [m.ps("dS1A"), m.ps("dS1B")]
        TR = [m.ps("dTRA"), m.ps("dTRB")]

        names = ("w_loaded wz_loaded wo_loaded misc_loaded xb_loaded grow_loaded "
                 "qkv_done z_done ssum_done vt_done gram_done t1_done s1_done tr_done s64_done r64_done "
                 "z0_done a21_done z1_done o_done ogT_done out_done "
                 "tap_done conv_done thqk_done thv_done silu_done sq_done thz_done zs_done ns_done rk_done "
                 "sc_done kn_done cols_done arg_done dec_done up_done dg_done r1_done t1_copied cm_done "
                 "w_done tr_copied s64_copied r64_copied V_done z0_copied v1_done z1_copied oss_done "
                 "orr_done rs_done og_done ogT_copied acc_done halves tmp_done nq_done zeroed powers").split()
        s = {n: m.sem("d_" + n) for n in names}
        inner = stack.enter_context(ExitStack())
        block = inner.enter_context(nc.Block())

        def head(j):
            return j // B

        def seq(j):
            return j % B

        @block.sync
        def _(sp):
            sp.dma_start(cw[:, :, :, :], conv_w).then_inc(s["misc_loaded"], 16)
            sp.dma_start(nw[:, :], norm_w).then_inc(s["misc_loaded"], 16)

            def fixed(value):
                return value if isinstance(value, int) else sp.snap(value)

            def load_decays(j):
                h0, t0 = fixed(2 * head(j)), fixed(seq(j) * S)
                wait(sp, s["arg_done"], 4 * j)
                sp.dma_start(grow[:, :, :], g_dram[None, bass.ds(h0, 2), bass.ds(t0, S)]
                             .to_broadcast([P, 2, S])).then_inc(s["grow_loaded"], 16)

            def load_head(g):
                wait(sp, s["qkv_done"], 2 * B * g)
                sp.dma_start(wp[:, :, :, :], w_qkv[g]).then_inc(s["w_loaded"], 16)

            def load_late(g):
                wait(sp, s["z_done"], B * g)
                sp.dma_start(wz[:, :, :], w_z[g]).then_inc(s["wz_loaded"], 16)
                wait(sp, s["out_done"], B * g)
                sp.dma_start(wo[:, :, :], w_out[g]).then_inc(s["wo_loaded"], 16)

            def load_steps(g):
                load_decays(g * B)
                load_late(g)
                with sp.Fori(1, B) as b:
                    load_decays(g * B + b)

            load_head(0)
            load_steps(0)
            with sp.Fori(1, steps // B) as g:
                load_head(g)
                load_steps(g)

        @block.tensor
        def _(pe):
            mm, tr = nc.tensor.matmul, nc.tensor.transpose

            def project(j):
                pe.wait_ge(s["w_loaded"], 16 * (head(j) + 1))
                for bank, f0 in ((X0, 0), (X1, 2)):
                    if f0 == 0:
                        wait(pe, s["ns_done"], j)
                    else:
                        wait(pe, s["V_done"], 2 * j)
                    for f in (f0, f0 + 1):
                        for k in range(KT):
                            ins = mm(bank[:, (f - f0) * S:(f - f0 + 1) * S], wp[:, k, f, :],
                                     c.xnT[:, k, bass.ds(seq(j) * S, S)], start=(k == 0), stop=(k == KT - 1))
                    ins.then_inc(s["qkv_done"], 1)

            def project_z(j, n):
                t, k = n // KT, n % KT
                if n == 0:
                    pe.wait_ge(s["wz_loaded"], 16 * (head(j) + 1))
                    pe.wait_ge(s["xb_loaded"], 16 * (j + 1))
                    wait(pe, s["zs_done"], j)
                ins = mm(X2[:, t * S:(t + 1) * S], xb[:, k, t * P:(t + 1) * P], wz[:, k, :],
                         start=(k == 0), stop=(k == KT - 1))
                if n == 3:
                    ins.then_inc(s["z_done"], 1)

            def square_sums(j):
                pe.wait_ge(s["sq_done"], j + 1)
                pe.wait_ge(s["conv_done"], 12 * (j + 1))
                for i in range(2):
                    for t in range(2):
                        ins = mm(X0[:, 2 * i + t:2 * i + t + 1], sq[:, i, t * P:(t + 1) * P], c.ones[:, 0:1],
                                 start=True, stop=True)
                ins.then_inc(s["ssum_done"], 1)

            def turn_v(j):
                pe.wait_ge(s["silu_done"], 2 * (j + 1))
                for t in range(2):
                    for h in range(2):
                        ins = tr(X1[:, (2 * t + h) * P:(2 * t + h + 1) * P], s2[:, 2 + h, t * P:(t + 1) * P],
                                 c.ident[:, :])
                ins.then_inc(s["vt_done"], 1)

            def gram(j):
                mm(TR[1][:, :], s2[:, 0, 0:P], s2[:, 0:2, :], start=True, stop=True).then_inc(s["gram_done"], 1)
                wait(pe, s["v1_done"], j)
                mm(S1[1][:, 0:S], s2[:, 0, P:S], s2[:, 0:2, P:S], start=True, stop=True).then_inc(s["gram_done"], 1)

            def turn_r(j):
                pe.wait_ge(s["r1_done"], j + 1)
                for i in range(4):
                    ins = tr(TR[0][:, i * P:(i + 1) * P], R[:, i, :], c.ident[:, :])
                ins.then_inc(s["t1_done"], 1)

            def turn_output(j):
                pe.wait_ge(s["og_done"], j + 1)
                for i in range(4):
                    ins = tr(X3[:, i * P:(i + 1) * P], og[:, i, :], c.ident[:, :])
                ins.then_inc(s["ogT_done"], 1)

            def project_out(j, n):
                t, h = n // 2, n % 2
                if n == 0:
                    pe.wait_ge(s["wo_loaded"], 16 * (head(j) + 1))
                    pe.wait_ge(s["ogT_copied"], j + 1)
                ins = mm(X3[:, t * S:(t + 1) * S], ogT[:, 2 * t + h, :], wo[:, h, :],
                         start=(h == 0), stop=(h == 1))
                if n == 3:
                    ins.then_inc(s["out_done"], 1)

            def join(j, l, a):
                pe.wait_ge(s["cm_done"], LEVELS * j + l + 1)
                if l == 0:
                    pe.wait_ge(s["t1_copied"], j + 1)
                else:
                    pe.wait_ge(s["tr_copied"], 2 * (LEVELS * j + l - 1) + a + 1)
                for i in (2 * a, 2 * a + 1):
                    ins = mm(S1[a][:, (i % 2) * P:(i % 2 + 1) * P], cm[:, l, i, :], T[:, i, :],
                             start=True, stop=True)
                ins.then_inc(s["s1_done"], 1)

            def grow_inverse(j, l, a):
                pe.wait_ge(s["w_done"], 2 * (LEVELS * j + l) + a + 1)
                for i in (2 * a, 2 * a + 1):
                    o = (i % 2) * P
                    mm(TR[a][:, o:o + P], R[:, i, :], W[:, i, :], start=True, stop=True)
                    ins = mm(TR[a][:, 2 * P + o:3 * P + o], W[:, i, :], R[:, i, :], start=True, stop=True)
                ins.then_inc(s["tr_done"], 1)

            def join64(j):
                pe.wait_ge(s["tr_copied"], 2 * LEVELS * (j + 1))
                for i in range(4):
                    ins = mm(S1[0][64:P, i * 64:(i + 1) * 64], dg[:, i, 64:P], T[:, i, 0:64],
                             start=True, stop=True)
                ins.then_inc(s["s64_done"], 1)

            def corner64(j):
                pe.wait_ge(s["s64_copied"], j + 1)
                for i in range(4):
                    ins = mm(S1[1][0:64, i * 64:(i + 1) * 64], s64[:, i, :], R[:, i, 64:P],
                             start=True, stop=True)
                ins.then_inc(s["r64_done"], 1)

            def solve0(j):
                pe.wait_ge(s["r64_copied"], j + 1)
                for h in range(2):
                    ins = mm(S1[0][:, h * P:(h + 1) * P], R[:, h, :], V[:, 0, h, :], start=True, stop=True)
                ins.then_inc(s["z0_done"], 1)

            def carry(j):
                pe.wait_ge(s["z0_copied"], j + 1)
                for h in range(2):
                    ins = mm(S1[1][:, h * P:(h + 1) * P], up[:, 2, h, :], Z0[:, h, :], start=True, stop=True)
                ins.then_inc(s["a21_done"], 1)

            def solve1(j):
                pe.wait_ge(s["v1_done"], j + 1)
                for h in range(2):
                    ins = mm(TR[0][:, h * P:(h + 1) * P], R[:, 2 + h, :], V1[:, h, :], start=True, stop=True)
                ins.then_inc(s["z1_done"], 1)

            def output_of_0(j):
                wait(pe, s["acc_done"], j)
                for t in range(2):
                    for h in range(2):
                        mm(X3[:, (2 * t + h) * P:(2 * t + h + 1) * P], up[:, 4 + 2 * t, h, :], Z0[:, h, :],
                           start=(t == 0 and h == 0), stop=(t == 0), skip_group_check=True)

            def output_of_1(j):
                pe.wait_ge(s["z1_copied"], j + 1)
                for h in range(2):
                    ins = mm(X3[:, (2 + h) * P:(3 + h) * P], up[:, 3, h, :], Z1[:, h, :],
                             start=False, stop=True, skip_group_check=True)
                ins.then_inc(s["o_done"], 1)

            def body(j, before, after):
                if after:
                    project(j + 1)
                turn_r(j)
                project_z(j, 0)
                project_z(j, 1)
                if before:
                    turn_output(j - 1)
                for l in range(LEVELS):
                    join(j, l, 0)
                    if l == LEVELS - 1:
                        project_z(j, 2)
                    elif before:
                        project_out(j - 1, l)
                    join(j, l, 1)
                    grow_inverse(j, l, 0)
                    grow_inverse(j, l, 1)
                project_z(j, 3)
                join64(j)
                if after:
                    square_sums(j + 1)
                corner64(j)
                if after:
                    turn_v(j + 1)
                solve0(j)
                carry(j)
                output_of_0(j)
                solve1(j)
                output_of_1(j)
                if after:
                    gram(j + 1)

            pe.wait_ge(s["misc_loaded"], 32)
            project(0)
            square_sums(0)
            turn_v(0)
            gram(0)
            body(0, False, True)
            with pe.Fori(1, steps - 1) as j:
                body(j, True, True)
            body(steps - 1, True, False)
            turn_output(steps - 1)
            for n in range(4):
                project_out(steps - 1, n)

        @block.scalar
        def _(act):
            f = nc.scalar.activation

            def last_tap(j):
                act.wait_ge(s["misc_loaded"], 32)
                for i in range(NF):
                    act.wait_ge(s["qkv_done"], 2 * j + i // 2 + 1)
                    if i == 0:
                        wait(act, s["silu_done"], 2 * j)
                        wait(act, s["thv_done"], j)
                    bank = (X0, X1)[i // 2]
                    f(cv[:, i, :], bank[:, (i % 2) * S:(i % 2 + 1) * S], ACT.Copy,
                      scale=cwj[:, i, TAPS - 1:TAPS]).then_inc(s["tap_done"], 1)

            def load_taps(j):
                wait(act, s["conv_done"], 12 * j)
                act.wait_ge(s["misc_loaded"], 32)
                f(cwj[:, :, :], cw[:, head(j), :, :], ACT.Copy).then_inc(s["cols_done"], 1)
                act.wait_ge(s["cols_done"], j + 1)

            def load_tokens(j):
                act.dma_start(xb[:, :, :], c.xnT[:, :, bass.ds(seq(j) * S, S)]).then_inc(s["xb_loaded"], 16)

            def tanh_z(j):
                act.wait_ge(s["z_done"], j + 1)
                wait(act, s["zs_done"], j)
                f(thz[:, :, :], X2[:, :].rearrange("p (t n) -> p t n", t=2), ACT.Tanh, scale=0.5)\
                    .then_inc(s["thz_done"], 1)

            def copy_t(j):
                act.wait_ge(s["t1_done"], j + 1)
                f(T[:, :, :], TR[0][:, :].rearrange("p (i t) -> p i t", i=4), ACT.Copy).then_inc(s["t1_copied"], 1)

            def copy_ogT(j):
                act.wait_ge(s["ogT_done"], j + 1)
                f(ogT[:, :, :], X3[:, :].rearrange("p (i t) -> p i t", i=4), ACT.Copy, scale=nw[:, 0:1])\
                    .then_inc(s["ogT_copied"], 1)

            def copy_level(j, l):
                for a in range(2):
                    act.wait_ge(s["tr_done"], 2 * (LEVELS * j + l) + a + 1)
                    f(TRs[:, :, 2 * a:2 * a + 2, :], TR[a][:, :].rearrange("p (x i t) -> p x i t", x=2, i=2),
                      ACT.Copy).then_inc(s["tr_copied"], 1)

            def tanh_qkv(j):
                act.wait_ge(s["conv_done"], 12 * j + 12)
                wait(act, s["silu_done"], 2 * j)
                f(th[:, 0:2, :], cv[:, 0:2, :], ACT.Tanh, scale=0.5).then_inc(s["thqk_done"], 1)
                f(th[:, 2:4, :], cv[:, 2:4, :], ACT.Tanh, scale=0.5).then_inc(s["thv_done"], 1)

            def squares(j):
                act.wait_ge(s["silu_done"], 2 * j + 1)
                wait(act, s["ssum_done"], j)
                f(sq[:, :, :], s2[:, 0:2, :], ACT.Square).then_inc(s["sq_done"], 1)

            def decays(j):
                act.wait_ge(s["arg_done"], 4 * (j + 1))
                wait(act, s["up_done"], 4 * j)
                f(dec[:, :, :], arg[:, :, :], ACT.Exp).then_inc(s["dec_done"], 1)

            def copy_V(j):
                act.wait_ge(s["vt_done"], j + 1)
                act.wait_ge(s["kn_done"], j + 1)
                wait(act, s["v1_done"], j)
                wait(act, s["z0_done"], j)
                for t in range(2):
                    f(V[:, t, :, :], X1[:, t * S:(t + 1) * S].rearrange("p (h d) -> p h d", h=2), ACT.Copy,
                      scale=kn[:, t:t + 1]).then_inc(s["V_done"], 1)

            def copy_z(j, bank, done, to, copied):
                act.wait_ge(s[done], j + 1)
                f(to[:, :, :], bank[:, 0:S].rearrange("p (h d) -> p h d", h=2), ACT.Copy).then_inc(s[copied], 1)

            def output_squares(j):
                act.wait_ge(s["o_done"], j + 1)
                wait(act, s["orr_done"], j)
                for i in range(4):
                    f(osq[:, i, :], X3[:, i * P:(i + 1) * P], ACT.Square, accum_out=oss[:, i:i + 1])\
                        .then_inc(s["oss_done"], 1)

            def body(j, before, after):
                copy_t(j)
                if after:
                    load_taps(j + 1)
                    last_tap(j + 1)
                if before:
                    copy_ogT(j - 1)
                for l in range(LEVELS - 1):
                    copy_level(j, l)
                if after:
                    tanh_qkv(j + 1)
                copy_level(j, LEVELS - 1)
                tanh_z(j)
                if after:
                    load_tokens(j + 1)
                    squares(j + 1)
                    decays(j + 1)
                copy_z(j, S1[0], "z0_done", Z0, "z0_copied")
                copy_z(j, TR[0], "z1_done", Z1, "z1_copied")
                if after:
                    copy_V(j + 1)
                output_squares(j)

            load_tokens(0)
            load_taps(0)
            last_tap(0)
            tanh_qkv(0)
            squares(0)
            decays(0)
            copy_V(0)
            body(0, False, True)
            with act.Fori(1, steps - 1) as j:
                body(j, True, True)
            body(steps - 1, True, False)
            copy_ogT(steps - 1)

        @block.vector
        def _(vec):
            stt = nc.vector.scalar_tensor_tensor

            def seed_inverse(j):
                vec.wait_ge(s["up_done"], 4 * (j + 1))
                wait(vec, s["r1_done"], j)
                nc.vector.tensor_tensor(seed[:, :, :], dg, c.level[:, 0:1, :].to_broadcast([P, 4, P]), ALU.mult)\
                    .then_inc(s["tmp_done"], 1)
                vec.wait_ge(s["tmp_done"], j + 1)
                wait(vec, s["z1_done"], j)
                nc.vector.tensor_tensor(R, seed[:, :, :], c.ident[:, None, :].to_broadcast([P, 4, P]), ALU.add)\
                    .then_inc(s["r1_done"], 1)

            def gate_output(j):
                vec.wait_ge(s["rs_done"], j + 1)
                vec.wait_ge(s["zs_done"], j + 1)
                wait(vec, s["ogT_done"], j)
                for i in range(4):
                    ins = stt(out=og[:, i, :], in0=X3[:, i * P:(i + 1) * P], scalar=rs[:, i:i + 1],
                              in1=zs[:, i // 2, (i % 2) * P:(i % 2 + 1) * P], op0=ALU.mult, op1=ALU.mult)
                ins.then_inc(s["og_done"], 1)

            def w_of_level(j, l):
                for a in range(2):
                    vec.wait_ge(s["s1_done"], 2 * (LEVELS * j + l) + a + 1)
                    nc.vector.tensor_tensor(W[:, 2 * a:2 * a + 2, :], c.ident[:, None, :].to_broadcast([P, 2, P]),
                                            S1[a][:, 0:S].rearrange("p (i t) -> p i t", i=2), ALU.subtract)\
                        .then_inc(s["w_done"], 1)

            def accumulate(j):
                vec.wait_ge(s["out_done"], j + 1)
                wait(vec, s["acc_done"], j)
                rows = c.y[:, bass.ds(2 * seq(j), 2), :]
                nc.vector.tensor_tensor(rows, rows, X3[:, :].rearrange("p (t n) -> p t n", t=2), ALU.add)\
                    .then_inc(s["acc_done"], 1)

            def silu_z(j):
                vec.wait_ge(s["thz_done"], j + 1)
                stt(out=zs[:, :, :], in0=thz[:, :, :], scalar=1.0, in1=X2[:, :].rearrange("p (t n) -> p t n", t=2),
                    op0=ALU.add, op1=ALU.mult).then_inc(s["zs_done"], 1)

            def other_taps(j, which):
                vec.wait_ge(s["tap_done"], 4 * (j + 1))
                for n in which:
                    shift, i = n // NF + 1, n % NF
                    wait(vec, s["conv_done"], 12 * j + n - NF + 1)
                    bank = (X0, X1)[i // 2]
                    stt(out=cv[:, i, shift:S], in0=bank[:, (i % 2) * S:(i % 2 + 1) * S - shift],
                        scalar=cwj[:, i, TAPS - 1 - shift:TAPS - shift], in1=cv[:, i, shift:S],
                        op0=ALU.mult, op1=ALU.add).then_inc(s["conv_done"], 1)

            def silu_qkv(j):
                for n, ready in enumerate(("thqk_done", "thv_done")):
                    vec.wait_ge(s[ready], j + 1)
                    stt(out=s2[:, 2 * n:2 * n + 2, :], in0=th[:, 2 * n:2 * n + 2, :], scalar=1.0,
                        in1=cv[:, 2 * n:2 * n + 2, :], op0=ALU.add, op1=ALU.mult).then_inc(s["silu_done"], 1)

            def exponents(j):
                wait(vec, s["sc_done"], j)
                tiles, heads = bass.ds(2 * seq(j), 2), bass.ds(2 * head(j), 2)
                nc.vector.tensor_copy(gcol[:, :, :], c.G[:, tiles, heads]).then_inc(s["halves"], 1)
                nc.vector.tensor_copy(bcol[:, :, :], c.beta[:, tiles, heads]).then_inc(s["halves"], 1)
                vec.wait_ge(s["halves"], 2 * (j + 1))
                vec.wait_ge(s["grow_loaded"], 16 * (j + 1))
                wait(vec, s["dec_done"], j)
                for h in range(2):
                    stt(out=arg[:, h, 0:S], in0=grow[:, h, :], scalar=gcol[:, 0, h:h + 1], in1=c.cut[:, :],
                        op0=ALU.subtract, op1=ALU.min).then_inc(s["arg_done"], 1)
                    stt(out=arg[:, h, S:3 * P], in0=grow[:, h, P:S], scalar=gcol[:, 1, h:h + 1], in1=c.cut[:, 0:P],
                        op0=ALU.subtract, op1=ALU.min).then_inc(s["arg_done"], 1)

            def norms(j):
                vec.wait_ge(s["ssum_done"], j + 1)
                wait(vec, s["kn_done"], j)
                wait(vec, s["nq_done"], j)
                nc.vector.tensor_scalar(ns[:, :], X0[:, 0:4], 4.0 * DELTA_EPS ** 2, None, ALU.max)\
                    .then_inc(s["ns_done"], 1)
                vec.wait_ge(s["ns_done"], j + 1)
                wait(vec, s["sc_done"], j)
                nc.vector.reciprocal(rk[:, :], ns[:, 0:2]).then_inc(s["rk_done"], 1)
                vec.wait_ge(s["rk_done"], j + 1)
                wait(vec, s["up_done"], 4 * j)
                nc.vector.tensor_tensor(sc[:, :, :], bcol[:, :, :], rk[:, :, None].to_broadcast([P, 2, 2]), ALU.mult)\
                    .then_inc(s["sc_done"], 1)

            def inverse64(j):
                vec.wait_ge(s["s64_done"], j + 1)
                nc.vector.tensor_copy(s64[64:P, :, :], S1[0][64:P, 0:S].rearrange("p (i t) -> p i t", i=4))\
                    .then_inc(s["s64_copied"], 1)
                vec.wait_ge(s["r64_done"], j + 1)
                nc.vector.tensor_scalar(R[0:64, :, 64:P], S1[1][0:64, 0:S].rearrange("p (i t) -> p i t", i=4),
                                        -1.0, None, ALU.mult).then_inc(s["r64_copied"], 1)

            def second_tile(j):
                vec.wait_ge(s["a21_done"], j + 1)
                nc.vector.tensor_tensor(V1[:, :, :], V[:, 1, :, :], S1[1][:, 0:S].rearrange("p (h d) -> p h d", h=2),
                                        ALU.subtract).then_inc(s["v1_done"], 1)

            def scale_gram(j):
                vec.wait_ge(s["dec_done"], j + 1)
                vec.wait_ge(s["sc_done"], j + 1)
                for bank, tile, n in ((TR[1], 0, 2), (S1[1], 1, 1)):
                    vec.wait_ge(s["gram_done"], 2 * j + tile + 1)
                    for h in range(2):
                        to = up[:, 0:8:2, h, :] if tile == 0 else up[:, 1:5:2, h, :]
                        d = dec[:, h, 0:S] if tile == 0 else dec[:, h, S:3 * P]
                        stt(out=to.rearrange("p (x n) t -> p x n t", x=2),
                            in0=bank[:, 0:2 * n * P].rearrange("p (x n t) -> p x n t", x=2, n=n),
                            scalar=sc[:, tile, h:h + 1],
                            in1=d.rearrange("p (n t) -> p n t", n=n)[:, None, :, :].to_broadcast([P, 2, n, P]),
                            op0=ALU.mult, op1=ALU.mult).then_inc(s["up_done"], 1)

            def root_mean_square(j):
                vec.wait_ge(s["oss_done"], 4 * (j + 1))
                vec.wait_ge(s["nq_done"], j + 1)
                wait(vec, s["rs_done"], j)
                stt(out=orr[:, :].rearrange("p (t h) -> p t h", t=2), in0=oss[:, :].rearrange("p (t h) -> p t h", t=2),
                    scalar=4.0 / DK, in1=nq[:, :, None].to_broadcast([P, 2, 2]),
                    op0=ALU.mult, op1=ALU.add).then_inc(s["orr_done"], 1)

            def q_guard(j):
                vec.wait_ge(s["ns_done"], j + 1)
                wait(vec, s["orr_done"], j)
                nc.vector.tensor_scalar(nq[:, :], ns[:, 2:4], 4.0 * EPS_Q, None, ALU.mult).then_inc(s["nq_done"], 1)

            def body(j, before, after):
                seed_inverse(j)
                if before:
                    gate_output(j - 1)
                for l in range(LEVELS):
                    w_of_level(j, l)
                    if after and l < 3:
                        other_taps(j + 1, range(4 * l, 4 * l + 4))
                    if after and l == 3:
                        exponents(j + 1)
                if before:
                    accumulate(j - 1)
                if after:
                    silu_qkv(j + 1)
                inverse64(j)
                silu_z(j)
                if after:
                    norms(j + 1)
                second_tile(j)
                root_mean_square(j)
                if after:
                    q_guard(j + 1)
                    scale_gram(j + 1)

            nc.vector.memset(c.y[:, :, :], 0.0).then_inc(s["zeroed"], 1)
            nc.vector.memset(s64[0:64, :, :], 0.0).then_inc(s["zeroed"], 1)
            vec.wait_ge(s["zeroed"], 2)
            other_taps(0, range(12))
            exponents(0)
            silu_qkv(0)
            norms(0)
            q_guard(0)
            scale_gram(0)
            body(0, False, True)
            with vec.Fori(1, steps - 1) as j:
                body(j, True, True)
            body(steps - 1, True, False)
            gate_output(steps - 1)
            accumulate(steps - 1)

        @block.gpsimd
        def _(pool):
            tt = nc.gpsimd.tensor_tensor

            def joining_blocks(j):
                pool.wait_ge(s["up_done"], 4 * (j + 1))
                for l in range(LEVELS):
                    wait(pool, s["s1_done"], 2 * LEVELS * (j - 1) + 2 * l + 2)
                    tt(cm[:, l, :, :], dg, c.level[:, l + 1:l + 2, :].to_broadcast([P, 4, P]), ALU.mult)\
                        .then_inc(s["cm_done"], 1)

            def key_norm(j):
                pool.wait_ge(s["ns_done"], j + 1)
                wait(pool, s["V_done"], 2 * j)
                tt(kn[:, :], ns[:, 0:2], half[:, 0:2], ALU.pow).then_inc(s["kn_done"], 1)

            def output_scale(j):
                pool.wait_ge(s["orr_done"], j + 1)
                wait(pool, s["og_done"], j)
                tt(rs[:, :], orr[:, :], mhalf[:, :], ALU.pow).then_inc(s["rs_done"], 1)

            nc.gpsimd.memset(half[:, :], 0.5).then_inc(s["powers"], 1)
            nc.gpsimd.memset(mhalf[:, :], -0.5).then_inc(s["powers"], 1)
            pool.wait_ge(s["powers"], 2)
            key_norm(0)
            joining_blocks(0)
            key_norm(1)
            output_scale(0)
            with pool.Fori(1, steps - 1) as j:
                joining_blocks(j)
                key_norm(j + 1)
                output_scale(j)
            joining_blocks(steps - 1)
            output_scale(steps - 1)

        inner.close()
        m.clear()


CH = 512
NCH = TOK // CH


class FeedForward:

    def __init__(self, m, tag, xnT, gate, up, down, inner, y, banks):
        self.tag, self.xnT, self.gate, self.up, self.down, self.y = tag, xnT, gate, up, down, y
        self.tiles = [(i, min(P, inner - i)) for i in range(0, inner, P)]
        self.n = len(self.tiles)
        self.pairs, self.out = [(banks[0], banks[1]), (banks[2], banks[3]), (banks[4], banks[5])], banks[6:8]
        self.th = m.sb(tag + "th", [P, 2, CH])
        self.gated = m.sb(tag + "gated", [P, 2, CH])
        self.hid = m.sb(tag + "hid", [P, self.n, CH])
        self.inner_done, self.tanh_done, self.gated_done, self.hid_done, self.out_done, self.out_copied = (
            m.sem(tag + n) for n in ("inner_done", "tanh_done", "gated_done", "hid_done", "out_done", "out_copied"))

    def tensor(self, nc, pe, c):
        for i, (lo, rows) in enumerate(self.tiles):
            t = c * self.n + i
            wait(pe, self.hid_done, t - 2)
            for w, bank in ((self.gate, self.pairs[i % 3][0]), (self.up, self.pairs[i % 3][1])):
                for k in range(KT):
                    ins = nc.tensor.matmul(bank[0:rows, :], w[:, k, lo:lo + rows],
                                           self.xnT[:, k, bass.ds(c * CH, CH)], start=(k == 0), stop=(k == KT - 1))
            ins.then_inc(self.inner_done, 1)
        pe.wait_ge(self.hid_done, (c + 1) * self.n)
        for half in range(2):
            wait(pe, self.out_copied, 2 * (c - 1) + half + 1)
            for r in range(2):
                s = (2 * half + r) * P
                for i, (lo, rows) in enumerate(self.tiles):
                    ins = nc.tensor.matmul(self.out[half][:, r * H:(r + 1) * H], self.hid[0:rows, i, s:s + P],
                                           self.down[0:rows, i, :], start=(i == 0), stop=(i == self.n - 1))
            ins.then_inc(self.out_done, 1)

    def scalar(self, nc, act, c):
        for i, (lo, rows) in enumerate(self.tiles):
            t = c * self.n + i
            act.wait_ge(self.inner_done, t + 1)
            wait(act, self.gated_done, t - 1)
            nc.scalar.activation(self.th[0:rows, i % 2, :], self.pairs[i % 3][0][0:rows, :], ACT.Tanh, scale=0.5)\
                .then_inc(self.tanh_done, 1)
        for half in range(2):
            act.wait_ge(self.out_done, 2 * c + half + 1)
            nc.scalar.activation(self.y[:, bass.ds(4 * c + 2 * half, 2), :],
                                 self.out[half][:, :].rearrange("p (t n) -> p t n", t=2), ACT.Copy)\
                .then_inc(self.out_copied, 1)

    def vector(self, nc, vec, c):
        stt = nc.vector.scalar_tensor_tensor
        for i, (lo, rows) in enumerate(self.tiles):
            t = c * self.n + i
            gate, up = self.pairs[i % 3]
            g = self.gated[0:rows, i % 2, :]
            vec.wait_ge(self.tanh_done, t + 1)
            wait(vec, self.hid_done, t - 1)
            stt(out=g, in0=self.th[0:rows, i % 2, :], scalar=1.0, in1=gate[0:rows, :], op0=ALU.add, op1=ALU.mult)\
                .then_inc(self.gated_done, 1)
            vec.wait_ge(self.gated_done, t + 1)
            if i == 0:
                wait(vec, self.out_done, 2 * c)
            stt(out=self.hid[0:rows, i, :], in0=g, scalar=0.5, in1=up[0:rows, :], op0=ALU.mult, op1=ALU.mult)\
                .then_inc(self.hid_done, 1)


E, TOPK, I_E, I_S, CAP = 16, 4, 176, 352, 128
IR = I_E - P
NS = (I_S + P - 1) // P


def experts(nc, c, gate_w, w_gate, w_up, w_down, sw_gate, sw_up, sw_down, rows_dram, out_dram):
    NSLOT = E * CAP
    with ExitStack() as stack:
        m = Memory(nc, stack)
        gw = m.sb("gw", [P, KT, E])
        sg = m.sb("sg", [P, KT, I_S])
        su = m.sb("su", [P, KT, I_S])
        sd = m.sb("sd", [P, NS, H])
        zero = m.sb("zero", [P, 4, H])
        lg = m.sb("lg", [P, NT, E])
        mx = m.sb("mx", [P, NT])
        ex = m.sb("ex", [P, NT, E])
        sm = m.sb("sm", [P, NT])
        rc = m.sb("rc", [P, NT])
        score = m.sb("score", [P, NT, E])
        top = m.sb("top", [P, NT, 8])
        topi = m.sb("topi", [P, NT, 8], U32)
        topf = m.sb("topf", [P, NT, 8])
        den = m.sb("den", [P, NT])
        wgt = m.sb("wgt", [P, NT, TOPK])
        iota_e = m.sb("iota_e", [P, E])
        hot = m.sb("hot", [P, TOPK, NT, E])
        mask = m.sb("mask", [P, NT, E])
        before = m.sb("before", [P, NT, E])
        rank = m.sb("rank", [P, NT, E])
        mine = m.sb("mine", [P, TOPK, NT, E])
        rk = m.sb("rk_e", [P, TOPK, NT])
        fits = m.sb("fits", [P, TOPK, NT])
        slot = m.sb("slot", [P, TOPK, NT])
        slot_i = m.sb("slot_i", [P, TOPK, NT], U32)
        got = m.sb("got", [P, NT, TOPK, H])
        xe = m.sb("xe", [P, 2, H])
        xT = m.sb("xT", [P, 2, KT, P])
        wg = m.sb("wg", [P, 2, KT, I_E])
        wu = m.sb("wu", [P, 2, KT, I_E])
        wd0 = m.sb("wd0", [P, 2, H])
        wd1 = m.sb("wd1", [IR, 2, H])
        th = m.sb("th_e", [P, 2, 2, P])
        ga = m.sb("ga_e", [P, 2, 2, P])
        hT = m.sb("hT_e", [P, 2, 2, P])
        eo = m.sb("eo", [P, 2, H])
        banks = [m.ps(f"me{i}") for i in range(8)]
        XT, GU, EO = banks[0:2], banks[2:4], banks[4:6]
        ff = FeedForward(m, "sh_", c.xnT, sg, su, sd, I_S, c.y, banks)
        ROUTED = 3 + 2 * NT + 3 + TOPK + 1 + NT
        names = ("small_loaded shared_loaded zero_ready zeroed logits_done iota_done route exp_done ranks_done slots_ready "
                 "scattered turned turned_copied inner_done tanh_done gated_done "
                 "hid_done outer_done outer_copied combined").split()
        s = {n: m.sem("m_" + n) for n in names}
        weights_loaded, rows_loaded, stored = ([m.sem(f"m_{n}{u}") for u in range(2)]
                                               for n in ("weights_loaded", "rows_loaded", "stored"))
        gathered = [m.sem(f"m_gathered{i}") for i in range(4)]
        inner = stack.enter_context(ExitStack())
        block = inner.enter_context(nc.Block())

        def round_of(e, u):
            return (e - u) // 2 + 1

        @block.sync
        def _(sp):
            sp.dma_start(gw[:, :, :], gate_w).then_inc(s["small_loaded"], 16)
            for w, src in ((sg, sw_gate), (su, sw_up)):
                sp.dma_start(w[:, :, :], src.rearrange("(k p) i -> p k i", p=P)).then_inc(s["shared_loaded"], 16)
            for i in range(NS):
                r = min(P, I_S - i * P)
                sp.dma_start(sd[0:r, i, :], sw_down[i * P:i * P + r, :]).then_inc(s["shared_loaded"], 16)
            sp.wait_ge(s["zero_ready"], 1)
            for i in range(NSLOT // 512):
                sp.dma_start(rows_dram[512 * i:512 * i + 512, :].rearrange("(p n) h -> p n h", p=P), zero[:, :, :])\
                    .then_inc(s["zeroed"], 16)
            sp.dma_start(out_dram[NSLOT:NSLOT + 1, :], zero[0:1, 0, :]).then_inc(s["zeroed"], 16)

            def load(e, u):
                wait(sp, s["hid_done"], e - 1)
                for w, src in ((wg, w_gate), (wu, w_up)):
                    sp.dma_start(w[:, u, :, :], src[e].rearrange("(k p) i -> p k i", p=P))\
                        .then_inc(weights_loaded[u], 16)
                wait(sp, s["outer_copied"], e - 1)
                sp.dma_start(wd0[:, u, :], w_down[e, 0:P, :]).then_inc(weights_loaded[u], 16)
                sp.dma_start(wd1[:, u, :], w_down[e, P:I_E, :]).then_inc(weights_loaded[u], 16)
                if isinstance(e, int) and e == 0:
                    sp.wait_ge(s["scattered"], 16 * NT * TOPK)
                wait(sp, s["turned"], e - 1)
                sp.dma_start(xe[:, u, :], rows_dram[e * CAP:(e + 1) * CAP, :] if isinstance(e, int)
                             else rows_dram[bass.ds(e * CAP, CAP), :]).then_inc(rows_loaded[u], 16)

            load(0, 0)
            load(1, 1)
            with sp.Fori(1, E // 2) as q:
                load(2 * q, 0)
                load(2 * q + 1, 1)

        @block.gpsimd
        def _(pool):
            nc.gpsimd.memset(zero[:, :, :], 0.0).then_inc(s["zero_ready"], 1)
            nc.gpsimd.iota(iota_e[:, :], pattern=[[1, E]], base=0, channel_multiplier=0,
                           allow_small_or_imprecise_dtypes=True).then_inc(s["iota_done"], 1)
            pool.wait_ge(s["zeroed"], 16 * (NSLOT // 512 + 1))
            pool.wait_ge(s["slots_ready"], 1)
            for t in range(NT):
                for k in range(TOPK):
                    nc.gpsimd.indirect_dma_start(
                        out=rows_dram, out_offset=bass.IndirectOffsetOnAxis(ap=slot_i[:, k, t:t + 1], axis=0),
                        in_=c.xn[:, t, :], in_offset=None, bounds_check=NSLOT - 1, oob_is_err=False)\
                        .then_inc(s["scattered"], 16)
            for u in range(2):
                pool.wait_ge(stored[u], 16 * E // 2)
            for t in range(NT):
                for k in range(TOPK):
                    nc.gpsimd.indirect_dma_start(
                        out=got[:, t, k, :], out_offset=None, in_=out_dram,
                        in_offset=bass.IndirectOffsetOnAxis(ap=slot_i[:, k, t:t + 1], axis=0))\
                        .then_inc(gathered[t // 4], 16)
            for i in range(4):
                pool.wait_ge(gathered[i], 16 * NT * TOPK // 4)

        @block.tensor
        def _(pe):
            mm, tr = nc.tensor.matmul, nc.tensor.transpose
            pe.wait_ge(s["small_loaded"], 16)
            for t in range(NT):
                for k in range(KT):
                    ins = mm(banks[6][:, t * E:(t + 1) * E], c.xnT[:, k, t * P:(t + 1) * P], gw[:, k, :],
                             start=(k == 0), stop=(k == KT - 1))
            ins.then_inc(s["logits_done"], 1)
            pe.wait_ge(s["route"], ROUTED)
            mm(banks[6][:, 0:NT * E], c.tri_strict[:, :], mask[:, :, :], start=True, stop=False)
            mm(banks[6][:, 0:NT * E], c.ones[:, :], before[:, :, :], start=False, stop=True)\
                .then_inc(s["ranks_done"], 1)

            def turn(e, u):
                pe.wait_ge(rows_loaded[u], 16 * round_of(e, u))
                wait(pe, s["turned_copied"], e - 1)
                for k in range(KT):
                    ins = tr(XT[u][:, k * P:(k + 1) * P], xe[:, u, k * P:(k + 1) * P], c.ident[:, :])
                ins.then_inc(s["turned"], 1)

            def inner(e, u):
                pe.wait_ge(weights_loaded[u], 64 * round_of(e, u))
                pe.wait_ge(s["turned_copied"], e + 1)
                wait(pe, s["hid_done"], e - 1)
                for n, w in enumerate((wg, wu)):
                    for i, (lo, rows) in enumerate(((0, P), (P, IR))):
                        for k in range(KT):
                            ins = mm(GU[u][0:rows, (2 * n + i) * P:(2 * n + i + 1) * P], w[:, u, k, lo:lo + rows],
                                     xT[:, u, k, :], start=(k == 0), stop=(k == KT - 1))
                ins.then_inc(s["inner_done"], 1)

            def outer(e, u):
                pe.wait_ge(s["hid_done"], e + 1)
                wait(pe, s["outer_copied"], e - 1)
                mm(EO[u][:, 0:H], hT[:, u, 0, :], wd0[:, u, :], start=True, stop=False)
                mm(EO[u][:, 0:H], hT[0:IR, u, 1, :], wd1[:, u, :], start=False, stop=True)\
                    .then_inc(s["outer_done"], 1)

            pe.wait_ge(s["shared_loaded"], 16 * (2 + NS))
            pe.wait_ge(s["route"], ROUTED + 1)
            ff.tensor(nc, pe, 0)
            ff.tensor(nc, pe, 1)
            pe.wait_ge(ff.out_copied, 4)
            turn(0, 0)
            inner(0, 0)
            turn(1, 1)
            inner(1, 1)

            def two(q):
                outer(2 * q - 2, 0)
                turn(2 * q, 0)
                inner(2 * q, 0)
                outer(2 * q - 1, 1)
                turn(2 * q + 1, 1)
                inner(2 * q + 1, 1)

            two(1)
            with pe.Fori(2, E // 2) as q:
                two(q)
            outer(E - 2, 0)
            outer(E - 1, 1)
            pe.wait_ge(s["outer_copied"], E)
            ff.tensor(nc, pe, 2)
            ff.tensor(nc, pe, 3)

        @block.scalar
        def _(act):
            f = nc.scalar.activation
            act.wait_ge(s["route"], 2)
            f(ex[:, :, :], lg[:, :, :], ACT.Exp).then_inc(s["exp_done"], 1)
            ff.scalar(nc, act, 0)
            ff.scalar(nc, act, 1)

            def first(e, u):
                act.wait_ge(s["turned"], e + 1)
                wait(act, s["inner_done"], e - 1)
                f(xT[:, u, :, :], XT[u][:, 0:S].rearrange("p (k t) -> p k t", k=KT), ACT.Copy)\
                    .then_inc(s["turned_copied"], 1)
                act.wait_ge(s["inner_done"], e + 1)
                wait(act, s["gated_done"], 2 * (e - 1))
                f(th[:, u, 0, :], GU[u][:, 0:P], ACT.Tanh, scale=0.5).then_inc(s["tanh_done"], 1)
                f(th[0:IR, u, 1, :], GU[u][0:IR, P:2 * P], ACT.Tanh, scale=0.5).then_inc(s["tanh_done"], 1)

            def second(e, u):
                act.wait_ge(s["outer_done"], e + 1)
                wait(act, stored[u], 16 * (round_of(e, u) - 1))
                f(eo[:, u, :], EO[u][:, 0:H], ACT.Copy).then_inc(s["outer_copied"], 1)
                to = out_dram[e * CAP:(e + 1) * CAP, :] if isinstance(e, int) else out_dram[bass.ds(e * CAP, CAP), :]
                act.wait_ge(s["outer_copied"], e + 1)
                act.dma_start(to, eo[:, u, :]).then_inc(stored[u], 16)

            first(0, 0)
            first(1, 1)

            def two(q):
                second(2 * q - 2, 0)
                first(2 * q, 0)
                second(2 * q - 1, 1)
                first(2 * q + 1, 1)

            two(1)
            with act.Fori(2, E // 2) as q:
                two(q)
            second(E - 2, 0)
            second(E - 1, 1)
            ff.scalar(nc, act, 2)
            ff.scalar(nc, act, 3)

        @block.vector
        def _(vec):
            stt, tt, ts = nc.vector.scalar_tensor_tensor, nc.vector.tensor_tensor, nc.vector.tensor_scalar
            n = 0

            def step(ins):
                nonlocal n
                n += 1
                ins.then_inc(s["route"], 1)

            def done(ins):
                step(ins)
                vec.wait_ge(s["route"], n)

            def over(col, width):
                return col[:, :, None].to_broadcast([P, NT, width])

            logits = banks[6][:, 0:NT * E].rearrange("p (t e) -> p t e", e=E)
            vec.wait_ge(s["logits_done"], 1)
            done(nc.vector.tensor_reduce(mx[:, :], logits, AX.X, ALU.max))
            done(tt(lg[:, :, :], logits, over(mx, E), ALU.subtract))
            vec.wait_ge(s["exp_done"], 1)
            done(nc.vector.tensor_reduce(sm[:, :], ex[:, :, :], AX.X, ALU.add))
            nc.vector.reciprocal(rc[:, :], sm[:, :]).then_inc(s["combined"], 1)
            vec.wait_ge(s["combined"], 1)
            tt(score[:, :, :], ex[:, :, :], over(rc, E), ALU.mult).then_inc(s["combined"], 1)
            vec.wait_ge(s["combined"], 2)
            for t in range(NT):
                step(nc.vector.max(top[:, t, :], score[:, t, :]))
            vec.wait_ge(s["route"], n)
            for t in range(NT):
                step(nc.vector.max_index(topi[:, t, :], top[:, t, :], score[:, t, :]))
            vec.wait_ge(s["route"], n)
            done(nc.vector.tensor_copy(topf[:, :, :], topi[:, :, :]))
            done(nc.vector.tensor_reduce(den[:, :], top[:, :, 0:TOPK], AX.X, ALU.add))
            done(nc.vector.tensor_scalar(den[:, :], den[:, :], 1e-20, None, ALU.add))
            nc.vector.reciprocal(rc[:, :], den[:, :]).then_inc(s["combined"], 1)
            vec.wait_ge(s["combined"], 3)
            tt(wgt[:, :, :], top[:, :, 0:TOPK], over(rc, TOPK), ALU.mult).then_inc(s["combined"], 1)
            vec.wait_ge(s["iota_done"], 1)
            for k in range(TOPK):
                step(tt(hot[:, k, :, :], iota_e[:, None, :].to_broadcast([P, NT, E]),
                        over(topf[:, :, k], E), ALU.is_equal))
            vec.wait_ge(s["route"], n)
            done(nc.vector.tensor_reduce(mask[:, :, :], hot[:, :, :, :].rearrange("p k t e -> p t e k"),
                                         AX.X, ALU.add))
            done(nc.vector.memset(before[:, 0, :], 0.0))
            for t in range(1, NT):
                done(tt(before[:, t, :], before[:, t - 1, :], mask[:, t - 1, :], ALU.add))
            assert n == ROUTED
            vec.wait_ge(s["ranks_done"], 1)
            done(nc.vector.tensor_copy(rank[:, :, :], banks[6][:, 0:NT * E].rearrange("p (t e) -> p t e", e=E)))
            for k in range(TOPK):
                step(tt(mine[:, k, :, :], hot[:, k, :, :], rank[:, :, :], ALU.mult))
            vec.wait_ge(s["route"], n)
            done(nc.vector.tensor_reduce(rk[:, :, :], mine[:, :, :, :], AX.X, ALU.add))
            done(ts(fits[:, :, :], rk[:, :, :], float(CAP), None, ALU.is_lt))
            done(stt(out=slot[:, :, :], in0=topf[:, :, 0:TOPK].rearrange("p t k -> p k t"), scalar=float(CAP),
                     in1=rk[:, :, :], op0=ALU.mult, op1=ALU.add))
            done(stt(out=slot[:, :, :], in0=slot[:, :, :], scalar=-float(NSLOT), in1=fits[:, :, :],
                     op0=ALU.add, op1=ALU.mult))
            ts(slot_i[:, :, :], slot[:, :, :], float(NSLOT), None, ALU.add).then_inc(s["slots_ready"], 1)
            ff.vector(nc, vec, 0)
            ff.vector(nc, vec, 1)

            def gate(e, u):
                for i, rows in enumerate((P, IR)):
                    vec.wait_ge(s["tanh_done"], 2 * e + 2)
                    if i == 0:
                        wait(vec, s["hid_done"], e - 1)
                    stt(out=ga[0:rows, u, i, :], in0=th[0:rows, u, i, :], scalar=1.0,
                        in1=GU[u][0:rows, i * P:(i + 1) * P], op0=ALU.add, op1=ALU.mult).then_inc(s["gated_done"], 1)
                for i, rows in enumerate((P, IR)):
                    vec.wait_ge(s["gated_done"], 2 * e + i + 1)
                    if i == 0:
                        wait(vec, s["outer_done"], e - 1)
                    ins = stt(out=hT[0:rows, u, i, :], in0=ga[0:rows, u, i, :], scalar=0.5,
                              in1=GU[u][0:rows, (2 + i) * P:(3 + i) * P], op0=ALU.mult, op1=ALU.mult)
                ins.then_inc(s["hid_done"], 1)

            gate(0, 0)
            gate(1, 1)
            with vec.Fori(1, E // 2) as q:
                gate(2 * q, 0)
                gate(2 * q + 1, 1)
            ff.vector(nc, vec, 2)
            ff.vector(nc, vec, 3)
            vec.wait_ge(ff.out_copied, 2 * NCH)
            n_c = 4
            for t0 in range(0, NT, 4):
                vec.wait_ge(gathered[t0 // 4], 16 * TOPK * 4)
                for k in range(TOPK):
                    for t in range(t0, t0 + 4):
                        if k:
                            vec.wait_ge(s["combined"], n_c - 3)
                        stt(out=c.y[:, t, :], in0=got[:, t, k, :], scalar=wgt[:, t, k:k + 1], in1=c.y[:, t, :],
                            op0=ALU.mult, op1=ALU.add).then_inc(s["combined"], 1)
                        n_c += 1
            vec.wait_ge(s["combined"], n_c)

        inner.close()
        m.clear()


HQ, HKV, DH = 16, 4, 128
QG = HQ // HKV
RANK = 32
MAX_LEN = 512.0
GAMMA_MIN = 1e-6
NB = QG + 2
SC = P + S
FAR = -1e30
ASTEPS = HKV * B


def attention_bias(nc, c, wa, wb, pol_dir, pol_gate, gtp):
    with ExitStack() as stack:
        m = Memory(nc, stack)
        wab = m.sb("wab_pol", [P, KT, 2, RANK])
        pd, gt, pg = (m.sb(n, [P, HQ]) for n in ("pol_dir_b", "gtp_b", "pol_gate_b"))
        mn, ex, ln, soft, pc, ch, tg = (m.sb("ab_" + n, [P, HQ]) for n in "mn ex ln soft pc ch tg".split())
        dist = m.sb("dist", [P, SC])
        cut = m.sb("later", [P, SC])
        at = m.sb("at", [RANK, TOK])
        bt = m.sb("bt", [RANK, TOK])
        banks = [m.ps(f"ab{i}") for i in range(4)]
        loaded, tables, dve, act_done, projected, copied, products, nb_step = (
            m.sem("bias_" + n) for n in "loaded tables dve act_done projected copied products nb_step".split())
        inner = stack.enter_context(ExitStack())
        block = inner.enter_context(nc.Block())

        @block.sync
        def _(sp):
            for i, w in enumerate((wa, wb)):
                sp.dma_start(wab[:, :, i, :], w.rearrange("(k p) r -> p k r", p=P)).then_inc(loaded, 16)
            for to, src in ((pd, pol_dir), (gt, gtp), (pg, pol_gate)):
                sp.dma_start(to[:, :], src[None, :].to_broadcast([P, HQ])).then_inc(loaded, 16)

        @block.gpsimd
        def _(pool):
            nc.gpsimd.iota(dist[:, 0:P], pattern=[[-1, P]], base=0, channel_multiplier=1,
                           allow_small_or_imprecise_dtypes=True).then_inc(tables, 1)
            nc.gpsimd.iota(dist[:, P:SC], pattern=[[-1, S]], base=P, channel_multiplier=1,
                           allow_small_or_imprecise_dtypes=True).then_inc(tables, 1)
            nc.gpsimd.memset(cut[:, :], 0.0).then_inc(tables, 1)
            pool.wait_ge(tables, 3)
            for lo, n, base in ((0, P, 0), (P, S, P)):
                nc.gpsimd.affine_select(out=cut[:, lo:lo + n], in_=cut[:, lo:lo + n], compare_op=ALU.is_ge, fill=FAR,
                                        base=base, pattern=[[-1, n]], channel_multiplier=1).then_inc(tables, 1)

        @block.tensor
        def _(pe):
            pe.wait_ge(loaded, 80)
            for i in range(2 * NCH):
                wait(pe, copied, i - 3)
                for k in range(KT):
                    ins = nc.tensor.matmul(banks[i % 4][0:RANK, :], wab[:, k, i // NCH, :],
                                           c.xnT[:, k, (i % NCH) * CH:(i % NCH + 1) * CH],
                                           start=(k == 0), stop=(k == KT - 1))
                ins.then_inc(projected, 1)
            pe.wait_ge(copied, 2 * NCH)
            for b in range(B):
                wait(pe, act_done, 4 + b - 3)
                t0 = b * S
                nc.tensor.matmul(banks[b % 4][:, 0:P], at[:, t0:t0 + P], bt[:, t0:t0 + P], start=True, stop=True)
                nc.tensor.matmul(banks[b % 4][:, P:SC], at[:, t0 + P:t0 + S], bt[:, t0:t0 + S],
                                 start=True, stop=True).then_inc(products, 1)

        @block.scalar
        def _(act):
            f = nc.scalar.activation
            act.wait_ge(dve, 1)
            f(ex[:, :], mn[:, :], ACT.Exp).then_inc(act_done, 1)
            act.wait_ge(act_done, 1)
            f(ln[:, :], ex[:, :], ACT.Ln, bias=c.ones[:, 0:1]).then_inc(act_done, 1)
            f(tg[:, :], pg[:, :], ACT.Tanh, scale=0.5).then_inc(act_done, 1)
            for b in range(B):
                act.wait_ge(products, b + 1)
                f(c.mt[:, b, :], banks[b % 4][:, 0:SC], ACT.Tanh, scale=0.5).then_inc(act_done, 1)

        @block.vector
        def _(vec):
            stt, ts = nc.vector.scalar_tensor_tensor, nc.vector.tensor_scalar
            n = 0

            def done(ins):
                nonlocal n
                n += 1
                ins.then_inc(dve, 1)
                vec.wait_ge(dve, n)

            vec.wait_ge(loaded, 80)
            done(stt(out=mn[:, :], in0=gt[:, :], scalar=-1.0, in1=gt[:, :], op0=ALU.mult, op1=ALU.min))
            for i in range(2 * NCH):
                vec.wait_ge(projected, i + 1)
                to = (at, bt)[i // NCH]
                nc.vector.tensor_copy(to[:, (i % NCH) * CH:(i % NCH + 1) * CH], banks[i % 4][0:RANK, :])\
                    .then_inc(copied, 1)
            vec.wait_ge(act_done, 3)
            done(stt(out=soft[:, :], in0=gt[:, :], scalar=0.0, in1=ln[:, :], op0=ALU.max, op1=ALU.add))
            done(ts(soft[:, :], soft[:, :], GAMMA_MIN, None, ALU.max))
            done(ts(pc[:, :], pd[:, :], -1.0, 1.0, ALU.max, ALU.min))
            done(stt(out=ch[:, :], in0=pc[:, :], scalar=-1.0 / MAX_LEN, in1=soft[:, :],
                     op0=ALU.mult, op1=ALU.subtract))
            done(ts(c.gh[:, :], tg[:, :], 0.25, 0.25, ALU.mult, ALU.add))
            vec.wait_ge(tables, 5)
            for h in range(HQ):
                ts(c.nb[:, h, :], dist[:, :], ch[:, h:h + 1], c.gh[:, h:h + 1], ALU.mult, ALU.add)\
                    .then_inc(nb_step, 1)
            vec.wait_ge(nb_step, HQ)
            nc.vector.tensor_tensor(c.nb[:, :, :], c.nb[:, :, :], cut[:, None, :].to_broadcast([P, HQ, SC]), ALU.add)\
                .then_inc(nb_step, 1)

        inner.close()
        m.clear()


def softmax_attention(nc, c, w_att, wo_att, rope):
    with ExitStack() as stack:
        m = Memory(nc, stack)
        wat = m.sb("wat", [P, KT, NB * P])
        wot = m.sb("wot", [P, QG, H])
        tab = m.sb("rope_tab", [P, 4, S])
        xs = m.sb("xs", [P, KT, S])
        mc = m.sb("mc", [P, QG + 1, S])
        ms = m.sb("ms", [P, QG + 1, S])
        qk = m.sb("qk", [P, QG + 1, S])
        v = m.sb("v_att", [P, 2, P])
        sc = m.sb("sc_att", [P, QG, SC])
        pr = m.sb("pr", [P, QG, SC])
        pT = m.sb("pT", [P, QG, SC])
        oT = m.sb("oT", [P, QG, S])
        mx, nm, sm, rc = (m.sb("at_" + n, [P, QG, 2]) for n in ("mx", "nm", "sm", "rc"))
        QA, QB, KV, OUT = (m.ps("at_" + n) for n in ("QA", "QB", "KV", "OUT"))
        SH = [m.ps(f"at_S{h}") for h in range(QG)]
        names = ("tab_loaded w_loaded wo_loaded x_loaded projected multiplied turned_qk v_copied scores_done biased "
                 "added max_done neg_done exp_done rc_done scaled turned pT_copied pv_done oT_copied out_done "
                 "y_added zeroed").split()
        s = {n: m.sem("t_" + n) for n in names}
        inner = stack.enter_context(ExitStack())
        block = inner.enter_context(nc.Block())

        def head(j):
            return j // B

        def seq(j):
            return j % B

        @block.sync
        def _(sp):
            sp.dma_start(tab[:, :, :], rope).then_inc(s["tab_loaded"], 16)

            def load_tokens(j):
                t0 = seq(j) * S if isinstance(j, int) else sp.snap(seq(j) * S)
                wait(sp, s["projected"], 3 * j - 2)
                sp.dma_start(xs[:, :, :], c.xnT[:, :, bass.ds(t0, S)]).then_inc(s["x_loaded"], 16)

            def load(g):
                wait(sp, s["projected"], 3 * B * g)
                sp.dma_start(wat[:, :, :], w_att[g]).then_inc(s["w_loaded"], 16)
                load_tokens(B * g)
                wait(sp, s["out_done"], B * g)
                sp.dma_start(wot[:, :, :], wo_att[g]).then_inc(s["wo_loaded"], 16)
                with sp.Fori(1, B) as b:
                    load_tokens(B * g + b)

            load(0)
            with sp.Fori(1, HKV) as g:
                load(g)

        @block.tensor
        def _(pe):
            mm, tr = nc.tensor.matmul, nc.tensor.transpose

            def project(j):
                pe.wait_ge(s["w_loaded"], 16 * (head(j) + 1))
                pe.wait_ge(s["x_loaded"], 16 * (j + 1))
                wait(pe, s["multiplied"], 9 * j)
                wait(pe, s["v_copied"], j)
                toks = bass.ds(seq(j) * S, S)
                for k in range(KT):
                    mm(KV[:, 0:S], wat[:, k, QG * P:(QG + 1) * P], c.xnT[:, k, toks],
                       start=(k == 0), stop=(k == KT - 1))
                for t in range(2):
                    for k in range(KT):
                        ins = mm(KV[:, S + t * P:S + (t + 1) * P], xs[:, k, t * P:(t + 1) * P],
                                 wat[:, k, (QG + 1) * P:], start=(k == 0), stop=(k == KT - 1))
                ins.then_inc(s["projected"], 1)
                for q in range(QG):
                    for k in range(KT):
                        ins = mm((QA, QB)[q // 2][:, (q % 2) * S:(q % 2 + 1) * S], wat[:, k, q * P:(q + 1) * P],
                                 c.xnT[:, k, toks], start=(k == 0), stop=(k == KT - 1))
                    if q % 2:
                        ins.then_inc(s["projected"], 1)

            def scores(j, h):
                pe.wait_ge(s["turned_qk"], 3 * j + 2 + h // 2)
                wait(pe, s["oT_copied"], 4 * j - 3 + h)
                mm(SH[h][:, 0:P], qk[:, h, 0:P], qk[:, QG, 0:P], start=True, stop=True)
                mm(SH[h][:, P:SC], qk[:, h, P:S], qk[:, QG, :], start=True, stop=True)\
                    .then_inc(s["scores_done"], 1)

            def turn(j, h):
                pe.wait_ge(s["scaled"], 8 * j + 2 * h + 2)
                for i in range(3):
                    ins = tr(SH[h][:, i * P:(i + 1) * P], pr[:, h, i * P:(i + 1) * P], c.ident[:, :])
                ins.then_inc(s["turned"], 1)

            def values(j, h):
                pe.wait_ge(s["pT_copied"], 4 * j + h + 1)
                pe.wait_ge(s["v_copied"], j + 1)
                mm(SH[h][:, 0:S], v[:, 0, :], pT[:, h, 0:S], start=True, stop=False, skip_group_check=True)
                mm(SH[h][:, P:S], v[:, 1, :], pT[:, h, S:SC], start=False, stop=True, skip_group_check=True)\
                    .then_inc(s["pv_done"], 1)

            def out(j, h):
                pe.wait_ge(s["oT_copied"], 4 * j + h + 1)
                if h == 0:
                    pe.wait_ge(s["wo_loaded"], 16 * (head(j) + 1))
                    wait(pe, s["y_added"], j)
                for t in range(2):
                    ins = mm(OUT[:, t * H:(t + 1) * H], oT[:, h, t * P:(t + 1) * P], wot[:, h, :],
                             start=(h == 0 and t == 0), stop=(h == QG - 1 and t == 1), skip_group_check=True)
                if h == QG - 1:
                    ins.then_inc(s["out_done"], 1)

            def step(j, last=False):
                for h in range(QG):
                    scores(j, h)
                if not last:
                    project(j + 1)
                turn(j, 0)
                turn(j, 1)
                values(j, 0)
                turn(j, 2)
                values(j, 1)
                out(j, 0)
                turn(j, 3)
                values(j, 2)
                out(j, 1)
                values(j, 3)
                out(j, 2)
                out(j, 3)

            project(0)
            step(0)
            with pe.Fori(1, ASTEPS - 1) as j:
                step(j)
            step(ASTEPS - 1, last=True)

        @block.gpsimd
        def _(pool):
            def turned(j):
                for i, (lo, n) in enumerate(((QG, 1), (0, 2), (2, 2))):
                    pool.wait_ge(s["multiplied"], 9 * j + 3 * i + 3)
                    if i == 0:
                        wait(pool, s["scores_done"], 4 * j)
                    nc.gpsimd.tensor_tensor(qk[:, lo:lo + n, :], mc[:, lo:lo + n, :], ms[:, lo:lo + n, :], ALU.add)\
                        .then_inc(s["turned_qk"], 1)

            turned(0)
            with pool.Fori(1, ASTEPS) as j:
                turned(j)

        @block.scalar
        def _(act):
            f = nc.scalar.activation

            def exponent(j, h):
                act.wait_ge(s["neg_done"], 4 * j + h + 1)
                wait(act, s["turned"], 4 * j - 3 + h)
                for t, (lo, hi) in enumerate(((0, P), (P, SC))):
                    f(pr[:, h, lo:hi], sc[:, h, lo:hi], ACT.Exp, bias=nm[:, h, t:t + 1],
                      accum_out=sm[:, h, t:t + 1]).then_inc(s["exp_done"], 1)

            def copy_turned(j, h):
                act.wait_ge(s["turned"], 4 * j + h + 1)
                wait(act, s["pv_done"], 4 * j - 3 + h)
                f(pT[:, h, :], SH[h][:, 0:SC], ACT.Copy).then_inc(s["pT_copied"], 1)

            def copy_output(j, h):
                act.wait_ge(s["pv_done"], 4 * j + h + 1)
                wait(act, s["out_done"], j)
                f(oT[:, h, :], SH[h][:, 0:S], ACT.Copy).then_inc(s["oT_copied"], 1)

            def copy_values(j):
                act.wait_ge(s["projected"], 3 * j + 1)
                act.wait_ge(s["multiplied"], 9 * j + 3)
                wait(act, s["pv_done"], 4 * j)
                f(v[:, :, :], KV[:, S:2 * S].rearrange("p (t d) -> p t d", t=2), ACT.Copy)\
                    .then_inc(s["v_copied"], 1)

            def step(j, last=False):
                for h in range(QG):
                    exponent(j, h)
                copy_turned(j, 0)
                copy_turned(j, 1)
                copy_output(j, 0)
                copy_turned(j, 2)
                copy_output(j, 1)
                copy_turned(j, 3)
                copy_output(j, 2)
                copy_output(j, 3)
                if not last:
                    copy_values(j + 1)

            copy_values(0)
            step(0)
            with act.Fori(1, ASTEPS - 1) as j:
                step(j)
            step(ASTEPS - 1, last=True)

        @block.vector
        def _(vec):
            stt, tt, ts = nc.vector.scalar_tensor_tensor, nc.vector.tensor_tensor, nc.vector.tensor_scalar

            def rotate(j):
                for i, (bank, lo, n, o) in enumerate(((KV, QG, 1, 2), (QA, 0, 2, 0), (QB, 2, 2, 0))):
                    vec.wait_ge(s["projected"], 3 * j + i + 1)
                    wait(vec, s["turned_qk"], 3 * j - 2 + i)
                    src = bank[:, 0:n * S].rearrange("p (n t) -> p n t", n=n)
                    tt(mc[:, lo:lo + n, :], src, tab[:, o:o + 1, :].to_broadcast([P, n, S]), ALU.mult)\
                        .then_inc(s["multiplied"], 1)
                    for a, b in ((0, 64), (64, 0)):
                        tt(ms[a:a + 64, lo:lo + n, :], src[b:b + 64], tab[b:b + 64, o + 1:o + 2, :]
                           .to_broadcast([64, n, S]), ALU.mult).then_inc(s["multiplied"], 1)

            def bias(j):
                for h in range(QG):
                    wait(vec, s["exp_done"], 8 * (j - 1) + 2 * h + 2)
                    n = QG * head(j) + h
                    stt(out=sc[:, h, :], in0=c.mt[:, bass.ds(seq(j), 1), :][:, 0, :], scalar=c.gh[:, bass.ds(n, 1)],
                        in1=c.nb[:, bass.ds(n, 1), :][:, 0, :], op0=ALU.mult, op1=ALU.add).then_inc(s["biased"], 1)

            def maxima(j, h):
                vec.wait_ge(s["scores_done"], 4 * j + h + 1)
                vec.wait_ge(s["biased"], 4 * j + h + 1)
                tt(sc[:, h, :], SH[h][:, 0:SC], sc[:, h, :], ALU.add).then_inc(s["added"], 1)
                vec.wait_ge(s["added"], 4 * j + h + 1)
                wait(vec, s["exp_done"], 8 * j)
                for t, (lo, hi) in enumerate(((0, P), (P, SC))):
                    nc.vector.tensor_reduce(mx[:, h, t:t + 1], sc[:, h, lo:hi], AX.X, ALU.max)\
                        .then_inc(s["max_done"], 1)
                vec.wait_ge(s["max_done"], 8 * j + 2 * h + 2)
                ts(nm[:, h, :], mx[:, h, :], -1.0, None, ALU.mult).then_inc(s["neg_done"], 1)

            def scale(j, h):
                vec.wait_ge(s["exp_done"], 8 * j + 2 * h + 2)
                wait(vec, s["scaled"], 8 * j)
                nc.vector.reciprocal(rc[:, h, :], sm[:, h, :]).then_inc(s["rc_done"], 1)
                vec.wait_ge(s["rc_done"], 4 * j + h + 1)
                for t, (lo, hi) in enumerate(((0, P), (P, SC))):
                    ts(pr[:, h, lo:hi], pr[:, h, lo:hi], rc[:, h, t:t + 1], None, ALU.mult).then_inc(s["scaled"], 1)

            def add_output(j):
                vec.wait_ge(s["out_done"], j + 1)
                wait(vec, s["y_added"], j)
                rows = c.y[:, bass.ds(2 * seq(j), 2), :]
                tt(rows, OUT[:, :].rearrange("p (t n) -> p t n", t=2), rows, ALU.add).then_inc(s["y_added"], 1)

            def step(j, last=False):
                for h in range(QG):
                    maxima(j, h)
                for h in range(QG):
                    scale(j, h)
                if not last:
                    rotate(j + 1)
                    bias(j + 1)
                add_output(j)

            nc.vector.memset(c.y[:, :, :], 0.0).then_inc(s["zeroed"], 1)
            vec.wait_ge(s["tab_loaded"], 16)
            rotate(0)
            bias(0)
            vec.wait_ge(s["zeroed"], 1)
            step(0)
            with vec.Fori(1, ASTEPS - 1) as j:
                step(j)
            step(ASTEPS - 1, last=True)

        inner.close()
        m.clear()


LUT, INNER = 16, 688
NI = (INNER + P - 1) // P
NCOL = KT * INNER * 2 + NI * H


def table_feed_forward(nc, c, lut, index):
    with ExitStack() as stack:
        m = Memory(nc, stack)
        table = m.sb("table", [P, LUT])
        ix = m.sb("ix", [P, NCOL], I32)
        ixf = m.sb("ixf", [P, NCOL])
        w = m.sb("w_table", [P, NCOL])
        hit = m.sb("hit", [P, 4, 536])
        NCHUNK = NCOL // 536
        gate = w[:, 0:KT * INNER].rearrange("p (k i) -> p k i", k=KT)
        up = w[:, KT * INNER:2 * KT * INNER].rearrange("p (k i) -> p k i", k=KT)
        down = w[:, 2 * KT * INNER:].rearrange("p (n h) -> p n h", n=NI)
        banks = [m.ps(f"tf{i}") for i in range(8)]
        ff = FeedForward(m, "tf_", c.xnT, gate, up, down, INNER, c.y, banks)
        loaded, converted, hits, summed = (m.sem("table_" + n) for n in "loaded converted hits summed".split())
        inner = stack.enter_context(ExitStack())
        block = inner.enter_context(nc.Block())

        @block.sync
        def _(sp):
            sp.dma_start(table[:, :], lut[None, :].to_broadcast([P, LUT])).then_inc(loaded, 16)
            sp.dma_start(ix[:, :], index).then_inc(loaded, 16)

        @block.vector
        def _(vec):
            vec.wait_ge(loaded, 32)
            nc.vector.tensor_copy(ixf[:, :], ix[:, :]).then_inc(converted, 1)
            vec.wait_ge(converted, 1)
            n = 0
            for i in range(NCHUNK):
                cols = slice(i * 536, (i + 1) * 536)
                for k in range(LUT):
                    wait(vec, summed, n - 3)
                    out = w[:, cols] if k == 0 else hit[:, n % 4, :]
                    nc.vector.tensor_scalar(out, ixf[:, cols], float(k), table[:, k:k + 1],
                                            ALU.is_equal, ALU.mult).then_inc(hits, 1)
                    n += 1
            vec.wait_ge(summed, n)
            for ch in range(NCH):
                ff.vector(nc, vec, ch)

        @block.gpsimd
        def _(pool):
            n = 0
            for i in range(NCHUNK):
                cols = slice(i * 536, (i + 1) * 536)
                for k in range(LUT):
                    pool.wait_ge(hits, n + 1)
                    wait(pool, summed, n)
                    if k == 0:
                        nc.gpsimd.nop().then_inc(summed, 1)
                    else:
                        nc.gpsimd.tensor_tensor(w[:, cols], w[:, cols], hit[:, n % 4, :], ALU.add).then_inc(summed, 1)
                    n += 1

        @block.tensor
        def _(pe):
            pe.wait_ge(summed, LUT * NCHUNK)
            for ch in range(NCH):
                ff.tensor(nc, pe, ch)

        @block.scalar
        def _(act):
            for ch in range(NCH):
                ff.scalar(nc, act, ch)

        inner.close()
        m.clear()


def build(nc, stack, a, out=None, layers=("delta", "experts", "softmax", "ffn"), steps=STEPS):
    m = Memory(nc, stack)

    class c:
        pass

    c.ident = m.sb("ident", [P, P])
    c.ones = m.sb("ones", [P, P])
    c.tri = m.sb("tri", [P, P])
    c.tri_strict = m.sb("tri_strict", [P, P])
    c.cut = m.sb("cut", [P, S])
    c.x = m.sb("x_rows", [P, NT, H])
    c.xn = m.sb("xn_rows", [P, NT, H])
    c.xnT = m.sb("xnT", [P, KT, TOK])
    c.y = m.sb("y_rows", [P, NT, H])
    tokens = a["x"].rearrange("(n p) h -> p n h", p=P)
    g_dram = nc.dram_tensor("decay_rows", (HV, TOK), F32).ap()
    slots_dram = nc.dram_tensor("slot_rows", (E * CAP, H), F32).ap()
    outs_dram = nc.dram_tensor("expert_outs", (E * CAP + 1, H), F32).ap()
    first = True
    with ExitStack() as layer:
        ml = Memory(nc, layer)
        c.level = ml.sb("level", [P, LEVELS + 1, P])
        make_constants(nc, c)
        if "delta" in layers:
            normalise(nc, c, "n0_", tokens, first=True)
            c.G = ml.sb("G", [P, NT, HV])
            c.beta = ml.sb("beta", [P, NT, HV])
            delta_gates(nc, c, a["w_ab"], a["a_log"], a["dt_bias"], g_dram)
            delta_rule(nc, c, a["w_qkv"], a["w_z"], a["conv_w"], a["w_out"], a["norm_w"], g_dram, steps)
            first = False
    if "experts" in layers:
        normalise(nc, c, "n1_", tokens if first else c.y, first=first)
        experts(nc, c, *(a[n] for n in "gate_w w_gate w_up w_down sw_gate sw_up sw_down".split()),
                slots_dram, outs_dram)
        first = False
    if "softmax" in layers:
        normalise(nc, c, "n2_", tokens if first else c.y, first=first)
        with ExitStack() as layer:
            ml = Memory(nc, layer)
            c.mt = ml.sb("mt", [P, B, SC])
            c.nb = ml.sb("nb", [P, HQ, SC])
            c.gh = ml.sb("gh", [P, HQ])
            attention_bias(nc, c, a["pol_WA"], a["pol_WB"], a["pol_dir"], a["pol_gate"], a["gtp_gamma"])
            softmax_attention(nc, c, a["w_att"], a["wo_att"], a["rope"])
        first = False
    if "ffn" in layers:
        normalise(nc, c, "n3_", tokens if first else c.y, first=first)
        table_feed_forward(nc, c, a["lut"], a["index"])
    if out is not None:
        normalise(nc, c, "n4_", c.y, last=out.rearrange("(n p) h -> p n h", p=P))
    return c


def kernel(**inputs):
    import concourse.bacc as bacc
    from concourse.bass_utils import run_bass_kernel_spmd

    def get(name):
        return np.asarray(inputs[name])

    HKVD, OUTER = HKV * DH, QG * DH
    a = {"x": get("L0_attn_hidden_states").reshape(TOK, H)}
    w = get("L0_attn_W_qkv")
    nk = HK * DK
    blocks = [w[nk:2 * nk].reshape(HK, 1, DK, KT, P), w[:nk].reshape(HK, 1, DK, KT, P),
              w[2 * nk:].reshape(HK, 2, DK, KT, P)]
    a["w_qkv"] = np.concatenate(blocks, 1).transpose(0, 4, 3, 1, 2)
    w = get("L0_attn_conv_w")
    blocks = [w[nk:2 * nk].reshape(HK, 1, DK, TAPS), w[:nk].reshape(HK, 1, DK, TAPS),
              w[2 * nk:].reshape(HK, 2, DK, TAPS)]
    a["conv_w"] = np.concatenate(blocks, 1).transpose(2, 0, 1, 3)
    a["w_z"] = get("L0_attn_W_z").reshape(HK, 2 * DK, KT, P).transpose(0, 3, 2, 1)
    w = np.concatenate([get("L0_attn_W_a"), get("L0_attn_W_b")], 0)
    a["w_ab"] = w.reshape(2 * HV, KT, P).transpose(2, 1, 0)
    a["w_out"] = get("L0_attn_W_out").reshape(H, HK, 2, DK).transpose(1, 3, 2, 0)
    a["a_log"], a["dt_bias"] = get("L0_attn_A_log"), get("L0_attn_dt_bias")
    a["norm_w"] = get("L0_attn_norm_w").reshape(DK, 1)
    a["gate_w"] = get("L0_ffn_gate_w").reshape(E, KT, P).transpose(2, 1, 0)
    for n in "w_gate w_up w_down sw_gate sw_up sw_down".split():
        a[n] = get("L0_ffn_" + n)
    q = get("L1_attn_Wq").reshape(KT, P, HKV, OUTER)
    k, v = (get("L1_attn_" + n).reshape(KT, P, HKV, DH) for n in ("Wk", "Wv"))
    a["w_att"] = np.concatenate([q, k, v], 3).transpose(2, 1, 0, 3)
    a["wo_att"] = get("L1_attn_Wo").reshape(HKV, QG, DH, H).transpose(0, 2, 1, 3)
    for n in "pol_dir pol_WA pol_WB pol_gate gtp_gamma".split():
        a[n] = get("L1_attn_" + n)
    freq = np.float32(1) / np.float32(10000.0) ** (np.arange(0, DH, 2, dtype=np.float32) / np.float32(DH))
    ang = (np.arange(S, dtype=np.float32)[None, :] * freq[:, None]).astype(np.float64)
    cos, sin = np.concatenate([np.cos(ang)] * 2), np.concatenate([np.sin(ang), -np.sin(ang)])
    a["rope"] = np.stack([cos * DH ** -0.5, sin * DH ** -0.5, cos, sin], 1).astype(np.float32)
    a["lut"] = get("L1_ffn_lut")
    ix = [get("L1_ffn_" + n).T.reshape(KT, P, INNER).transpose(1, 0, 2).reshape(P, KT * INNER)
          for n in ("gate_idx", "up_idx")]
    down = get("L1_ffn_down_idx").T
    down = np.concatenate([down, np.zeros((NI * P - INNER, H), down.dtype)])
    a["index"] = np.concatenate(ix + [down.reshape(NI, P, H).transpose(1, 0, 2).reshape(P, NI * H)], 1)

    nc = bacc.Bacc("TRN2", target_bir_lowering=False, num_devices=1)
    arrays = {"in_" + n: np.ascontiguousarray(v) for n, v in a.items()}
    aps = {n: nc.dram_tensor("in_" + n, arrays["in_" + n].shape, mybir.dt.from_np(arrays["in_" + n].dtype),
                             kind="ExternalInput").ap() for n in a}
    out = nc.dram_tensor("out", (TOK, H), F32, kind="ExternalOutput").ap()
    with ExitStack() as stack:
        build(nc, stack, aps, out)
    r = run_bass_kernel_spmd(nc, [arrays], core_ids=[0])
    return r.results[0]["out"].reshape(B, S, H)
```

```python
from contextlib import ExitStack

import numpy as np

import concourse.bass as bass
from concourse import mybir

ALU = mybir.AluOpType
ACT = mybir.ActivationFunctionType
AX = mybir.AxisListType
F32 = mybir.dt.float32
I32 = mybir.dt.int32
U32 = mybir.dt.uint32

P = 128
B, S, H = 8, 256, 256
TOK = B * S
NT = TOK // P
KT = H // P
LN_EPS = 1e-5

HV, HK, DK = 32, 16, 128
TAPS = 4
NF = 4
LEVELS = 4
DELTA_EPS = 1e-6

LUT, INNER = 16, 688
NI = (INNER + P - 1) // P
NCOL = KT * INNER * 2 + NI * H

STEPS = HK * B
LOOKED_UP = NCOL * LUT // STEPS


def wait(eng, sem, value):
    if isinstance(value, int) and value <= 0:
        return
    eng.wait_ge(sem, value)


class Memory:

    def __init__(self, nc, stack):
        self.nc, self.stack, self.sems = nc, stack, []

    def sb(self, name, shape, dt=F32):
        return self.stack.enter_context(self.nc.sbuf_tensor(name, shape, dt))

    def ps(self, name, shape=(P, 512), dt=F32):
        return self.stack.enter_context(self.nc.psum_tensor(name, list(shape), dt))

    def sem(self, name):
        handle = self.stack.enter_context(self.nc.semaphore(name))
        self.sems.append(handle)
        return handle

    def clear(self):
        with self.nc.Block() as block:

            @block.gpsimd
            def _(pool):
                for handle in self.sems:
                    pool.sem_clear(handle)


def make_constants(nc, c, tokens):
    with ExitStack() as stack:
        m = Memory(nc, stack)
        step, loaded = m.sem("const_step"), m.sem("x_loaded")
        inner = stack.enter_context(ExitStack())
        block = inner.enter_context(nc.Block())

        @block.sync
        def _(sp):
            sp.dma_start(c.x[:, :, :], tokens).then_inc(loaded, 16)
            sp.wait_ge(loaded, 16)

        @block.gpsimd
        def _(pool):
            n = 0

            def done(ins):
                nonlocal n
                n += 1
                ins.then_inc(step, 1)
                pool.wait_ge(step, n)

            def select(ap, op, base, pattern, mult, fill):
                done(nc.gpsimd.affine_select(out=ap, in_=ap, compare_op=op, fill=fill, base=base,
                                             pattern=pattern, channel_multiplier=mult))

            done(nc.gpsimd.memset(c.ones[:, :], 1.0))
            done(nc.gpsimd.memset(c.ident[:, :], 0.0))
            select(c.ident[:, :], ALU.not_equal, 0, [[-1, P]], 1, 1.0)
            done(nc.gpsimd.memset(c.tri[:, :], 1.0))
            select(c.tri[:, :], ALU.is_ge, 0, [[1, P]], -1, 0.0)
            done(nc.gpsimd.memset(c.tri_strict[:, :], 1.0))
            select(c.tri_strict[:, :], ALU.is_gt, 0, [[1, P]], -1, 0.0)
            done(nc.gpsimd.memset(c.cut[:, :], 0.0))
            select(c.cut[:, 0:P], ALU.is_ge, 0, [[1, P]], -1, -1e30)
            for l in range(LEVELS + 1):
                b = 1 << l
                val = -1.0 if l == 0 else 1.0
                v = c.level[:, l, :].rearrange("p (n two i) -> p n two i", two=2, i=b)
                done(nc.gpsimd.memset(c.level[:, l, :], val))
                done(nc.gpsimd.memset(v[:, :, 0, :], 0.0))
                odd = v[:, :, 1, :]
                select(odd, ALU.is_ge, 0, [[-2 * b, P // (2 * b)], [0, b]], 1, 0.0)
                select(odd, ALU.is_gt, b, [[2 * b, P // (2 * b)], [0, b]], -1, 0.0)

        inner.close()
        m.clear()


def normalise(nc, c, tag, src, first=False, last=None):
    with ExitStack() as stack:
        m = Memory(nc, stack)
        stats = m.sb(tag + "stats", [P, NT, 6])
        mv_y = m.sb(tag + "mv_y", [P, NT, 2])
        mv_x = m.sb(tag + "mv_x", [P, NT, 2])
        var_y = m.sb(tag + "var_y", [P, NT])
        var_x = m.sb(tag + "var_x", [P, NT])
        power = m.sb(tag + "power", [P, NT])
        rstd_y = m.sb(tag + "rstd_y", [P, NT])
        rstd_x = m.sb(tag + "rstd_x", [P, NT])
        xn = c.xn
        pt = [m.ps(f"{tag}pt{i}") for i in range(4)]
        dve, var_ready, rstd_ready, xn_ready, turned, copied, stored, power_ready = (
            m.sem(tag + n) for n in ("dve", "var_ready", "rstd_ready", "xn_ready", "turned",
                                     "copied", "stored", "power_ready"))
        inner = stack.enter_context(ExitStack())
        block = inner.enter_context(nc.Block())

        @block.sync
        def _(sp):
            if last is not None:
                for q in range(4):
                    sp.wait_ge(xn_ready, 4 * q + 4)
                    sp.dma_start(last[:, 4 * q:4 * q + 4, :], c.x[:, 4 * q:4 * q + 4, :]).then_inc(stored, 16)
                sp.wait_ge(stored, 64)

        @block.gpsimd
        def _(pool):
            nc.gpsimd.memset(power[:, :], -0.5).then_inc(power_ready, 1)
            pool.wait_ge(power_ready, 1)
            pairs = ([] if first else [(rstd_y, var_y)]) + ([] if last is not None else [(rstd_x, var_x)])
            for i, (out, var) in enumerate(pairs):
                pool.wait_ge(var_ready, i + 1)
                nc.gpsimd.tensor_tensor(out[:, :], var[:, :], power[:, :], ALU.pow).then_inc(rstd_ready, 1)

        @block.vector
        def _(vec):
            n = 0

            def chain(ins):
                nonlocal n
                n += 1
                ins.then_inc(dve, 1)

            def statistics(of, mv, var):
                for t in range(NT):
                    chain(nc.vector.bn_stats(stats[:, t, :], of[:, t, :]))
                vec.wait_ge(dve, n)
                for t in range(NT):
                    chain(nc.vector.bn_aggr(mv[:, t, :], stats[:, t, :]))
                vec.wait_ge(dve, n)
                nc.vector.tensor_scalar(var[:, :], mv[:, :, 1], LN_EPS, None, ALU.add).then_inc(var_ready, 1)

            if not first:
                statistics(src, mv_y, var_y)
                vec.wait_ge(rstd_ready, 1)
                for t in range(NT):
                    chain(nc.vector.tensor_scalar(src[:, t, :], src[:, t, :], mv_y[:, t, 0:1], rstd_y[:, t:t + 1],
                                                  ALU.subtract, ALU.mult))
                    vec.wait_ge(dve, n)
                    ins = nc.vector.tensor_tensor(c.x[:, t, :], c.x[:, t, :], src[:, t, :], ALU.add)
                    if last is not None:
                        ins.then_inc(xn_ready, 1)
                    else:
                        chain(ins)
                vec.wait_ge(dve, n)
            if last is None:
                statistics(c.x, mv_x, var_x)
                vec.wait_ge(rstd_ready, 1 if first else 2)
                for t in range(NT):
                    nc.vector.tensor_scalar(xn[:, t, :], c.x[:, t, :], mv_x[:, t, 0:1], rstd_x[:, t:t + 1],
                                            ALU.subtract, ALU.mult).then_inc(xn_ready, 1)

        if last is None:
            @block.tensor
            def _(pe):
                for u in range(NT // 2):
                    if u >= 4:
                        pe.wait_ge(copied, u - 3)
                    pe.wait_ge(xn_ready, 2 * u + 2)
                    for k in range(KT):
                        for i in range(2):
                            ins = nc.tensor.transpose(pt[u % 4][:, (2 * k + i) * P:(2 * k + i + 1) * P],
                                                      xn[:, 2 * u + i, k * P:(k + 1) * P], c.ident[:, :])
                    ins.then_inc(turned, 1)

            @block.scalar
            def _(act):
                for u in range(NT // 2):
                    act.wait_ge(turned, u + 1)
                    nc.scalar.activation(c.xnT[:, :, u * S:(u + 1) * S],
                                         pt[u % 4][:, :].rearrange("p (k t) -> p k t", k=KT),
                                         ACT.Copy).then_inc(copied, 1)

        inner.close()
        m.clear()


def delta_gates(nc, c, w_ab, a_log, dt_bias, g_dram):
    with ExitStack() as stack:
        m = Memory(nc, stack)
        wab = m.sb("wab", [P, KT, 2 * HV])
        dtb = m.sb("dtb", [P, HV])
        alog = m.sb("alog", [P, HV])
        ea = m.sb("ea", [P, HV])
        u = m.sb("g_u", [P, NT, HV])
        mn = m.sb("g_mn", [P, NT, HV])
        ex = m.sb("g_ex", [P, NT, HV])
        ln = m.sb("g_ln", [P, NT, HV])
        sp_ = m.sb("g_sp", [P, NT, HV])
        g = m.sb("g_g", [P, NT, HV])
        th = m.sb("g_th", [P, NT, HV])
        gT = m.sb("g_gT", [HV, TOK])
        pab = [m.ps(f"pab{i}", (P, NT // 2, 2 * HV)) for i in range(2)]
        pg = m.ps("pg", (P, NT, HV))
        pgT = [m.ps(f"pgT{i}", (HV, 512)) for i in range(4)]
        loaded, projected, dve, act_done, g_ready, summed, G_ready, turned, gT_ready, stored = (
            m.sem("gates_" + n) for n in ("loaded", "projected", "dve", "act_done", "g_ready", "summed",
                                          "G_ready", "turned", "gT_ready", "stored"))
        inner = stack.enter_context(ExitStack())
        block = inner.enter_context(nc.Block())

        @block.sync
        def _(sp):
            sp.dma_start(wab[:, :, :], w_ab).then_inc(loaded, 16)
            sp.dma_start(dtb[:, :], dt_bias[None, :].to_broadcast([P, HV])).then_inc(loaded, 16)
            sp.dma_start(alog[:, :], a_log[None, :].to_broadcast([P, HV])).then_inc(loaded, 16)
            sp.wait_ge(gT_ready, 4)
            sp.dma_start(g_dram, gT[:, :]).then_inc(stored, 16)
            sp.wait_ge(stored, 16)

        @block.tensor
        def _(pe):
            pe.wait_ge(loaded, 48)
            for t in range(NT):
                for k in range(KT):
                    ins = nc.tensor.matmul(pab[t // 8][:, t % 8, :], c.xnT[:, k, t * P:(t + 1) * P], wab[:, k, :],
                                           start=(k == 0), stop=(k == KT - 1))
                if t % 8 == 7:
                    ins.then_inc(projected, 1)
            pe.wait_ge(g_ready, 1)
            nc.tensor.matmul(pg[:, :, :], c.tri[:, :], g[:, :, :], start=True, stop=False, skip_group_check=True)
            pairs = g[:, :, :].rearrange("p (b c) h -> p b c h", c=2)
            out = pg[:, :, :].rearrange("p (b c) h -> p b c h", c=2)
            nc.tensor.matmul(out[:, :, 1, :], c.ones[:, :], pairs[:, :, 0, :], start=False, stop=True,
                             skip_group_check=True).then_inc(summed, 1)
            pe.wait_ge(G_ready, 1)
            for t in range(NT):
                ins = nc.tensor.transpose(pgT[t // 4][:, (t % 4) * P:(t % 4 + 1) * P], c.G[:, t, :], c.ident[:, :])
                if t % 4 == 3:
                    ins.then_inc(turned, 1)

        @block.vector
        def _(vec):
            n = 0

            def done(ins):
                nonlocal n
                n += 1
                ins.then_inc(dve, 1)
                vec.wait_ge(dve, n)

            vec.wait_ge(loaded, 48)
            for i in range(2):
                vec.wait_ge(projected, i + 1)
                half = slice(8 * i, 8 * i + 8)
                done(nc.vector.tensor_tensor(u[:, half, :], pab[i][:, :, 0:HV],
                                             dtb[:, None, :].to_broadcast([P, 8, HV]), ALU.add))
                done(nc.vector.tensor_copy(c.beta[:, half, :], pab[i][:, :, HV:2 * HV]))
            done(nc.vector.scalar_tensor_tensor(out=mn[:, :, :], in0=u[:, :, :], scalar=-1.0, in1=u[:, :, :],
                                                op0=ALU.mult, op1=ALU.min))
            vec.wait_ge(act_done, 4)
            done(nc.vector.scalar_tensor_tensor(out=sp_[:, :, :], in0=u[:, :, :], scalar=0.0, in1=ln[:, :, :],
                                                op0=ALU.max, op1=ALU.add))
            nc.vector.scalar_tensor_tensor(out=g[:, :, :], in0=sp_[:, :, :], scalar=-1.0,
                                           in1=ea[:, None, :].to_broadcast([P, NT, HV]),
                                           op0=ALU.mult, op1=ALU.mult).then_inc(g_ready, 1)
            done(nc.vector.tensor_scalar(c.beta[:, :, :], th[:, :, :], 0.5, 0.5, ALU.mult, ALU.add))
            vec.wait_ge(summed, 1)
            nc.vector.tensor_copy(c.G[:, :, :], pg[:, :, :]).then_inc(G_ready, 1)
            for i in range(4):
                vec.wait_ge(turned, i + 1)
                nc.vector.tensor_copy(gT[:, 512 * i:512 * i + 512], pgT[i][:, :]).then_inc(gT_ready, 1)

        @block.scalar
        def _(act):
            act.wait_ge(loaded, 48)
            nc.scalar.activation(ea[:, :], alog[:, :], ACT.Exp).then_inc(act_done, 1)
            act.wait_ge(dve, 5)
            nc.scalar.activation(ex[:, :, :], mn[:, :, :], ACT.Exp).then_inc(act_done, 1)
            act.wait_ge(act_done, 2)
            nc.scalar.activation(ln[:, :, :], ex[:, :, :], ACT.Ln, bias=c.ones[:, 0:1]).then_inc(act_done, 1)
            nc.scalar.activation(th[:, :, :], c.beta[:, :, :], ACT.Tanh, scale=0.5).then_inc(act_done, 1)

        inner.close()
        m.clear()


def delta_rule(nc, c, w_qkv, w_z, conv_w, w_out, norm_w, lut, index, g_dram):
    CM = LEVELS + 1
    EPS_Q = DELTA_EPS * 4.0 * DK
    with ExitStack() as stack:
        m = Memory(nc, stack)
        wp = m.sb("wp", [P, KT, NF, P])
        wz = m.sb("wz", [P, KT, 2 * P])
        cw = m.sb("cw", [P, HK, NF, TAPS])
        wo = m.sb("wo", [P, 2, H])
        nw = m.sb("nw", [P, 1])
        xb = m.sb("xb", [P, KT, S])
        grow = m.sb("grow", [P, 2, S])
        gcol = m.sb("gcol", [P, 2, 2])
        bcol = m.sb("bcol", [P, 2, 2])
        table = m.sb("table", [P, LUT])
        entry = m.sb("entry", [P, LUT])
        ix = m.sb("ix", [P, NCOL], I32)
        hit = m.sb("hit", [P, LOOKED_UP])
        osum = m.sb("osum", [P, 2, H])
        cv = m.sb("cv", [P, NF, S])
        th = m.sb("th", [P, NF, S])
        s2 = m.sb("s2", [P, NF, S])
        sq = m.sb("sq", [P, 2, S])
        thz = m.sb("thz", [P, 2, 2 * P])
        zs = m.sb("zs", [P, 2, 2 * P])
        ns = m.sb("ns", [P, 4])
        nq = [m.sb(f"nq_{u}", [P, 2]) for u in range(2)]
        rk = m.sb("rk", [P, 2])
        sc = m.sb("sc", [P, 2, 2])
        kn = m.sb("kn", [P, 2])
        half = m.sb("half", [P, 4])
        mhalf = m.sb("mhalf", [P, 4])
        arg = m.sb("arg", [P, 2, 3 * P])
        dec = m.sb("dec", [P, 2, 3 * P])
        up = [m.sb(f"up_{u}", [P, 8, 2, P]) for u in range(2)]
        dg = [x[:, 0:2, :, :].rearrange("p n h t -> p (n h) t") for x in up]
        cm = m.sb("cm", [P, LEVELS, 4, P])
        RT = [m.sb(f"RT_{u}", [P, 2, 4, P]) for u in range(2)]
        R, T = [x[:, 0] for x in RT], [x[:, 1] for x in RT]
        seed = m.sb("seed", [P, 4, P])
        cwj = m.sb("cwj", [P, NF, TAPS])
        W = m.sb("W", [P, 4, P])
        x32 = m.sb("x32", [P, 4, 32])
        s64 = m.sb("s64", [P, 4, 64])
        V = [m.sb(f"V_{u}", [P, 2, 2, P]) for u in range(2)]
        Z0 = m.sb("Z0", [P, 2, P])
        V1 = m.sb("V1", [P, 2, P])
        Z1 = m.sb("Z1", [P, 2, P])
        osq = m.sb("osq", [P, 4, P])
        oss = m.sb("oss", [P, 4])
        orr = m.sb("orr", [P, 4])
        rs = m.sb("rs", [P, 4])
        osc = m.sb("osc", [P, 4, P])
        og = m.sb("og", [P, 4, P])
        ogT = m.sb("ogT", [P, 4, P])
        X0, X1, X2, X3 = (m.ps(f"dx{i}") for i in range(4))
        LV = [m.ps("dLVA"), m.ps("dLVB")]
        TL = [m.ps("dTLA"), m.ps("dTLB")]

        names = ("w_loaded wz_loaded wo_loaded misc_loaded xb_loaded grow_loaded "
                 "qkv_done z_done ssum_done vt_done gram_done s1_done tr_done s64_done r64_done "
                 "z0_done a21_done z1_done o_done ogT_done out_done "
                 "tap_done conv_done thqk_done thv_done silu_done thv_used siluv_done sq_done thz_done "
                 "zs_done ns_done rk_done x32_done x32_copied t32_done t32_copied r32_done sc_done kn_done "
                 "cols_done arg_done dec_done up_done r1_done t1_done r_done cm_done "
                 "w_done tr_copied s64_copied r64_copied V_done z0_copied v1_done z1_copied oss_done "
                 "orr_done rs_done og_done ogT_copied acc_done halves tmp_done nq_done zeroed powers "
                 "out_copied osc_done index_loaded entries hit_done looked_up").split()
        s = {n: m.sem("d_" + n) for n in names}
        inner = stack.enter_context(ExitStack())
        block = inner.enter_context(nc.Block())

        def head(j):
            return j // B

        def seq(j):
            return j % B

        def parts(j):
            if not isinstance(j, int):
                return True, True, True, True
            return j + 1 < STEPS, j < STEPS, 0 <= j - 1 < STEPS, j >= 2

        @block.sync
        def _(sp):
            sp.dma_start(cw[:, :, :, :], conv_w).then_inc(s["misc_loaded"], 16)
            sp.dma_start(nw[:, :], norm_w).then_inc(s["misc_loaded"], 16)
            sp.dma_start(table[:, :], lut[None, :].to_broadcast([P, LUT])).then_inc(s["index_loaded"], 16)
            sp.dma_start(ix[:, :], index).then_inc(s["index_loaded"], 16)

            def fixed(value):
                return value if isinstance(value, int) else sp.snap(value)

            def load_decays(j):
                h0, t0 = fixed(2 * head(j)), fixed(seq(j) * S)
                wait(sp, s["arg_done"], 2 * j)
                sp.dma_start(grow[:, :, :], g_dram[None, bass.ds(h0, 2), bass.ds(t0, S)]
                             .to_broadcast([P, 2, S])).then_inc(s["grow_loaded"], 16)

            def load_head(g):
                wait(sp, s["qkv_done"], 2 * B * g)
                sp.dma_start(wp[:, :, :, :], w_qkv[g]).then_inc(s["w_loaded"], 16)

            def load_steps(g):
                load_decays(g * B)
                load_decays(g * B + 1)
                wait(sp, s["z_done"], B * g)
                sp.dma_start(wz[:, :, :], w_z[g]).then_inc(s["wz_loaded"], 16)
                load_decays(g * B + 2)
                wait(sp, s["out_done"], B * g)
                sp.dma_start(wo[:, :, :], w_out[g]).then_inc(s["wo_loaded"], 16)
                with sp.Fori(3, B) as b:
                    load_decays(g * B + b)

            load_head(0)
            load_steps(0)
            with sp.Fori(1, STEPS // B) as g:
                load_head(g)
                load_steps(g)

        @block.tensor
        def _(pe):
            mm, tr = nc.tensor.matmul, nc.tensor.transpose

            def project(j):
                pe.wait_ge(s["w_loaded"], 16 * (head(j) + 1))
                for bank, f0 in ((X0, 0), (X1, 2)):
                    if f0 == 0:
                        wait(pe, s["ns_done"], j)
                    else:
                        wait(pe, s["V_done"], 2 * j)
                    for f in (f0, f0 + 1):
                        for k in range(KT):
                            ins = mm(bank[:, (f - f0) * S:(f - f0 + 1) * S], wp[:, k, f, :],
                                     c.xnT[:, k, bass.ds(seq(j) * S, S)], start=(k == 0), stop=(k == KT - 1))
                    ins.then_inc(s["qkv_done"], 1)

            def project_z(j, n):
                t, k = n // KT, n % KT
                if n == 0:
                    pe.wait_ge(s["wz_loaded"], 16 * (head(j) + 1))
                    pe.wait_ge(s["xb_loaded"], 16 * (j + 1))
                    wait(pe, s["zs_done"], j)
                ins = mm(X2[:, t * S:(t + 1) * S], xb[:, k, t * P:(t + 1) * P], wz[:, k, :],
                         start=(k == 0), stop=(k == KT - 1))
                if n == 3:
                    ins.then_inc(s["z_done"], 1)

            def square_sums(j):
                pe.wait_ge(s["sq_done"], j + 1)
                pe.wait_ge(s["conv_done"], 12 * j + 6)
                for i in range(2):
                    for t in range(2):
                        ins = mm(X0[:, 2 * i + t:2 * i + t + 1], sq[:, i, t * P:(t + 1) * P], c.ones[:, 0:1],
                                 start=True, stop=True)
                ins.then_inc(s["ssum_done"], 1)

            def turn_v(j):
                pe.wait_ge(s["siluv_done"], j + 1)
                for t in range(2):
                    for h in range(2):
                        ins = tr(X1[:, (2 * t + h) * P:(2 * t + h + 1) * P], s2[:, 2 + h, t * P:(t + 1) * P],
                                 c.ident[:, :])
                ins.then_inc(s["vt_done"], 1)

            def gram0(j):
                wait(pe, s["v1_done"], j - 1)
                mm(TL[1][:, :], s2[:, 0, 0:P], s2[:, 0:2, :], start=True, stop=True).then_inc(s["gram_done"], 1)

            def gram1(j):
                wait(pe, s["z1_copied"], j - 1)
                mm(TL[0][:, 0:S], s2[:, 0, P:S], s2[:, 0:2, P:S], start=True, stop=True).then_inc(s["gram_done"], 1)

            def turn_output(j):
                pe.wait_ge(s["og_done"], j + 1)
                for i in range(4):
                    ins = tr(X3[:, i * P:(i + 1) * P], og[:, i, :], c.ident[:, :])
                ins.then_inc(s["ogT_done"], 1)

            def project_out(j, n):
                t, h = n // 2, n % 2
                if n == 0:
                    pe.wait_ge(s["wo_loaded"], 16 * (head(j) + 1))
                    pe.wait_ge(s["ogT_copied"], j + 1)
                ins = mm(X3[:, t * S:(t + 1) * S], ogT[:, 2 * t + h, :], wo[:, h, :],
                         start=(h == 0), stop=(h == 1))
                if n == 3:
                    ins.then_inc(s["out_done"], 1)

            def join(j, u, l, a):
                pe.wait_ge(s["cm_done"], CM * j + (a + 1 if l == 0 else l + 2))
                if l == 0:
                    pe.wait_ge(s["t1_done"], 2 * j + a + 1)
                    wait(pe, s["x32_copied"], 2 * j)
                    wait(pe, s["r32_done"], 2 * j)
                else:
                    pe.wait_ge(s["tr_copied"], 2 * (LEVELS * j + l - 1) + a + 1)
                for i in (2 * a, 2 * a + 1):
                    ins = mm(LV[a][:, (i % 2) * P:(i % 2 + 1) * P], cm[:, l, i, :], T[u][:, i, :],
                             start=True, stop=True)
                ins.then_inc(s["s1_done"], 1)

            def grow_inverse(j, u, l, a):
                pe.wait_ge(s["w_done"], 2 * (LEVELS * j + l) + a + 1)
                if l:
                    pe.wait_ge(s["r_done"], 2 * (LEVELS * j + l - 1) + a + 1)
                for i in (2 * a, 2 * a + 1):
                    o = (i % 2) * P
                    ins = mm(LV[a][:, 2 * P + o:3 * P + o], R[u][:, i, :], W[:, i, :], start=True, stop=True)
                ins.then_inc(s["tr_done"], 1)

            def join32(j, u, a):
                pe.wait_ge(s["tr_copied"], 2 * LEVELS * j + 2 * (LEVELS - 1) + a + 1)
                for i in (2 * a, 2 * a + 1):
                    for r in (0, 64):
                        ins = mm(LV[a][r + 32:r + 64, (i % 2) * 32:(i % 2 + 1) * 32], dg[u][:, i, r + 32:r + 64],
                                 T[u][:, i, r:r + 32], start=True, stop=True)
                ins.then_inc(s["x32_done"], 1)

            def corner32(j, u, a):
                pe.wait_ge(s["x32_copied"], 2 * j + a + 1)
                pe.wait_ge(s["r_done"], 2 * LEVELS * j + 2 * (LEVELS - 1) + a + 1)
                for i in (2 * a, 2 * a + 1):
                    for r in (0, 64):
                        ins = mm(LV[0][r + 32:r + 64, S + i * 32:S + (i + 1) * 32], R[u][:, i, r + 32:r + 64],
                                 x32[:, i, :], start=True, stop=True)
                ins.then_inc(s["t32_done"], 1)

            def join64(j, u, front):
                pe.wait_ge(s["t32_copied"], j + 1)
                if front:
                    pe.wait_ge(s["up_done"], 8 * (j + 2))
                for i in range(4):
                    ins = mm(TL[0][64:P, i * 64:(i + 1) * 64], dg[u][:, i, 64:P], T[u][:, i, 0:64],
                             start=True, stop=True)
                ins.then_inc(s["s64_done"], 1)

            def corner64(j, u):
                pe.wait_ge(s["s64_copied"], j + 1)
                pe.wait_ge(s["r32_done"], 2 * (j + 1))
                for i in range(4):
                    ins = mm(TL[1][0:64, i * 64:(i + 1) * 64], s64[:, i, :], R[u][:, i, 64:P],
                             start=True, stop=True)
                ins.then_inc(s["r64_done"], 1)

            def solve0(j, u):
                pe.wait_ge(s["r64_copied"], j + 1)
                for h in range(2):
                    ins = mm(TL[0][:, h * P:(h + 1) * P], R[u][:, h, :], V[u][:, 0, h, :], start=True, stop=True)
                ins.then_inc(s["z0_done"], 1)

            def carry(j, u):
                pe.wait_ge(s["z0_copied"], j + 1)
                for h in range(2):
                    ins = mm(TL[1][:, h * P:(h + 1) * P], up[u][:, 2, h, :], Z0[:, h, :], start=True, stop=True)
                ins.then_inc(s["a21_done"], 1)

            def solve1(j, u):
                pe.wait_ge(s["v1_done"], j + 1)
                for h in range(2):
                    ins = mm(TL[0][:, h * P:(h + 1) * P], R[u][:, 2 + h, :], V1[:, h, :], start=True, stop=True)
                ins.then_inc(s["z1_done"], 1)

            def output_of_0(j, u):
                wait(pe, s["out_copied"], j)
                for t in range(2):
                    for h in range(2):
                        mm(X3[:, (2 * t + h) * P:(2 * t + h + 1) * P], up[u][:, 4 + 2 * t, h, :], Z0[:, h, :],
                           start=(t == 0 and h == 0), stop=(t == 0), skip_group_check=True)

            def output_of_1(j, u):
                pe.wait_ge(s["z1_copied"], j + 1)
                for h in range(2):
                    ins = mm(X3[:, (2 + h) * P:(3 + h) * P], up[u][:, 3, h, :], Z1[:, h, :],
                             start=False, stop=True, skip_group_check=True)
                ins.then_inc(s["o_done"], 1)

            def body(j, u):
                front, levels, tail, out = parts(j)
                v = 1 - u
                if front:
                    project(j + 1)
                if levels:
                    join(j, u, 0, 0)
                if tail:
                    join64(j - 1, v, levels)
                if levels:
                    join(j, u, 0, 1)
                if tail:
                    corner64(j - 1, v)
                if levels:
                    grow_inverse(j, u, 0, 0)
                    grow_inverse(j, u, 0, 1)
                if out:
                    turn_output(j - 2)
                if levels:
                    join(j, u, 1, 0)
                if tail:
                    solve0(j - 1, v)
                if levels:
                    join(j, u, 1, 1)
                if out:
                    project_out(j - 2, 0)
                if levels:
                    grow_inverse(j, u, 1, 0)
                if out:
                    project_out(j - 2, 1)
                if levels:
                    grow_inverse(j, u, 1, 1)
                if tail:
                    carry(j - 1, v)
                if levels:
                    join(j, u, 2, 0)
                if out:
                    project_out(j - 2, 2)
                if levels:
                    join(j, u, 2, 1)
                if out:
                    project_out(j - 2, 3)
                if levels:
                    grow_inverse(j, u, 2, 0)
                if tail:
                    solve1(j - 1, v)
                    project_z(j - 1, 0)
                if levels:
                    grow_inverse(j, u, 2, 1)
                if front:
                    square_sums(j + 1)
                if levels:
                    join(j, u, 3, 0)
                if front:
                    gram0(j + 1)
                if tail:
                    project_z(j - 1, 1)
                if levels:
                    join(j, u, 3, 1)
                if tail:
                    output_of_0(j - 1, v)
                if levels:
                    grow_inverse(j, u, 3, 0)
                if tail:
                    output_of_1(j - 1, v)
                if levels:
                    grow_inverse(j, u, 3, 1)
                if front:
                    gram1(j + 1)
                if levels:
                    join32(j, u, 0)
                if tail:
                    project_z(j - 1, 2)
                if levels:
                    join32(j, u, 1)
                if front:
                    turn_v(j + 1)
                if levels:
                    corner32(j, u, 0)
                if tail:
                    project_z(j - 1, 3)
                if levels:
                    corner32(j, u, 1)

            pe.wait_ge(s["misc_loaded"], 32)
            project(0)
            square_sums(0)
            turn_v(0)
            gram0(0)
            gram1(0)
            for j in range(3):
                body(j, j % 2)
            with pe.Fori(1, STEPS // 2 - 1) as q:
                body(2 * q + 1, 1)
                body(2 * q + 2, 0)
            for j in range(STEPS - 1, STEPS + 2):
                body(j, j % 2)

        @block.scalar
        def _(act):
            f = nc.scalar.activation

            def last_tap(j):
                act.wait_ge(s["misc_loaded"], 32)
                for i in range(NF):
                    act.wait_ge(s["qkv_done"], 2 * j + i // 2 + 1)
                    if i == 0:
                        wait(act, s["silu_done"], j)
                        wait(act, s["siluv_done"], j)
                        wait(act, s["thv_done"], j)
                    bank = (X0, X1)[i // 2]
                    f(cv[:, i, :], bank[:, (i % 2) * S:(i % 2 + 1) * S], ACT.Copy,
                      scale=cwj[:, i, TAPS - 1:TAPS]).then_inc(s["tap_done"], 1)

            def load_taps(j):
                wait(act, s["conv_done"], 12 * j)
                act.wait_ge(s["misc_loaded"], 32)
                f(cwj[:, :, :], cw[:, head(j), :, :], ACT.Copy).then_inc(s["cols_done"], 1)
                act.wait_ge(s["cols_done"], j + 1)

            def load_tokens(j):
                act.dma_start(xb[:, :, :], c.xnT[:, :, bass.ds(seq(j) * S, S)]).then_inc(s["xb_loaded"], 16)

            def tanh_z(j):
                act.wait_ge(s["z_done"], j + 1)
                wait(act, s["zs_done"], j)
                f(thz[:, :, :], X2[:, :].rearrange("p (t n) -> p t n", t=2), ACT.Tanh, scale=0.5)\
                    .then_inc(s["thz_done"], 1)

            def copy_ogT(j):
                act.wait_ge(s["ogT_done"], j + 1)
                f(ogT[:, :, :], X3[:, :].rearrange("p (i t) -> p i t", i=4), ACT.Copy, scale=nw[:, 0:1])\
                    .then_inc(s["ogT_copied"], 1)

            def copy_level(j, u, l, a):
                act.wait_ge(s["tr_done"], 2 * (LEVELS * j + l) + a + 1)
                f(T[u][:, 2 * a:2 * a + 2, :], LV[a][:, S:2 * S].rearrange("p (i t) -> p i t", i=2), ACT.Copy)\
                    .then_inc(s["tr_copied"], 1)

            def copy_x32(j, a):
                act.wait_ge(s["x32_done"], 2 * j + a + 1)
                wait(act, s["t32_done"], 2 * j)
                f(x32[:, 2 * a:2 * a + 2, :], LV[a][:, 0:64].rearrange("p (i t) -> p i t", i=2), ACT.Copy, scale=-1.0)\
                    .then_inc(s["x32_copied"], 1)

            def copy_t32(j, u):
                act.wait_ge(s["t32_done"], 2 * j + 2)
                f(T[u][32:64, :, 0:32], LV[0][32:64, S:S + P].rearrange("p (i t) -> p i t", i=4), ACT.Copy)\
                    .then_inc(s["t32_copied"], 1)

            def tanh_qkv(j, n):
                act.wait_ge(s["conv_done"], 12 * j + 6 * n + 6)
                wait(act, s[("silu_done", "siluv_done")[n]], j)
                f(th[:, 2 * n:2 * n + 2, :], cv[:, 2 * n:2 * n + 2, :], ACT.Tanh, scale=0.5)\
                    .then_inc(s[("thqk_done", "thv_done")[n]], 1)

            def squares(j):
                act.wait_ge(s["silu_done"], j + 1)
                wait(act, s["ssum_done"], j)
                f(sq[:, :, :], s2[:, 0:2, :], ACT.Square).then_inc(s["sq_done"], 1)

            def decays(j):
                act.wait_ge(s["arg_done"], 2 * (j + 1))
                act.wait_ge(s["halves"], 2 * (j + 1))
                wait(act, s["up_done"], 8 * j)
                for t, (lo, hi) in enumerate(((0, S), (S, 3 * P))):
                    for h in range(2):
                        f(dec[:, h, lo:hi], arg[:, h, lo:hi], ACT.Exp, bias=gcol[:, t, h:h + 1])\
                            .then_inc(s["dec_done"], 1)

            def copy_V(j, u):
                act.wait_ge(s["vt_done"], j + 1)
                act.wait_ge(s["kn_done"], j + 1)
                wait(act, s["v1_done"], j - 1)
                wait(act, s["z0_done"], j - 1)
                for t in range(2):
                    f(V[u][:, t, :, :], X1[:, t * S:(t + 1) * S].rearrange("p (h d) -> p h d", h=2), ACT.Copy,
                      scale=kn[:, t:t + 1]).then_inc(s["V_done"], 1)

            def copy_z(j, bank, done, to, copied):
                act.wait_ge(s[done], j + 1)
                f(to[:, :, :], bank[:, 0:S].rearrange("p (h d) -> p h d", h=2), ACT.Copy).then_inc(s[copied], 1)

            def scale_output(j):
                act.wait_ge(s["rs_done"], j + 1)
                wait(act, s["og_done"], j)
                for i in range(4):
                    f(osc[:, i, :], X3[:, i * P:(i + 1) * P], ACT.Copy, scale=rs[:, i:i + 1])\
                        .then_inc(s["osc_done"], 1)

            def copy_out(j):
                act.wait_ge(s["out_done"], j + 1)
                wait(act, s["acc_done"], j)
                f(osum[:, :, :], X3[:, :].rearrange("p (t n) -> p t n", t=2), ACT.Copy).then_inc(s["out_copied"], 1)

            def copy64(j):
                act.wait_ge(s["s64_done"], j + 1)
                f(s64[64:P, :, :], TL[0][64:P, 0:S].rearrange("p (i t) -> p i t", i=4), ACT.Copy)\
                    .then_inc(s["s64_copied"], 1)

            def corner64(j, u):
                act.wait_ge(s["r64_done"], j + 1)
                f(R[u][0:64, :, 64:P], TL[1][0:64, 0:S].rearrange("p (i t) -> p i t", i=4), ACT.Copy, scale=-1.0)\
                    .then_inc(s["r64_copied"], 1)

            def output_squares(j):
                act.wait_ge(s["o_done"], j + 1)
                wait(act, s["orr_done"], j)
                for i in range(4):
                    f(osq[:, i, :], X3[:, i * P:(i + 1) * P], ACT.Square, accum_out=oss[:, i:i + 1])\
                        .then_inc(s["oss_done"], 1)

            def body(j, u):
                front, levels, tail, out = parts(j)
                if front:
                    load_taps(j + 1)
                    last_tap(j + 1)
                if tail:
                    copy64(j - 1)
                if out:
                    scale_output(j - 2)
                if tail:
                    corner64(j - 1, 1 - u)
                if levels:
                    copy_level(j, u, 0, 0)
                    copy_level(j, u, 0, 1)
                if out:
                    copy_ogT(j - 2)
                if tail:
                    copy_z(j - 1, TL[0], "z0_done", Z0, "z0_copied")
                if front:
                    tanh_qkv(j + 1, 0)
                if levels:
                    copy_level(j, u, 1, 0)
                    copy_level(j, u, 1, 1)
                if front:
                    squares(j + 1)
                    decays(j + 1)
                if levels:
                    copy_level(j, u, 2, 0)
                if out:
                    copy_out(j - 2)
                if tail:
                    copy_z(j - 1, TL[0], "z1_done", Z1, "z1_copied")
                if levels:
                    copy_level(j, u, 2, 1)
                if front:
                    tanh_qkv(j + 1, 1)
                if levels:
                    copy_level(j, u, 3, 0)
                    copy_level(j, u, 3, 1)
                    copy_x32(j, 0)
                    copy_x32(j, 1)
                    copy_t32(j, u)
                if tail:
                    output_squares(j - 1)
                if front:
                    copy_V(j + 1, 1 - u)
                if tail:
                    tanh_z(j - 1)
                if tail and levels:
                    load_tokens(j)

            load_tokens(0)
            load_taps(0)
            last_tap(0)
            tanh_qkv(0, 0)
            tanh_qkv(0, 1)
            squares(0)
            decays(0)
            copy_V(0, 0)
            for j in range(3):
                body(j, j % 2)
            with act.Fori(1, STEPS // 2 - 1) as q:
                body(2 * q + 1, 1)
                body(2 * q + 2, 0)
            for j in range(STEPS - 1, STEPS + 2):
                body(j, j % 2)

        @block.vector
        def _(vec):
            stt = nc.vector.scalar_tensor_tensor

            def neighbours(j, u, a):
                pair = slice(2 * a, 2 * a + 2)
                vec.wait_ge(s["up_done"], 8 * j + 2 * a + 2)
                wait(vec, s["r1_done"], 2 * j - 1 + a)
                nc.vector.tensor_tensor(seed[:, pair, :], dg[u][:, pair, :],
                                        c.level[:, 0:1, :].to_broadcast([P, 2, P]), ALU.mult)\
                    .then_inc(s["tmp_done"], 1)

            def seed_r(j, u, a):
                pair = slice(2 * a, 2 * a + 2)
                vec.wait_ge(s["tmp_done"], 2 * j + a + 1)
                wait(vec, s["z1_done"], j - 1)
                nc.vector.tensor_tensor(R[u][:, pair, :], seed[:, pair, :],
                                        c.ident[:, None, :].to_broadcast([P, 2, P]), ALU.add)\
                    .then_inc(s["r1_done"], 1)

            def seed_t(j, u, a):
                pair = slice(2 * a, 2 * a + 2)
                vec.wait_ge(s["r1_done"], 2 * j + a + 1)
                nc.vector.transpose(T[u][:, pair, :].rearrange("p i t -> p (i t)"),
                                    R[u][:, pair, :].rearrange("p i t -> p (i t)")).then_inc(s["t1_done"], 1)

            def turn_level(j, u, l, a):
                vec.wait_ge(s["tr_copied"], 2 * (LEVELS * j + l) + a + 1)
                nc.vector.transpose(R[u][:, 2 * a:2 * a + 2, :].rearrange("p i t -> p (i t)"),
                                    T[u][:, 2 * a:2 * a + 2, :].rearrange("p i t -> p (i t)"))\
                    .then_inc(s["r_done"], 1)

            def turn32(j, u):
                vec.wait_ge(s["t32_copied"], j + 1)
                quarters = LV[0][:, S:S + P].rearrange("p (i t) -> p i t", i=4)
                for r in (0, 64):
                    nc.vector.transpose(R[u][r:r + 32, :, r + 32:r + 64], quarters[r + 32:r + 64])\
                        .then_inc(s["r32_done"], 1)

            def look_up(j):
                vec.wait_ge(s["index_loaded"], 32)
                vec.wait_ge(s["entries"], 1)
                wait(vec, s["looked_up"], j)
                k = bass.ds(j % LUT, 1)
                nc.vector.tensor_scalar(hit[:, :], ix[:, bass.ds(j // LUT * LOOKED_UP, LOOKED_UP)], entry[:, k],
                                        table[:, k], ALU.is_equal, ALU.mult).then_inc(s["hit_done"], 1)

            def w_of_level(j, l, a):
                vec.wait_ge(s["s1_done"], 2 * (LEVELS * j + l) + a + 1)
                nc.vector.tensor_tensor(W[:, 2 * a:2 * a + 2, :], c.ident[:, None, :].to_broadcast([P, 2, P]),
                                        LV[a][:, 0:S].rearrange("p (i t) -> p i t", i=2), ALU.subtract)\
                    .then_inc(s["w_done"], 1)

            def silu_z(j):
                vec.wait_ge(s["thz_done"], j + 1)
                wait(vec, s["og_done"], j)
                stt(out=zs[:, :, :], in0=thz[:, :, :], scalar=1.0, in1=X2[:, :].rearrange("p (t n) -> p t n", t=2),
                    op0=ALU.add, op1=ALU.mult).then_inc(s["zs_done"], 1)

            def other_tap(j, n):
                bank, shift, i = (X0, X1)[n // 6], n % 6 // 2 + 1, n // 6 * 2 + n % 2
                vec.wait_ge(s["tap_done"], 4 * j + 2 * (n // 6) + 2)
                if n % 6 >= 2:
                    vec.wait_ge(s["conv_done"], 12 * j + n - 1)
                stt(out=cv[:, i, shift:S], in0=bank[:, (i % 2) * S:(i % 2 + 1) * S - shift],
                    scalar=cwj[:, i, TAPS - 1 - shift:TAPS - shift], in1=cv[:, i, shift:S],
                    op0=ALU.mult, op1=ALU.add).then_inc(s["conv_done"], 1)

            def silu_kq(j):
                vec.wait_ge(s["thqk_done"], j + 1)
                stt(out=s2[:, 0:2, :], in0=th[:, 0:2, :], scalar=1.0, in1=cv[:, 0:2, :],
                    op0=ALU.add, op1=ALU.mult).then_inc(s["silu_done"], 1)

            def columns(j):
                wait(vec, s["sc_done"], j)
                wait(vec, s["dec_done"], 4 * j)
                tiles, heads = bass.ds(2 * seq(j), 2), bass.ds(2 * head(j), 2)
                nc.vector.tensor_scalar(gcol[:, :, :], c.G[:, tiles, heads], -1.0, None, ALU.mult)\
                    .then_inc(s["halves"], 1)
                nc.vector.tensor_copy(bcol[:, :, :], c.beta[:, tiles, heads]).then_inc(s["halves"], 1)

            def norms(j):
                vec.wait_ge(s["ssum_done"], j + 1)
                wait(vec, s["kn_done"], j)
                wait(vec, s["nq_done"], j)
                nc.vector.tensor_scalar(ns[:, :], X0[:, 0:4], 4.0 * DELTA_EPS ** 2, None, ALU.max)\
                    .then_inc(s["ns_done"], 1)
                vec.wait_ge(s["ns_done"], j + 1)
                vec.wait_ge(s["halves"], 2 * (j + 1))
                nc.vector.reciprocal(rk[:, :], ns[:, 0:2]).then_inc(s["rk_done"], 1)
                vec.wait_ge(s["rk_done"], j + 1)
                wait(vec, s["up_done"], 8 * j)
                nc.vector.tensor_tensor(sc[:, :, :], bcol[:, :, :], rk[:, :, None].to_broadcast([P, 2, 2]), ALU.mult)\
                    .then_inc(s["sc_done"], 1)

            def second_tile(j, u):
                vec.wait_ge(s["a21_done"], j + 1)
                nc.vector.tensor_tensor(V1[:, :, :], V[u][:, 1, :, :], TL[1][:, 0:S].rearrange("p (h d) -> p h d", h=2),
                                        ALU.subtract).then_inc(s["v1_done"], 1)

            def scale_gram(j, u, x, tile, h):
                wait(vec, s["o_done"], j - 1)
                wait(vec, s["cm_done"], CM * (j - 1))
                vec.wait_ge(s["dec_done"], 4 * (j + 1))
                vec.wait_ge(s["sc_done"], j + 1)
                vec.wait_ge(s["gram_done"], 2 * j + tile + 1)
                n = 2 - tile
                to = up[u][:, 4 * x:4 * x + 3:2, h, :] if tile == 0 else up[u][:, 1 + 2 * x:2 + 2 * x, h, :]
                bank, d = (TL[1], dec[:, h, 0:S]) if tile == 0 else (TL[0], dec[:, h, S:3 * P])
                stt(out=to, in0=bank[:, x * n * P:(x + 1) * n * P].rearrange("p (n t) -> p n t", n=n),
                    scalar=sc[:, tile, h:h + 1], in1=d.rearrange("p (n t) -> p n t", n=n),
                    op0=ALU.mult, op1=ALU.mult).then_inc(s["up_done"], 1)

            def decayed_products(j, u, between):
                scale_gram(j, u, 0, 0, 0)
                scale_gram(j, u, 0, 0, 1)
                neighbours(j, u, 0)
                scale_gram(j, u, 0, 1, 0)
                seed_r(j, u, 0)
                scale_gram(j, u, 0, 1, 1)
                seed_t(j, u, 0)
                neighbours(j, u, 1)
                between()
                seed_r(j, u, 1)
                seed_t(j, u, 1)

            def decayed_q_products(j, u):
                for tile in range(2):
                    for h in range(2):
                        scale_gram(j, u, 1, tile, h)

            def root_mean_square(j, u):
                vec.wait_ge(s["oss_done"], 4 * (j + 1))
                vec.wait_ge(s["nq_done"], j + 1)
                wait(vec, s["rs_done"], j)
                stt(out=orr[:, :].rearrange("p (t h) -> p t h", t=2), in0=oss[:, :].rearrange("p (t h) -> p t h", t=2),
                    scalar=4.0 / DK, in1=nq[u][:, :, None].to_broadcast([P, 2, 2]),
                    op0=ALU.mult, op1=ALU.add).then_inc(s["orr_done"], 1)

            def q_guard(j, u):
                vec.wait_ge(s["ns_done"], j + 1)
                wait(vec, s["orr_done"], j - 1)
                nc.vector.tensor_scalar(nq[u][:, :], ns[:, 2:4], 4.0 * EPS_Q, None, ALU.mult).then_inc(s["nq_done"], 1)

            def body(j, u):
                front, levels, tail, out = parts(j)
                v = 1 - u
                if out:
                    silu_z(j - 2)
                if front:
                    other_tap(j + 1, 0)
                    other_tap(j + 1, 1)
                if levels:
                    w_of_level(j, 0, 0)
                if front:
                    other_tap(j + 1, 2)
                if levels:
                    w_of_level(j, 0, 1)
                if front:
                    other_tap(j + 1, 3)
                if levels:
                    turn_level(j, u, 0, 0)
                if front:
                    other_tap(j + 1, 4)
                if levels:
                    turn_level(j, u, 0, 1)
                if front:
                    other_tap(j + 1, 5)
                if levels:
                    w_of_level(j, 1, 0)
                if front:
                    other_tap(j + 1, 6)
                if levels:
                    w_of_level(j, 1, 1)
                if front:
                    silu_kq(j + 1)
                if levels:
                    turn_level(j, u, 1, 0)
                if front:
                    other_tap(j + 1, 7)
                if levels:
                    turn_level(j, u, 1, 1)
                if front:
                    other_tap(j + 1, 8)
                    columns(j + 1)
                if levels:
                    w_of_level(j, 2, 0)
                if tail:
                    second_tile(j - 1, v)
                if levels:
                    w_of_level(j, 2, 1)
                if front:
                    other_tap(j + 1, 9)
                if levels:
                    turn_level(j, u, 2, 0)
                if front:
                    other_tap(j + 1, 10)
                if levels:
                    turn_level(j, u, 2, 1)
                if front:
                    other_tap(j + 1, 11)
                if levels:
                    w_of_level(j, 3, 0)
                if front:
                    norms(j + 1)
                if levels:
                    w_of_level(j, 3, 1)
                    look_up(j)
                    turn_level(j, u, 3, 0)
                if levels:
                    turn_level(j, u, 3, 1)
                if front:
                    decayed_products(j + 1, v, lambda: turn32(j, u))
                if levels and not front:
                    turn32(j, u)
                if tail:
                    root_mean_square(j - 1, v)
                if front:
                    q_guard(j + 1, v)
                    decayed_q_products(j + 1, v)

            nc.vector.memset(c.y[:, :, :], 0.0).then_inc(s["zeroed"], 1)
            nc.vector.memset(s64[0:64, :, :], 0.0).then_inc(s["zeroed"], 1)
            nc.vector.memset(c.w_table[:, :], 0.0).then_inc(s["zeroed"], 1)
            vec.wait_ge(s["zeroed"], 3)
            for n in range(12):
                other_tap(0, n)
            columns(0)
            silu_kq(0)
            norms(0)
            q_guard(0, 0)
            decayed_products(0, 0, lambda: None)
            decayed_q_products(0, 0)
            for j in range(3):
                body(j, j % 2)
            with vec.Fori(1, STEPS // 2 - 1) as q:
                body(2 * q + 1, 1)
                body(2 * q + 2, 0)
            for j in range(STEPS - 1, STEPS + 2):
                body(j, j % 2)

        @block.gpsimd
        def _(pool):
            tt = nc.gpsimd.tensor_tensor

            def exponents(j):
                pool.wait_ge(s["grow_loaded"], 16 * (j + 1))
                wait(pool, s["dec_done"], 4 * j)
                tt(arg[:, :, 0:S], grow[:, :, :], c.cut[:, None, :].to_broadcast([P, 2, S]), ALU.add)\
                    .then_inc(s["arg_done"], 1)
                tt(arg[:, :, S:3 * P], grow[:, :, P:S], c.cut[:, None, 0:P].to_broadcast([P, 2, P]), ALU.add)\
                    .then_inc(s["arg_done"], 1)

            def joining_blocks(j, u, which):
                for n in which:
                    a, l = (n, 0) if n < 2 else (1, n - 1)
                    pair = slice(2 * n, 2 * n + 2) if l == 0 else slice(0, 4)
                    pool.wait_ge(s["up_done"], 8 * j + 2 * a + 2)
                    wait(pool, s["s1_done"], 2 * LEVELS * (j - 1) + 2 * l + a + 1)
                    tt(cm[:, l, pair, :], dg[u][:, pair, :],
                       c.level[:, l + 1:l + 2, :].to_broadcast([P, pair.stop - pair.start, P]), ALU.mult)\
                        .then_inc(s["cm_done"], 1)

            def gate_output(j):
                pool.wait_ge(s["osc_done"], 4 * (j + 1))
                pool.wait_ge(s["zs_done"], j + 1)
                wait(pool, s["ogT_done"], j)
                tt(og[:, :, :], osc[:, :, :], zs[:, :, :].rearrange("p t (h d) -> p (t h) d", h=2), ALU.mult)\
                    .then_inc(s["og_done"], 1)

            def accumulate(j):
                pool.wait_ge(s["out_copied"], j + 1)
                if isinstance(j, int) and j == 0:
                    pool.wait_ge(s["zeroed"], 3)
                wait(pool, s["acc_done"], j)
                rows = c.y[:, bass.ds(2 * seq(j), 2), :]
                tt(rows, rows, osum[:, :, :], ALU.add).then_inc(s["acc_done"], 1)

            def silu_v(j):
                pool.wait_ge(s["thv_done"], j + 1)
                wait(pool, s["vt_done"], j)
                tt(th[:, 2:4, :], th[:, 2:4, :], cv[:, 2:4, :], ALU.mult).then_inc(s["thv_used"], 1)
                pool.wait_ge(s["thv_used"], j + 1)
                tt(s2[:, 2:4, :], th[:, 2:4, :], cv[:, 2:4, :], ALU.add).then_inc(s["siluv_done"], 1)

            def add_looked_up(j):
                pool.wait_ge(s["hit_done"], j + 1)
                if isinstance(j, int) and j == 0:
                    pool.wait_ge(s["zeroed"], 3)
                wait(pool, s["looked_up"], j)
                cols = bass.ds(j // LUT * LOOKED_UP, LOOKED_UP)
                tt(c.w_table[:, cols], c.w_table[:, cols], hit[:, :], ALU.add).then_inc(s["looked_up"], 1)

            def key_norm(j):
                pool.wait_ge(s["ns_done"], j + 1)
                wait(pool, s["V_done"], 2 * j)
                tt(kn[:, :], ns[:, 0:2], half[:, 0:2], ALU.pow).then_inc(s["kn_done"], 1)

            def output_scale(j):
                pool.wait_ge(s["orr_done"], j + 1)
                wait(pool, s["og_done"], j)
                tt(rs[:, :], orr[:, :], mhalf[:, :], ALU.pow).then_inc(s["rs_done"], 1)

            nc.gpsimd.memset(half[:, :], 0.5).then_inc(s["powers"], 1)
            nc.gpsimd.memset(mhalf[:, :], -0.5).then_inc(s["powers"], 1)
            nc.gpsimd.iota(entry[:, :], pattern=[[1, LUT]], base=0, channel_multiplier=0,
                           allow_small_or_imprecise_dtypes=True).then_inc(s["entries"], 1)
            pool.wait_ge(s["powers"], 2)
            def body(j, u):
                front, levels, tail, out = parts(j)
                if levels:
                    joining_blocks(j, u, range(2))
                if out:
                    output_scale(j - 2)
                if levels:
                    joining_blocks(j, u, range(2, 3))
                if out:
                    gate_output(j - 2)
                if levels:
                    joining_blocks(j, u, range(3, CM))
                if front:
                    exponents(j + 1)
                if out:
                    accumulate(j - 2)
                if front:
                    silu_v(j + 1)
                    key_norm(j + 1)
                if levels:
                    add_looked_up(j)

            exponents(0)
            silu_v(0)
            key_norm(0)
            for j in range(3):
                body(j, j % 2)
            with pool.Fori(1, STEPS // 2 - 1) as q:
                body(2 * q + 1, 1)
                body(2 * q + 2, 0)
            for j in range(STEPS - 1, STEPS + 2):
                body(j, j % 2)

        inner.close()
        m.clear()


CH = 512
NCH = TOK // CH


class FeedForward:

    def __init__(self, m, tag, xnT, gate, up, down, inner, y, banks):
        self.tag, self.xnT, self.gate, self.up, self.down, self.y = tag, xnT, gate, up, down, y
        self.tiles = [(i, min(P, inner - i)) for i in range(0, inner, P)]
        self.n = len(self.tiles)
        self.pairs, self.out = [(banks[0], banks[1]), (banks[2], banks[3]), (banks[4], banks[5])], banks[6:8]
        self.th = m.sb(tag + "th", [P, 2, CH])
        self.gated = m.sb(tag + "gated", [P, 2, CH])
        self.hid = m.sb(tag + "hid", [P, self.n, CH])
        self.inner_done, self.tanh_done, self.gated_done, self.hid_done, self.out_done, self.out_copied = (
            m.sem(tag + n) for n in ("inner_done", "tanh_done", "gated_done", "hid_done", "out_done", "out_copied"))

    def tensor(self, nc, pe, c):
        for i, (lo, rows) in enumerate(self.tiles):
            t = c * self.n + i
            wait(pe, self.hid_done, t - 2)
            for w, bank in ((self.gate, self.pairs[i % 3][0]), (self.up, self.pairs[i % 3][1])):
                for k in range(KT):
                    ins = nc.tensor.matmul(bank[0:rows, :], w[:, k, lo:lo + rows],
                                           self.xnT[:, k, bass.ds(c * CH, CH)], start=(k == 0), stop=(k == KT - 1))
            ins.then_inc(self.inner_done, 1)
        pe.wait_ge(self.hid_done, (c + 1) * self.n)
        for half in range(2):
            wait(pe, self.out_copied, 2 * (c - 1) + half + 1)
            for r in range(2):
                s = (2 * half + r) * P
                for i, (lo, rows) in enumerate(self.tiles):
                    ins = nc.tensor.matmul(self.out[half][:, r * H:(r + 1) * H], self.hid[0:rows, i, s:s + P],
                                           self.down[0:rows, i, :], start=(i == 0), stop=(i == self.n - 1))
            ins.then_inc(self.out_done, 1)

    def scalar(self, nc, act, c):
        for i, (lo, rows) in enumerate(self.tiles):
            t = c * self.n + i
            act.wait_ge(self.inner_done, t + 1)
            wait(act, self.gated_done, t - 1)
            nc.scalar.activation(self.th[0:rows, i % 2, :], self.pairs[i % 3][0][0:rows, :], ACT.Tanh, scale=0.5)\
                .then_inc(self.tanh_done, 1)
        for half in range(2):
            act.wait_ge(self.out_done, 2 * c + half + 1)
            nc.scalar.activation(self.y[:, bass.ds(4 * c + 2 * half, 2), :],
                                 self.out[half][:, :].rearrange("p (t n) -> p t n", t=2), ACT.Copy)\
                .then_inc(self.out_copied, 1)

    def vector(self, nc, vec, c):
        stt = nc.vector.scalar_tensor_tensor
        for i, (lo, rows) in enumerate(self.tiles):
            t = c * self.n + i
            gate, up = self.pairs[i % 3]
            g = self.gated[0:rows, i % 2, :]
            vec.wait_ge(self.tanh_done, t + 1)
            wait(vec, self.hid_done, t - 1)
            stt(out=g, in0=self.th[0:rows, i % 2, :], scalar=1.0, in1=gate[0:rows, :], op0=ALU.add, op1=ALU.mult)\
                .then_inc(self.gated_done, 1)
            vec.wait_ge(self.gated_done, t + 1)
            if i == 0:
                wait(vec, self.out_done, 2 * c)
            stt(out=self.hid[0:rows, i, :], in0=g, scalar=0.5, in1=up[0:rows, :], op0=ALU.mult, op1=ALU.mult)\
                .then_inc(self.hid_done, 1)


E, TOPK, I_E, I_S, CAP = 16, 4, 176, 352, 128
SLOTS = 4
IR = I_E - P
NS = (I_S + P - 1) // P


def experts(nc, c, gate_w, w_gate, w_up, w_down, sw_gate, sw_up, sw_down, rows_dram, out_dram):
    NSLOT = E * CAP
    with ExitStack() as stack:
        m = Memory(nc, stack)
        gw = m.sb("gw", [P, KT, E])
        sg = m.sb("sg", [P, KT, I_S])
        su = m.sb("su", [P, KT, I_S])
        sd = m.sb("sd", [P, NS, H])
        zero = m.sb("zero", [P, 4, H])
        lg = m.sb("lg", [P, NT, E])
        mx = m.sb("mx", [P, NT])
        ex = m.sb("ex", [P, NT, E])
        sm = m.sb("sm", [P, NT])
        rc = m.sb("rc", [P, NT])
        score = m.sb("score", [P, NT, E])
        top = m.sb("top", [P, NT, 8])
        topi = m.sb("topi", [P, NT, 8], U32)
        topf = m.sb("topf", [P, NT, 8])
        den = m.sb("den", [P, NT])
        wgt = m.sb("wgt", [P, NT, TOPK])
        iota_e = m.sb("iota_e", [P, E])
        hot = m.sb("hot", [P, TOPK, NT, E])
        mask = m.sb("mask", [P, NT, E])
        before = m.sb("before", [P, NT, E])
        rank = m.sb("rank", [P, NT, E])
        mine = m.sb("mine", [P, TOPK, NT, E])
        rk = m.sb("rk_e", [P, TOPK, NT])
        fits = m.sb("fits", [P, TOPK, NT])
        slot = m.sb("slot", [P, TOPK, NT])
        slot_i = m.sb("slot_i", [P, TOPK, NT], U32)
        got = m.sb("got", [P, 8, TOPK, H])
        xe = m.sb("xe", [P, SLOTS, H])
        xT = m.sb("xT", [P, 2, KT, P])
        wg = m.sb("wg", [P, SLOTS, KT, I_E])
        wu = m.sb("wu", [P, SLOTS, KT, I_E])
        wd0 = m.sb("wd0", [P, SLOTS, H])
        wd1 = m.sb("wd1", [IR, SLOTS, H])
        th = m.sb("th_e", [P, 2, 2, P])
        ga = m.sb("ga_e", [P, 2, 2, P])
        hT = m.sb("hT_e", [P, 2, 2, P])
        eo = m.sb("eo", [P, 2, H])
        banks = [m.ps(f"me{i}") for i in range(8)]
        XT, GU, EO = banks[0:2], banks[2:4], banks[4:6]
        ff = FeedForward(m, "sh_", c.xnT, sg, su, sd, I_S, c.y, banks)
        ROUTED = 3 + 2 * NT + 3 + TOPK + 1 + NT
        names = ("small_loaded shared_loaded zero_ready zeroed logits_done iota_done route exp_done "
                 "ranks_done slots_ready scattered turned turned_copied inner_done tanh_done gated_done "
                 "hid_done outer_done outer_copied combined").split()
        s = {n: m.sem("m_" + n) for n in names}
        weights_loaded, rows_loaded = ([m.sem(f"m_{n}{u}") for u in range(SLOTS)]
                                       for n in ("weights_loaded", "rows_loaded"))
        stored = [m.sem(f"m_stored{u}") for u in range(2)]
        gathered = [m.sem(f"m_gathered{i}") for i in range(4)]
        inner = stack.enter_context(ExitStack())
        block = inner.enter_context(nc.Block())

        def round_of(e, u, slots=SLOTS):
            return (e - u) // slots + 1

        @block.sync
        def _(sp):
            sp.dma_start(gw[:, :, :], gate_w).then_inc(s["small_loaded"], 16)
            for w, src in ((sg, sw_gate), (su, sw_up)):
                sp.dma_start(w[:, :, :], src.rearrange("(k p) i -> p k i", p=P)).then_inc(s["shared_loaded"], 16)
            for i in range(NS):
                r = min(P, I_S - i * P)
                sp.dma_start(sd[0:r, i, :], sw_down[i * P:i * P + r, :]).then_inc(s["shared_loaded"], 16)
            sp.wait_ge(s["zero_ready"], 1)
            for i in range(NSLOT // 512):
                sp.dma_start(rows_dram[512 * i:512 * i + 512, :].rearrange("(p n) h -> p n h", p=P), zero[:, :, :])\
                    .then_inc(s["zeroed"], 16)
            sp.dma_start(out_dram[NSLOT:NSLOT + 1, :], zero[0:1, 0, :]).then_inc(s["zeroed"], 16)

            def load(e, u):
                wait(sp, s["hid_done"], e - SLOTS + 1)
                for w, src in ((wg, w_gate), (wu, w_up)):
                    sp.dma_start(w[:, u, :, :], src[e].rearrange("(k p) i -> p k i", p=P))\
                        .then_inc(weights_loaded[u], 16)
                wait(sp, s["outer_copied"], e - SLOTS + 1)
                sp.dma_start(wd0[:, u, :], w_down[e, 0:P, :]).then_inc(weights_loaded[u], 16)
                sp.dma_start(wd1[:, u, :], w_down[e, P:I_E, :]).then_inc(weights_loaded[u], 16)

            def load_rows(e, u):
                if isinstance(e, int) and e == 0:
                    sp.wait_ge(s["scattered"], 16 * NT * TOPK)
                wait(sp, s["turned"], e - SLOTS + 1)
                sp.dma_start(xe[:, u, :], rows_dram[e * CAP:(e + 1) * CAP, :] if isinstance(e, int)
                             else rows_dram[bass.ds(e * CAP, CAP), :]).then_inc(rows_loaded[u], 16)

            for u in range(SLOTS):
                load(u, u)
            for u in range(SLOTS):
                load_rows(u, u)
            with sp.Fori(1, E // SLOTS) as q:
                for u in range(SLOTS):
                    load(SLOTS * q + u, u)
                    load_rows(SLOTS * q + u, u)

        @block.gpsimd
        def _(pool):
            nc.gpsimd.memset(zero[:, :, :], 0.0).then_inc(s["zero_ready"], 1)
            nc.gpsimd.iota(iota_e[:, :], pattern=[[1, E]], base=0, channel_multiplier=0,
                           allow_small_or_imprecise_dtypes=True).then_inc(s["iota_done"], 1)
            pool.wait_ge(s["zeroed"], 16 * (NSLOT // 512 + 1))
            pool.wait_ge(s["slots_ready"], 1)
            for t in range(NT):
                for k in range(TOPK):
                    nc.gpsimd.indirect_dma_start(
                        out=rows_dram, out_offset=bass.IndirectOffsetOnAxis(ap=slot_i[:, k, t:t + 1], axis=0),
                        in_=c.xn[:, t, :], in_offset=None, bounds_check=NSLOT - 1, oob_is_err=False)\
                        .then_inc(s["scattered"], 16)
            for u in range(2):
                pool.wait_ge(stored[u], 16 * E // 2)
            for t in range(NT):
                if t >= 8 and t % 4 == 0:
                    pool.wait_ge(s["combined"], 4 + (t - 4) * TOPK)
                for k in range(TOPK):
                    nc.gpsimd.indirect_dma_start(
                        out=got[:, t % 8, k, :], out_offset=None, in_=out_dram,
                        in_offset=bass.IndirectOffsetOnAxis(ap=slot_i[:, k, t:t + 1], axis=0))\
                        .then_inc(gathered[t // 4], 16)
            for i in range(4):
                pool.wait_ge(gathered[i], 16 * NT * TOPK // 4)

        @block.tensor
        def _(pe):
            mm, tr = nc.tensor.matmul, nc.tensor.transpose
            pe.wait_ge(s["small_loaded"], 16)
            for t in range(NT):
                for k in range(KT):
                    ins = mm(banks[6][:, t * E:(t + 1) * E], c.xnT[:, k, t * P:(t + 1) * P], gw[:, k, :],
                             start=(k == 0), stop=(k == KT - 1))
            ins.then_inc(s["logits_done"], 1)
            pe.wait_ge(s["route"], ROUTED)
            mm(banks[6][:, 0:NT * E], c.tri_strict[:, :], mask[:, :, :], start=True, stop=False)
            mm(banks[6][:, 0:NT * E], c.ones[:, :], before[:, :, :], start=False, stop=True)\
                .then_inc(s["ranks_done"], 1)

            def turn(e, u):
                pe.wait_ge(rows_loaded[u], 16 * round_of(e, u))
                wait(pe, s["turned_copied"], e - 1)
                for k in range(KT):
                    ins = tr(XT[u % 2][:, k * P:(k + 1) * P], xe[:, u, k * P:(k + 1) * P], c.ident[:, :])
                ins.then_inc(s["turned"], 1)

            def inner(e, u):
                pe.wait_ge(weights_loaded[u], 64 * round_of(e, u))
                pe.wait_ge(s["turned_copied"], e + 1)
                wait(pe, s["hid_done"], e - 1)
                for n, w in enumerate((wg, wu)):
                    for i, (lo, rows) in enumerate(((0, P), (P, IR))):
                        for k in range(KT):
                            ins = mm(GU[u % 2][0:rows, (2 * n + i) * P:(2 * n + i + 1) * P], w[:, u, k, lo:lo + rows],
                                     xT[:, u % 2, k, :], start=(k == 0), stop=(k == KT - 1))
                ins.then_inc(s["inner_done"], 1)

            def outer(e, u):
                pe.wait_ge(s["hid_done"], e + 1)
                wait(pe, s["outer_copied"], e - 1)
                mm(EO[u % 2][:, 0:H], hT[:, u % 2, 0, :], wd0[:, u, :], start=True, stop=False)
                mm(EO[u % 2][:, 0:H], hT[0:IR, u % 2, 1, :], wd1[:, u, :], start=False, stop=True)\
                    .then_inc(s["outer_done"], 1)

            pe.wait_ge(s["shared_loaded"], 16 * (2 + NS))
            pe.wait_ge(s["route"], ROUTED + 1)
            ff.tensor(nc, pe, 0)
            ff.tensor(nc, pe, 1)
            pe.wait_ge(ff.out_copied, 4)
            turn(0, 0)
            inner(0, 0)
            turn(1, 1)
            inner(1, 1)

            def expert(e, u):
                outer(e - 2, (u - 2) % SLOTS)
                turn(e, u)
                inner(e, u)

            for u in range(2, SLOTS):
                expert(u, u)
            with pe.Fori(1, E // SLOTS) as q:
                for u in range(SLOTS):
                    expert(SLOTS * q + u, u)
            outer(E - 2, SLOTS - 2)
            outer(E - 1, SLOTS - 1)
            pe.wait_ge(s["outer_copied"], E)
            ff.tensor(nc, pe, 2)
            ff.tensor(nc, pe, 3)

        @block.scalar
        def _(act):
            f = nc.scalar.activation
            act.wait_ge(s["route"], 2)
            f(ex[:, :, :], lg[:, :, :], ACT.Exp).then_inc(s["exp_done"], 1)
            ff.scalar(nc, act, 0)
            ff.scalar(nc, act, 1)

            def first(e, u):
                act.wait_ge(s["turned"], e + 1)
                wait(act, s["inner_done"], e - 1)
                f(xT[:, u, :, :], XT[u][:, 0:S].rearrange("p (k t) -> p k t", k=KT), ACT.Copy)\
                    .then_inc(s["turned_copied"], 1)
                act.wait_ge(s["inner_done"], e + 1)
                wait(act, s["gated_done"], 2 * (e - 1))
                f(th[:, u, 0, :], GU[u][:, 0:P], ACT.Tanh, scale=0.5).then_inc(s["tanh_done"], 1)
                f(th[0:IR, u, 1, :], GU[u][0:IR, P:2 * P], ACT.Tanh, scale=0.5).then_inc(s["tanh_done"], 1)

            def second(e, u):
                act.wait_ge(s["outer_done"], e + 1)
                wait(act, stored[u], 16 * (round_of(e, u, 2) - 1))
                f(eo[:, u, :], EO[u][:, 0:H], ACT.Copy).then_inc(s["outer_copied"], 1)
                to = out_dram[e * CAP:(e + 1) * CAP, :] if isinstance(e, int) else out_dram[bass.ds(e * CAP, CAP), :]
                act.wait_ge(s["outer_copied"], e + 1)
                act.dma_start(to, eo[:, u, :]).then_inc(stored[u], 16)

            first(0, 0)
            first(1, 1)

            for u in range(2, SLOTS):
                second(u - 2, u % 2)
                first(u, u % 2)
            with act.Fori(1, E // SLOTS) as q:
                for u in range(SLOTS):
                    second(SLOTS * q + u - 2, u % 2)
                    first(SLOTS * q + u, u % 2)
            second(E - 2, 0)
            second(E - 1, 1)
            ff.scalar(nc, act, 2)
            ff.scalar(nc, act, 3)

        @block.vector
        def _(vec):
            stt, tt, ts = nc.vector.scalar_tensor_tensor, nc.vector.tensor_tensor, nc.vector.tensor_scalar
            n = 0

            def step(ins):
                nonlocal n
                n += 1
                ins.then_inc(s["route"], 1)

            def done(ins):
                step(ins)
                vec.wait_ge(s["route"], n)

            def over(col, width):
                return col[:, :, None].to_broadcast([P, NT, width])

            logits = banks[6][:, 0:NT * E].rearrange("p (t e) -> p t e", e=E)
            vec.wait_ge(s["logits_done"], 1)
            done(nc.vector.tensor_reduce(mx[:, :], logits, AX.X, ALU.max))
            done(tt(lg[:, :, :], logits, over(mx, E), ALU.subtract))
            vec.wait_ge(s["exp_done"], 1)
            done(nc.vector.tensor_reduce(sm[:, :], ex[:, :, :], AX.X, ALU.add))
            nc.vector.reciprocal(rc[:, :], sm[:, :]).then_inc(s["combined"], 1)
            vec.wait_ge(s["combined"], 1)
            tt(score[:, :, :], ex[:, :, :], over(rc, E), ALU.mult).then_inc(s["combined"], 1)
            vec.wait_ge(s["combined"], 2)
            for t in range(NT):
                step(nc.vector.max(top[:, t, :], score[:, t, :]))
            vec.wait_ge(s["route"], n)
            for t in range(NT):
                step(nc.vector.max_index(topi[:, t, :], top[:, t, :], score[:, t, :]))
            vec.wait_ge(s["route"], n)
            done(nc.vector.tensor_copy(topf[:, :, :], topi[:, :, :]))
            done(nc.vector.tensor_reduce(den[:, :], top[:, :, 0:TOPK], AX.X, ALU.add))
            done(nc.vector.tensor_scalar(den[:, :], den[:, :], 1e-20, None, ALU.add))
            nc.vector.reciprocal(rc[:, :], den[:, :]).then_inc(s["combined"], 1)
            vec.wait_ge(s["combined"], 3)
            tt(wgt[:, :, :], top[:, :, 0:TOPK], over(rc, TOPK), ALU.mult).then_inc(s["combined"], 1)
            vec.wait_ge(s["iota_done"], 1)
            for k in range(TOPK):
                step(tt(hot[:, k, :, :], iota_e[:, None, :].to_broadcast([P, NT, E]),
                        over(topf[:, :, k], E), ALU.is_equal))
            vec.wait_ge(s["route"], n)
            done(nc.vector.tensor_reduce(mask[:, :, :], hot[:, :, :, :].rearrange("p k t e -> p t e k"),
                                         AX.X, ALU.add))
            done(nc.vector.memset(before[:, 0, :], 0.0))
            for t in range(1, NT):
                done(tt(before[:, t, :], before[:, t - 1, :], mask[:, t - 1, :], ALU.add))
            assert n == ROUTED
            vec.wait_ge(s["ranks_done"], 1)
            done(nc.vector.tensor_copy(rank[:, :, :], banks[6][:, 0:NT * E].rearrange("p (t e) -> p t e", e=E)))
            for k in range(TOPK):
                step(tt(mine[:, k, :, :], hot[:, k, :, :], rank[:, :, :], ALU.mult))
            vec.wait_ge(s["route"], n)
            done(nc.vector.tensor_reduce(rk[:, :, :], mine[:, :, :, :], AX.X, ALU.add))
            done(ts(fits[:, :, :], rk[:, :, :], float(CAP), None, ALU.is_lt))
            done(stt(out=slot[:, :, :], in0=topf[:, :, 0:TOPK].rearrange("p t k -> p k t"), scalar=float(CAP),
                     in1=rk[:, :, :], op0=ALU.mult, op1=ALU.add))
            done(stt(out=slot[:, :, :], in0=slot[:, :, :], scalar=-float(NSLOT), in1=fits[:, :, :],
                     op0=ALU.add, op1=ALU.mult))
            ts(slot_i[:, :, :], slot[:, :, :], float(NSLOT), None, ALU.add).then_inc(s["slots_ready"], 1)
            ff.vector(nc, vec, 0)
            ff.vector(nc, vec, 1)

            def gate(e, u):
                for i, rows in enumerate((P, IR)):
                    vec.wait_ge(s["tanh_done"], 2 * e + 2)
                    if i == 0:
                        wait(vec, s["hid_done"], e - 1)
                    stt(out=ga[0:rows, u, i, :], in0=th[0:rows, u, i, :], scalar=1.0,
                        in1=GU[u][0:rows, i * P:(i + 1) * P], op0=ALU.add, op1=ALU.mult).then_inc(s["gated_done"], 1)
                for i, rows in enumerate((P, IR)):
                    vec.wait_ge(s["gated_done"], 2 * e + i + 1)
                    if i == 0:
                        wait(vec, s["outer_done"], e - 1)
                    ins = stt(out=hT[0:rows, u, i, :], in0=ga[0:rows, u, i, :], scalar=0.5,
                              in1=GU[u][0:rows, (2 + i) * P:(3 + i) * P], op0=ALU.mult, op1=ALU.mult)
                ins.then_inc(s["hid_done"], 1)

            gate(0, 0)
            gate(1, 1)
            for u in range(2, SLOTS):
                gate(u, u % 2)
            with vec.Fori(1, E // SLOTS) as q:
                for u in range(SLOTS):
                    gate(SLOTS * q + u, u % 2)
            ff.vector(nc, vec, 2)
            ff.vector(nc, vec, 3)
            vec.wait_ge(ff.out_copied, 2 * NCH)
            n_c = 4
            for t0 in range(0, NT, 4):
                vec.wait_ge(gathered[t0 // 4], 16 * TOPK * 4)
                for k in range(TOPK):
                    for t in range(t0, t0 + 4):
                        if k:
                            vec.wait_ge(s["combined"], n_c - 3)
                        stt(out=c.y[:, t, :], in0=got[:, t % 8, k, :], scalar=wgt[:, t, k:k + 1], in1=c.y[:, t, :],
                            op0=ALU.mult, op1=ALU.add).then_inc(s["combined"], 1)
                        n_c += 1
            vec.wait_ge(s["combined"], n_c)

        inner.close()
        m.clear()


HQ, HKV, DH = 16, 4, 128
QG = HQ // HKV
RANK = 32
MAX_LEN = 512.0
GAMMA_MIN = 1e-6
NB = QG + 2
SC = P + S
FAR = -1e30
ASTEPS = HKV * B


def attention_bias(nc, c, wa, wb, pol_dir, pol_gate, gtp):
    with ExitStack() as stack:
        m = Memory(nc, stack)
        wab = m.sb("wab_pol", [P, KT, 2, RANK])
        pd, gt, pg = (m.sb(n, [P, HQ]) for n in ("pol_dir_b", "gtp_b", "pol_gate_b"))
        mn, ex, ln, soft, pc, ch, tg = (m.sb("ab_" + n, [P, HQ]) for n in "mn ex ln soft pc ch tg".split())
        dist = m.sb("dist", [P, SC])
        cut = m.sb("later", [P, SC])
        at = m.sb("at", [RANK, TOK])
        bt = m.sb("bt", [RANK, TOK])
        banks = [m.ps(f"ab{i}") for i in range(4)]
        loaded, tables, dve, act_done, projected, copied, products, nb_step = (
            m.sem("bias_" + n) for n in "loaded tables dve act_done projected copied products nb_step".split())
        inner = stack.enter_context(ExitStack())
        block = inner.enter_context(nc.Block())

        @block.sync
        def _(sp):
            for i, w in enumerate((wa, wb)):
                sp.dma_start(wab[:, :, i, :], w.rearrange("(k p) r -> p k r", p=P)).then_inc(loaded, 16)
            for to, src in ((pd, pol_dir), (gt, gtp), (pg, pol_gate)):
                sp.dma_start(to[:, :], src[None, :].to_broadcast([P, HQ])).then_inc(loaded, 16)

        @block.gpsimd
        def _(pool):
            nc.gpsimd.iota(dist[:, 0:P], pattern=[[-1, P]], base=0, channel_multiplier=1,
                           allow_small_or_imprecise_dtypes=True).then_inc(tables, 1)
            nc.gpsimd.iota(dist[:, P:SC], pattern=[[-1, S]], base=P, channel_multiplier=1,
                           allow_small_or_imprecise_dtypes=True).then_inc(tables, 1)
            nc.gpsimd.memset(cut[:, :], 0.0).then_inc(tables, 1)
            pool.wait_ge(tables, 3)
            for lo, n, base in ((0, P, 0), (P, S, P)):
                nc.gpsimd.affine_select(out=cut[:, lo:lo + n], in_=cut[:, lo:lo + n], compare_op=ALU.is_ge, fill=FAR,
                                        base=base, pattern=[[-1, n]], channel_multiplier=1).then_inc(tables, 1)

        @block.tensor
        def _(pe):
            pe.wait_ge(loaded, 80)
            for i in range(2 * NCH):
                wait(pe, copied, i - 3)
                for k in range(KT):
                    ins = nc.tensor.matmul(banks[i % 4][0:RANK, :], wab[:, k, i // NCH, :],
                                           c.xnT[:, k, (i % NCH) * CH:(i % NCH + 1) * CH],
                                           start=(k == 0), stop=(k == KT - 1))
                ins.then_inc(projected, 1)
            pe.wait_ge(copied, 2 * NCH)
            for b in range(B):
                wait(pe, act_done, 4 + b - 3)
                t0 = b * S
                nc.tensor.matmul(banks[b % 4][:, 0:P], at[:, t0:t0 + P], bt[:, t0:t0 + P], start=True, stop=True)
                nc.tensor.matmul(banks[b % 4][:, P:SC], at[:, t0 + P:t0 + S], bt[:, t0:t0 + S],
                                 start=True, stop=True).then_inc(products, 1)

        @block.scalar
        def _(act):
            f = nc.scalar.activation
            act.wait_ge(dve, 1)
            f(ex[:, :], mn[:, :], ACT.Exp).then_inc(act_done, 1)
            act.wait_ge(act_done, 1)
            f(ln[:, :], ex[:, :], ACT.Ln, bias=c.ones[:, 0:1]).then_inc(act_done, 1)
            f(tg[:, :], pg[:, :], ACT.Tanh, scale=0.5).then_inc(act_done, 1)
            for b in range(B):
                act.wait_ge(products, b + 1)
                f(c.mt[:, b, :], banks[b % 4][:, 0:SC], ACT.Tanh, scale=0.5).then_inc(act_done, 1)

        @block.vector
        def _(vec):
            stt, ts = nc.vector.scalar_tensor_tensor, nc.vector.tensor_scalar
            n = 0

            def done(ins):
                nonlocal n
                n += 1
                ins.then_inc(dve, 1)
                vec.wait_ge(dve, n)

            vec.wait_ge(loaded, 80)
            done(stt(out=mn[:, :], in0=gt[:, :], scalar=-1.0, in1=gt[:, :], op0=ALU.mult, op1=ALU.min))
            for i in range(2 * NCH):
                vec.wait_ge(projected, i + 1)
                to = (at, bt)[i // NCH]
                nc.vector.tensor_copy(to[:, (i % NCH) * CH:(i % NCH + 1) * CH], banks[i % 4][0:RANK, :])\
                    .then_inc(copied, 1)
            vec.wait_ge(act_done, 3)
            done(stt(out=soft[:, :], in0=gt[:, :], scalar=0.0, in1=ln[:, :], op0=ALU.max, op1=ALU.add))
            done(ts(soft[:, :], soft[:, :], GAMMA_MIN, None, ALU.max))
            done(ts(pc[:, :], pd[:, :], -1.0, 1.0, ALU.max, ALU.min))
            done(stt(out=ch[:, :], in0=pc[:, :], scalar=-1.0 / MAX_LEN, in1=soft[:, :],
                     op0=ALU.mult, op1=ALU.subtract))
            done(ts(c.gh[:, :], tg[:, :], 0.25, 0.25, ALU.mult, ALU.add))
            vec.wait_ge(tables, 5)
            for h in range(HQ):
                ts(c.nb[:, h, :], dist[:, :], ch[:, h:h + 1], c.gh[:, h:h + 1], ALU.mult, ALU.add)\
                    .then_inc(nb_step, 1)
            vec.wait_ge(nb_step, HQ)
            nc.vector.tensor_tensor(c.nb[:, :, :], c.nb[:, :, :], cut[:, None, :].to_broadcast([P, HQ, SC]), ALU.add)\
                .then_inc(nb_step, 1)

        inner.close()
        m.clear()


def softmax_attention(nc, c, w_att, wo_att, rope):
    with ExitStack() as stack:
        m = Memory(nc, stack)
        wat = m.sb("wat", [P, KT, NB * P])
        wot = m.sb("wot", [P, QG, H])
        tab = m.sb("rope_tab", [P, 4, S])
        xs = m.sb("xs", [P, KT, S])
        mc = m.sb("mc", [P, QG + 1, S])
        ms = m.sb("ms", [P, QG + 1, S])
        qk = m.sb("qk", [P, QG + 1, S])
        v = m.sb("v_att", [P, 2, P])
        sc = m.sb("sc_att", [P, QG, SC])
        pr = m.sb("pr", [P, QG, SC])
        pT = m.sb("pT", [P, QG, SC])
        oT = m.sb("oT", [P, QG, S])
        mx, nm, sm, rc = (m.sb("at_" + n, [P, QG, 2]) for n in ("mx", "nm", "sm", "rc"))
        QA, QB, KV, OUT = (m.ps("at_" + n) for n in ("QA", "QB", "KV", "OUT"))
        SH = [m.ps(f"at_S{h}") for h in range(QG)]
        names = ("tab_loaded w_loaded wo_loaded x_loaded projected multiplied turned_qk v_copied scores_done biased "
                 "added max_done neg_done exp_done rc_done scaled turned pT_copied pv_done oT_copied out_done "
                 "y_added zeroed").split()
        s = {n: m.sem("t_" + n) for n in names}
        inner = stack.enter_context(ExitStack())
        block = inner.enter_context(nc.Block())

        def head(j):
            return j // B

        def seq(j):
            return j % B

        @block.sync
        def _(sp):
            sp.dma_start(tab[:, :, :], rope).then_inc(s["tab_loaded"], 16)

            def load_tokens(j):
                t0 = seq(j) * S if isinstance(j, int) else sp.snap(seq(j) * S)
                wait(sp, s["projected"], 3 * j - 2)
                sp.dma_start(xs[:, :, :], c.xnT[:, :, bass.ds(t0, S)]).then_inc(s["x_loaded"], 16)

            def load(g):
                wait(sp, s["projected"], 3 * B * g)
                sp.dma_start(wat[:, :, :], w_att[g]).then_inc(s["w_loaded"], 16)
                load_tokens(B * g)
                wait(sp, s["out_done"], B * g)
                sp.dma_start(wot[:, :, :], wo_att[g]).then_inc(s["wo_loaded"], 16)
                with sp.Fori(1, B) as b:
                    load_tokens(B * g + b)

            load(0)
            with sp.Fori(1, HKV) as g:
                load(g)

        @block.tensor
        def _(pe):
            mm, tr = nc.tensor.matmul, nc.tensor.transpose

            def project(j):
                pe.wait_ge(s["w_loaded"], 16 * (head(j) + 1))
                pe.wait_ge(s["x_loaded"], 16 * (j + 1))
                wait(pe, s["multiplied"], 9 * j)
                wait(pe, s["v_copied"], j)
                toks = bass.ds(seq(j) * S, S)
                for k in range(KT):
                    mm(KV[:, 0:S], wat[:, k, QG * P:(QG + 1) * P], c.xnT[:, k, toks],
                       start=(k == 0), stop=(k == KT - 1))
                for t in range(2):
                    for k in range(KT):
                        ins = mm(KV[:, S + t * P:S + (t + 1) * P], xs[:, k, t * P:(t + 1) * P],
                                 wat[:, k, (QG + 1) * P:], start=(k == 0), stop=(k == KT - 1))
                ins.then_inc(s["projected"], 1)
                for q in range(QG):
                    for k in range(KT):
                        ins = mm((QA, QB)[q // 2][:, (q % 2) * S:(q % 2 + 1) * S], wat[:, k, q * P:(q + 1) * P],
                                 c.xnT[:, k, toks], start=(k == 0), stop=(k == KT - 1))
                    if q % 2:
                        ins.then_inc(s["projected"], 1)

            def scores(j, h):
                pe.wait_ge(s["turned_qk"], 3 * j + 2 + h // 2)
                wait(pe, s["oT_copied"], 4 * j - 3 + h)
                mm(SH[h][:, 0:P], qk[:, h, 0:P], qk[:, QG, 0:P], start=True, stop=True)
                mm(SH[h][:, P:SC], qk[:, h, P:S], qk[:, QG, :], start=True, stop=True)\
                    .then_inc(s["scores_done"], 1)

            def turn(j, h):
                pe.wait_ge(s["scaled"], 8 * j + 2 * h + 2)
                for i in range(3):
                    ins = tr(SH[h][:, i * P:(i + 1) * P], pr[:, h, i * P:(i + 1) * P], c.ident[:, :])
                ins.then_inc(s["turned"], 1)

            def values(j, h):
                pe.wait_ge(s["pT_copied"], 4 * j + h + 1)
                pe.wait_ge(s["v_copied"], j + 1)
                mm(SH[h][:, 0:S], v[:, 0, :], pT[:, h, 0:S], start=True, stop=False, skip_group_check=True)
                mm(SH[h][:, P:S], v[:, 1, :], pT[:, h, S:SC], start=False, stop=True, skip_group_check=True)\
                    .then_inc(s["pv_done"], 1)

            def out(j, h):
                pe.wait_ge(s["oT_copied"], 4 * j + h + 1)
                if h == 0:
                    pe.wait_ge(s["wo_loaded"], 16 * (head(j) + 1))
                    wait(pe, s["y_added"], j)
                for t in range(2):
                    ins = mm(OUT[:, t * H:(t + 1) * H], oT[:, h, t * P:(t + 1) * P], wot[:, h, :],
                             start=(h == 0 and t == 0), stop=(h == QG - 1 and t == 1), skip_group_check=True)
                if h == QG - 1:
                    ins.then_inc(s["out_done"], 1)

            def step(j, last=False):
                for h in range(QG):
                    scores(j, h)
                if not last:
                    project(j + 1)
                turn(j, 0)
                turn(j, 1)
                values(j, 0)
                turn(j, 2)
                values(j, 1)
                out(j, 0)
                turn(j, 3)
                values(j, 2)
                out(j, 1)
                values(j, 3)
                out(j, 2)
                out(j, 3)

            project(0)
            step(0)
            with pe.Fori(1, ASTEPS - 1) as j:
                step(j)
            step(ASTEPS - 1, last=True)

        @block.gpsimd
        def _(pool):
            def turned(j):
                for i, (lo, n) in enumerate(((QG, 1), (0, 2), (2, 2))):
                    pool.wait_ge(s["multiplied"], 9 * j + 3 * i + 3)
                    if i == 0:
                        wait(pool, s["scores_done"], 4 * j)
                    nc.gpsimd.tensor_tensor(qk[:, lo:lo + n, :], mc[:, lo:lo + n, :], ms[:, lo:lo + n, :], ALU.add)\
                        .then_inc(s["turned_qk"], 1)

            turned(0)
            with pool.Fori(1, ASTEPS) as j:
                turned(j)

        @block.scalar
        def _(act):
            f = nc.scalar.activation

            def exponent(j, h):
                act.wait_ge(s["neg_done"], 4 * j + h + 1)
                wait(act, s["turned"], 4 * j - 3 + h)
                for t, (lo, hi) in enumerate(((0, P), (P, SC))):
                    f(pr[:, h, lo:hi], sc[:, h, lo:hi], ACT.Exp, bias=nm[:, h, t:t + 1],
                      accum_out=sm[:, h, t:t + 1]).then_inc(s["exp_done"], 1)

            def copy_turned(j, h):
                act.wait_ge(s["turned"], 4 * j + h + 1)
                wait(act, s["pv_done"], 4 * j - 3 + h)
                f(pT[:, h, :], SH[h][:, 0:SC], ACT.Copy).then_inc(s["pT_copied"], 1)

            def copy_output(j, h):
                act.wait_ge(s["pv_done"], 4 * j + h + 1)
                wait(act, s["out_done"], j)
                f(oT[:, h, :], SH[h][:, 0:S], ACT.Copy).then_inc(s["oT_copied"], 1)

            def copy_values(j):
                act.wait_ge(s["projected"], 3 * j + 1)
                act.wait_ge(s["multiplied"], 9 * j + 3)
                wait(act, s["pv_done"], 4 * j)
                f(v[:, :, :], KV[:, S:2 * S].rearrange("p (t d) -> p t d", t=2), ACT.Copy)\
                    .then_inc(s["v_copied"], 1)

            def step(j, last=False):
                for h in range(QG):
                    exponent(j, h)
                copy_turned(j, 0)
                copy_turned(j, 1)
                copy_output(j, 0)
                copy_turned(j, 2)
                copy_output(j, 1)
                copy_turned(j, 3)
                copy_output(j, 2)
                copy_output(j, 3)
                if not last:
                    copy_values(j + 1)

            copy_values(0)
            step(0)
            with act.Fori(1, ASTEPS - 1) as j:
                step(j)
            step(ASTEPS - 1, last=True)

        @block.vector
        def _(vec):
            stt, tt, ts = nc.vector.scalar_tensor_tensor, nc.vector.tensor_tensor, nc.vector.tensor_scalar

            def rotate(j):
                for i, (bank, lo, n, o) in enumerate(((KV, QG, 1, 2), (QA, 0, 2, 0), (QB, 2, 2, 0))):
                    vec.wait_ge(s["projected"], 3 * j + i + 1)
                    wait(vec, s["turned_qk"], 3 * j - 2 + i)
                    src = bank[:, 0:n * S].rearrange("p (n t) -> p n t", n=n)
                    tt(mc[:, lo:lo + n, :], src, tab[:, o:o + 1, :].to_broadcast([P, n, S]), ALU.mult)\
                        .then_inc(s["multiplied"], 1)
                    for a, b in ((0, 64), (64, 0)):
                        tt(ms[a:a + 64, lo:lo + n, :], src[b:b + 64], tab[b:b + 64, o + 1:o + 2, :]
                           .to_broadcast([64, n, S]), ALU.mult).then_inc(s["multiplied"], 1)

            def bias(j):
                for h in range(QG):
                    wait(vec, s["exp_done"], 8 * (j - 1) + 2 * h + 2)
                    n = QG * head(j) + h
                    stt(out=sc[:, h, :], in0=c.mt[:, bass.ds(seq(j), 1), :][:, 0, :], scalar=c.gh[:, bass.ds(n, 1)],
                        in1=c.nb[:, bass.ds(n, 1), :][:, 0, :], op0=ALU.mult, op1=ALU.add).then_inc(s["biased"], 1)

            def maxima(j, h):
                vec.wait_ge(s["scores_done"], 4 * j + h + 1)
                vec.wait_ge(s["biased"], 4 * j + h + 1)
                tt(sc[:, h, :], SH[h][:, 0:SC], sc[:, h, :], ALU.add).then_inc(s["added"], 1)
                vec.wait_ge(s["added"], 4 * j + h + 1)
                wait(vec, s["exp_done"], 8 * j)
                for t, (lo, hi) in enumerate(((0, P), (P, SC))):
                    nc.vector.tensor_reduce(mx[:, h, t:t + 1], sc[:, h, lo:hi], AX.X, ALU.max)\
                        .then_inc(s["max_done"], 1)
                vec.wait_ge(s["max_done"], 8 * j + 2 * h + 2)
                ts(nm[:, h, :], mx[:, h, :], -1.0, None, ALU.mult).then_inc(s["neg_done"], 1)

            def scale(j, h):
                vec.wait_ge(s["exp_done"], 8 * j + 2 * h + 2)
                wait(vec, s["scaled"], 8 * j)
                nc.vector.reciprocal(rc[:, h, :], sm[:, h, :]).then_inc(s["rc_done"], 1)
                vec.wait_ge(s["rc_done"], 4 * j + h + 1)
                for t, (lo, hi) in enumerate(((0, P), (P, SC))):
                    ts(pr[:, h, lo:hi], pr[:, h, lo:hi], rc[:, h, t:t + 1], None, ALU.mult).then_inc(s["scaled"], 1)

            def add_output(j):
                vec.wait_ge(s["out_done"], j + 1)
                wait(vec, s["y_added"], j)
                rows = c.y[:, bass.ds(2 * seq(j), 2), :]
                tt(rows, OUT[:, :].rearrange("p (t n) -> p t n", t=2), rows, ALU.add).then_inc(s["y_added"], 1)

            def step(j, last=False):
                for h in range(QG):
                    maxima(j, h)
                for h in range(QG):
                    scale(j, h)
                if not last:
                    rotate(j + 1)
                    bias(j + 1)
                add_output(j)

            nc.vector.memset(c.y[:, :, :], 0.0).then_inc(s["zeroed"], 1)
            vec.wait_ge(s["tab_loaded"], 16)
            rotate(0)
            bias(0)
            vec.wait_ge(s["zeroed"], 1)
            step(0)
            with vec.Fori(1, ASTEPS - 1) as j:
                step(j)
            step(ASTEPS - 1, last=True)

        inner.close()
        m.clear()


def table_feed_forward(nc, c):
    with ExitStack() as stack:
        m = Memory(nc, stack)
        gate = c.w_table[:, 0:KT * INNER].rearrange("p (k i) -> p k i", k=KT)
        up = c.w_table[:, KT * INNER:2 * KT * INNER].rearrange("p (k i) -> p k i", k=KT)
        down = c.w_table[:, 2 * KT * INNER:].rearrange("p (n h) -> p n h", n=NI)
        banks = [m.ps(f"tf{i}") for i in range(8)]
        ff = FeedForward(m, "tf_", c.xnT, gate, up, down, INNER, c.y, banks)
        inner = stack.enter_context(ExitStack())
        block = inner.enter_context(nc.Block())

        @block.vector
        def _(vec):
            for ch in range(NCH):
                ff.vector(nc, vec, ch)

        @block.tensor
        def _(pe):
            for ch in range(NCH):
                ff.tensor(nc, pe, ch)

        @block.scalar
        def _(act):
            for ch in range(NCH):
                ff.scalar(nc, act, ch)

        inner.close()
        m.clear()


def build(nc, stack, a, out):
    m = Memory(nc, stack)

    class c:
        pass

    c.ident = m.sb("ident", [P, P])
    c.ones = m.sb("ones", [P, P])
    c.tri = m.sb("tri", [P, P])
    c.tri_strict = m.sb("tri_strict", [P, P])
    c.cut = m.sb("cut", [P, S])
    c.x = m.sb("x_rows", [P, NT, H])
    c.xn = m.sb("xn_rows", [P, NT, H])
    c.xnT = m.sb("xnT", [P, KT, TOK])
    c.y = m.sb("y_rows", [P, NT, H])
    c.w_table = m.sb("w_table", [P, NCOL])
    g_dram = nc.dram_tensor("decay_rows", (HV, TOK), F32).ap()
    slots_dram = nc.dram_tensor("slot_rows", (E * CAP, H), F32).ap()
    outs_dram = nc.dram_tensor("expert_outs", (E * CAP + 1, H), F32).ap()

    with ExitStack() as layer:
        ml = Memory(nc, layer)
        c.level = ml.sb("level", [P, LEVELS + 1, P])
        make_constants(nc, c, a["x"].rearrange("(n p) h -> p n h", p=P))
        normalise(nc, c, "n0_", None, first=True)
        c.G = ml.sb("G", [P, NT, HV])
        c.beta = ml.sb("beta", [P, NT, HV])
        delta_gates(nc, c, a["w_ab"], a["a_log"], a["dt_bias"], g_dram)
        delta_rule(nc, c, a["w_qkv"], a["w_z"], a["conv_w"], a["w_out"], a["norm_w"], a["lut"], a["index"], g_dram)

    normalise(nc, c, "n1_", c.y)
    experts(nc, c, *(a[n] for n in "gate_w w_gate w_up w_down sw_gate sw_up sw_down".split()),
            slots_dram, outs_dram)

    normalise(nc, c, "n2_", c.y)
    with ExitStack() as layer:
        ml = Memory(nc, layer)
        c.mt = ml.sb("mt", [P, B, SC])
        c.nb = ml.sb("nb", [P, HQ, SC])
        c.gh = ml.sb("gh", [P, HQ])
        attention_bias(nc, c, a["pol_WA"], a["pol_WB"], a["pol_dir"], a["pol_gate"], a["gtp_gamma"])
        softmax_attention(nc, c, a["w_att"], a["wo_att"], a["rope"])

    normalise(nc, c, "n3_", c.y)
    table_feed_forward(nc, c)
    normalise(nc, c, "n4_", c.y, last=out.rearrange("(n p) h -> p n h", p=P))


def kernel(**inputs):
    import concourse.bacc as bacc
    from concourse.bass_utils import run_bass_kernel_spmd

    def get(name):
        return np.asarray(inputs[name])

    a = {"x": get("L0_attn_hidden_states").reshape(TOK, H)}
    w = get("L0_attn_W_qkv")
    nk = HK * DK
    blocks = [w[nk:2 * nk].reshape(HK, 1, DK, KT, P), w[:nk].reshape(HK, 1, DK, KT, P),
              w[2 * nk:].reshape(HK, 2, DK, KT, P)]
    a["w_qkv"] = np.concatenate(blocks, 1).transpose(0, 4, 3, 1, 2)
    w = get("L0_attn_conv_w")
    blocks = [w[nk:2 * nk].reshape(HK, 1, DK, TAPS), w[:nk].reshape(HK, 1, DK, TAPS),
              w[2 * nk:].reshape(HK, 2, DK, TAPS)]
    a["conv_w"] = np.concatenate(blocks, 1).transpose(2, 0, 1, 3)
    a["w_z"] = get("L0_attn_W_z").reshape(HK, 2 * DK, KT, P).transpose(0, 3, 2, 1)
    w = np.concatenate([get("L0_attn_W_a"), get("L0_attn_W_b")], 0)
    a["w_ab"] = w.reshape(2 * HV, KT, P).transpose(2, 1, 0)
    a["w_out"] = get("L0_attn_W_out").reshape(H, HK, 2, DK).transpose(1, 3, 2, 0)
    a["a_log"], a["dt_bias"] = get("L0_attn_A_log"), get("L0_attn_dt_bias")
    a["norm_w"] = get("L0_attn_norm_w").reshape(DK, 1)
    a["gate_w"] = get("L0_ffn_gate_w").reshape(E, KT, P).transpose(2, 1, 0)
    for n in "w_gate w_up w_down sw_gate sw_up sw_down".split():
        a[n] = get("L0_ffn_" + n)
    q = get("L1_attn_Wq").reshape(KT, P, HKV, QG * DH)
    k, v = (get("L1_attn_" + n).reshape(KT, P, HKV, DH) for n in ("Wk", "Wv"))
    a["w_att"] = np.concatenate([q, k, v], 3).transpose(2, 1, 0, 3)
    a["wo_att"] = get("L1_attn_Wo").reshape(HKV, QG, DH, H).transpose(0, 2, 1, 3)
    for n in "pol_dir pol_WA pol_WB pol_gate gtp_gamma".split():
        a[n] = get("L1_attn_" + n)
    freq = np.float32(1) / np.float32(10000.0) ** (np.arange(0, DH, 2, dtype=np.float32) / np.float32(DH))
    ang = (np.arange(S, dtype=np.float32)[None, :] * freq[:, None]).astype(np.float64)
    cos, sin = np.concatenate([np.cos(ang)] * 2), np.concatenate([np.sin(ang), -np.sin(ang)])
    a["rope"] = np.stack([cos * DH ** -0.5, sin * DH ** -0.5, cos, sin], 1).astype(np.float32)
    a["lut"] = get("L1_ffn_lut")
    ix = [get("L1_ffn_" + n).T.reshape(KT, P, INNER).transpose(1, 0, 2).reshape(P, KT * INNER)
          for n in ("gate_idx", "up_idx")]
    down = get("L1_ffn_down_idx").T
    down = np.concatenate([down, np.zeros((NI * P - INNER, H), down.dtype)])
    a["index"] = np.concatenate(ix + [down.reshape(NI, P, H).transpose(1, 0, 2).reshape(P, NI * H)], 1)

    nc = bacc.Bacc("TRN2", target_bir_lowering=False, num_devices=1)
    arrays = {"in_" + n: np.ascontiguousarray(v) for n, v in a.items()}
    aps = {n: nc.dram_tensor("in_" + n, arrays["in_" + n].shape, mybir.dt.from_np(arrays["in_" + n].dtype),
                             kind="ExternalInput").ap() for n in a}
    out = nc.dram_tensor("out", (TOK, H), F32, kind="ExternalOutput").ap()
    with ExitStack() as stack:
        build(nc, stack, aps, out)
    r = run_bass_kernel_spmd(nc, [arrays], core_ids=[0])
    return r.results[0]["out"].reshape(B, S, H)
```
